# Optimizing a Trainium2 kernel written in Bass

```python
import numpy as np
import jax
import jax.numpy as jnp

def _softmax(x, axis=-1):
    return jax.nn.softmax(x, axis=axis)

def _gelu(x):
    return jax.nn.gelu(x, approximate=True)

def _silu(x):
    return jax.nn.silu(x)

def _sigmoid(x):
    return jax.nn.sigmoid(x)

def _layernorm(x, axis=-1, eps=1e-05):
    m = jnp.mean(x, axis=axis, keepdims=True)
    v = jnp.var(x, axis=axis, keepdims=True)
    return (x - m) / jnp.sqrt(v + eps)

def _scatter_add(tgt, idx, src, axis=0):
    return tgt.at[idx].add(src)

def _segment_sum(src, seg, n):
    return jax.ops.segment_sum(src, seg, n)
kernel_name = 'mk_vit_tower_d2_tok_img768_r4_d709d2'

def setup_inputs(seed: int=0):
    np.random.seed(seed)
    _w = jnp.asarray

    def _rec_inputs():
        import jax
        import jax.numpy as jnp
        _rk = jax.random.key(seed)
        x = -0.000348323 + 0.999952 * jax.random.normal(jax.random.fold_in(_rk, 1), (64, 3, 64, 64), jnp.float32)
        return x
    x = _rec_inputs()

    def _L0_tok_setup():
        import jax, jax.numpy as jnp
        import numpy as np
        PATCH = 16

        def _shifted_concat(x):
            B, C, H, W = x.shape
            xp = jnp.pad(x, ((0, 0), (0, 0), (1, 1), (1, 1)))
            right = xp[:, :, 1:1 + H, 0:W]
            left = xp[:, :, 1:1 + H, 2:2 + W]
            down = xp[:, :, 0:H, 1:1 + W]
            up = xp[:, :, 2:2 + H, 1:1 + W]
            return jnp.concatenate([x, right, left, down, up], axis=1)

        def _patchify(x, p):
            B, C, H, W = x.shape
            h, w = (H // p, W // p)
            x = x.reshape(B, C, h, p, w, p)
            x = x.transpose(0, 2, 4, 3, 5, 1)
            return x.reshape(B, h * w, p * p * C)

        def _layernorm(x, gamma, beta, eps=1e-05):
            mu = jnp.mean(x, axis=-1, keepdims=True)
            var = jnp.var(x, axis=-1, keepdims=True)
            return (x - mu) * jax.lax.rsqrt(var + eps) * gamma + beta
        key = jax.random.key(seed)
        k1, k2 = jax.random.split(key)
        B, H, W = (32, 96, 96)
        patch_dim = PATCH * PATCH * 15
        d_hidn = 192
        x = jax.random.normal(k1, (B, 3, H, W), dtype=jnp.float32)
        gamma = jnp.ones((patch_dim,), dtype=jnp.float32)
        beta = jnp.zeros((patch_dim,), dtype=jnp.float32)
        W_ = jax.random.normal(k2, (patch_dim, d_hidn), dtype=jnp.float32) * patch_dim ** (-0.5)
        b = jnp.zeros((d_hidn,), dtype=jnp.float32)
        return {'x': x, 'gamma': gamma, 'beta': beta, 'W': W_, 'b': b}
    _L0_tok_all = _L0_tok_setup()
    _L0_tok_in = {k: v for k, v in _L0_tok_all.items() if k in ('gamma', 'beta', 'W', 'b')}
    del _L0_tok_all

    def _L0_attn_setup():
        import jax, jax.numpy as jnp
        import numpy as np
        B, S, D = (2, 512, 192)
        H, STRIDE = (12, 8)
        HD = D // H

        def _stride_mask(S, stride, causal):
            i = jnp.arange(S)[:, None]
            j = jnp.arange(S)[None, :]
            strided = j % stride == 0
            if causal:
                strided = strided & (j <= i)
            return strided | (j == i) | (j == i - 1)
        key = jax.random.key(seed)
        k0, k1, k2 = jax.random.split(key, 3)
        x = jax.random.normal(k0, (B, S, D), dtype=jnp.float32)
        qkv_w = jax.random.normal(k1, (3 * D, D), dtype=jnp.float32) * 0.02
        qkv_b = jnp.zeros((3 * D,), dtype=jnp.float32)
        out_w = jax.random.normal(k2, (D, D), dtype=jnp.float32) * 0.02
        out_b = jnp.zeros((D,), dtype=jnp.float32)
        return {'x': x, 'qkv_w': qkv_w, 'qkv_b': qkv_b, 'out_w': out_w, 'out_b': out_b}
    _L0_attn_all = _L0_attn_setup()
    _L0_attn_in = {k: v for k, v in _L0_attn_all.items() if k in ('qkv_w', 'qkv_b', 'out_w', 'out_b')}
    del _L0_attn_all

    def _L0_ffn_setup():
        import jax, jax.numpy as jnp
        import numpy as np
        EMB = 192
        HID = 288
        NUM_EXPERTS = 8
        TOP_K = 2
        key = jax.random.key(seed)
        ks = jax.random.split(key, 8)
        s = 0.02
        x = jax.random.normal(ks[0], (4, 256, EMB), dtype=jnp.float32)
        router_w = jax.random.normal(ks[1], (EMB, NUM_EXPERTS), dtype=jnp.float32) * s
        router_b = jnp.zeros((NUM_EXPERTS,), dtype=jnp.float32)
        w1 = jax.random.normal(ks[2], (NUM_EXPERTS, EMB, HID), dtype=jnp.float32) * s
        b1 = jnp.zeros((NUM_EXPERTS, HID), dtype=jnp.float32)
        w2 = jax.random.normal(ks[3], (NUM_EXPERTS, HID, EMB), dtype=jnp.float32) * s
        b2 = jnp.zeros((NUM_EXPERTS, EMB), dtype=jnp.float32)
        return {'x': x, 'router_w': router_w, 'router_b': router_b, 'w1': w1, 'b1': b1, 'w2': w2, 'b2': b2}
    _L0_ffn_all = _L0_ffn_setup()
    _L0_ffn_in = {k: v for k, v in _L0_ffn_all.items() if k in ('router_w', 'router_b', 'w1', 'b1', 'w2', 'b2')}
    del _L0_ffn_all

    def _L1_attn_setup():
        import jax, jax.numpy as jnp
        import numpy as np
        EPS = 1e-05
        B, T, C = (8, 512, 192)
        H = 4 * C
        LAYER_ID, N_LAYER = (4, 12)

        def _ln(x, w, b):
            mu = x.mean(-1, keepdims=True)
            var = ((x - mu) ** 2).mean(-1, keepdims=True)
            return (x - mu) / jnp.sqrt(var + EPS) * w + b

        def _wkv_scan(w, k, v):
            a0 = jnp.zeros(k.shape[1:], k.dtype)
            b0 = jnp.zeros_like(a0)
            m0 = jnp.full_like(a0, -1e+38)

            def step(carry, kv):
                a, b, m = carry
                kt, vt = kv
                mm = jnp.maximum(m + w, kt)
                e1 = jnp.exp(m + w - mm)
                e2 = jnp.exp(kt - mm)
                return ((e1 * a + e2 * vt, e1 * b + e2, mm), (a, b, m))
            _, (A, Bd, M) = jax.lax.scan(step, (a0, b0, m0), (k, v))
            return (A, Bd, M)

        def bi_wkv(w, u, k, v):
            kt = jnp.swapaxes(k, 0, 1)
            vt = jnp.swapaxes(v, 0, 1)
            af, bf, mf = _wkv_scan(w, kt, vt)
            ab, bb, mb = _wkv_scan(w, kt[::-1], vt[::-1])
            ab, bb, mb = (ab[::-1], bb[::-1], mb[::-1])
            kk = kt + u
            M = jnp.maximum(jnp.maximum(mf, mb), kk)
            ef = jnp.exp(mf - M)
            eb = jnp.exp(mb - M)
            ec = jnp.exp(kk - M)
            y = (ef * af + eb * ab + ec * vt) / (ef * bf + eb * bb + ec)
            return jnp.swapaxes(y, 0, 1)
        key = jax.random.key(seed)
        ks = jax.random.split(key, 9)
        x = jax.random.normal(ks[0], (B, T, C), jnp.float32)
        r01 = LAYER_ID / (N_LAYER - 1)
        h = np.arange(C, dtype=np.float64)
        decay = (-5.0 + 8.0 * (h / (C - 1)) ** (0.7 + 1.3 * r01)).astype(np.float32)
        zigzag = ((np.arange(C) + 1) % 3 - 1).astype(np.float32) * 0.5
        first = (np.float32(np.log(0.3)) + zigzag).astype(np.float32)
        s = 0.02
        return {'x': x, 'ln1_w': jnp.ones((C,), jnp.float32), 'ln1_b': jnp.zeros((C,), jnp.float32), 'ln2_w': jnp.ones((C,), jnp.float32), 'ln2_b': jnp.zeros((C,), jnp.float32), 'decay': jnp.asarray(decay), 'first': jnp.asarray(first), 'Wk_a': s * jax.random.normal(ks[1], (C, C), jnp.float32), 'Wv_a': s * jax.random.normal(ks[2], (C, C), jnp.float32), 'Wr_a': s * jax.random.normal(ks[3], (C, C), jnp.float32), 'Wo_a': s * jax.random.normal(ks[4], (C, C), jnp.float32), 'Wk_f': s * jax.random.normal(ks[5], (H, C), jnp.float32), 'Wv_f': s * jax.random.normal(ks[6], (C, H), jnp.float32), 'Wr_f': s * jax.random.normal(ks[7], (C, C), jnp.float32)}
    _L1_attn_all = _L1_attn_setup()
    _L1_attn_in = {k: v for k, v in _L1_attn_all.items() if k in ('ln1_w', 'ln1_b', 'ln2_w', 'ln2_b', 'decay', 'first', 'Wk_a', 'Wv_a', 'Wr_a', 'Wo_a', 'Wk_f', 'Wv_f', 'Wr_f')}
    del _L1_attn_all

    def _L1_ffn_setup():
        import jax, jax.numpy as jnp
        import numpy as np
        DIM = 192
        NUM_HEADS = 12
        HEAD_DIM = DIM // NUM_HEADS
        SCALE = HEAD_DIM ** (-0.5)
        NUM_EXPERTS = 8
        RANK = 16
        ALPHA = 32
        TOPK = 2
        SCALING = ALPHA / RANK
        B, S = (8, 256)
        key = jax.random.key(seed)
        ks = jax.random.split(key, 12)
        d, e, r = (DIM, NUM_EXPERTS, RANK)
        inp = {'x': jax.random.normal(ks[0], (B, S, d), jnp.float32), 'Wg': jax.random.normal(ks[1], (e, d), jnp.float32) * 0.02, 'bg': jax.random.normal(ks[2], (e,), jnp.float32) * 0.02, 'Wqkv': jax.random.normal(ks[3], (3 * d, d), jnp.float32) * 0.02, 'bqkv': jax.random.normal(ks[4], (3 * d,), jnp.float32) * 0.02, 'Wproj': jax.random.normal(ks[5], (d, d), jnp.float32) * 0.02, 'bproj': jax.random.normal(ks[6], (d,), jnp.float32) * 0.02, 'A': jax.random.normal(ks[7], (e, r, d), jnp.float32) * 0.05, 'ba': jax.random.normal(ks[8], (e, r), jnp.float32) * 0.02, 'Bm': jax.random.normal(ks[9], (e, 3 * d, r), jnp.float32) * 0.05, 'bb': jax.random.normal(ks[10], (e, 3 * d), jnp.float32) * 0.02}
        return inp
    _L1_ffn_all = _L1_ffn_setup()
    _L1_ffn_in = {k: v for k, v in _L1_ffn_all.items() if k in ('Wg', 'bg', 'Wqkv', 'bqkv', 'Wproj', 'bproj', 'A', 'ba', 'Bm', 'bb')}
    del _L1_ffn_all
    return {'x': x, 'L0_tok_gamma': _L0_tok_in['gamma'], 'L0_tok_beta': _L0_tok_in['beta'], 'L0_tok_W': _L0_tok_in['W'], 'L0_tok_b': _L0_tok_in['b'], 'L0_attn_qkv_w': _L0_attn_in['qkv_w'], 'L0_attn_qkv_b': _L0_attn_in['qkv_b'], 'L0_attn_out_w': _L0_attn_in['out_w'], 'L0_attn_out_b': _L0_attn_in['out_b'], 'L0_ffn_router_w': _L0_ffn_in['router_w'], 'L0_ffn_router_b': _L0_ffn_in['router_b'], 'L0_ffn_w1': _L0_ffn_in['w1'], 'L0_ffn_b1': _L0_ffn_in['b1'], 'L0_ffn_w2': _L0_ffn_in['w2'], 'L0_ffn_b2': _L0_ffn_in['b2'], 'L1_attn_ln1_w': _L1_attn_in['ln1_w'], 'L1_attn_ln1_b': _L1_attn_in['ln1_b'], 'L1_attn_ln2_w': _L1_attn_in['ln2_w'], 'L1_attn_ln2_b': _L1_attn_in['ln2_b'], 'L1_attn_decay': _L1_attn_in['decay'], 'L1_attn_first': _L1_attn_in['first'], 'L1_attn_Wk_a': _L1_attn_in['Wk_a'], 'L1_attn_Wv_a': _L1_attn_in['Wv_a'], 'L1_attn_Wr_a': _L1_attn_in['Wr_a'], 'L1_attn_Wo_a': _L1_attn_in['Wo_a'], 'L1_attn_Wk_f': _L1_attn_in['Wk_f'], 'L1_attn_Wv_f': _L1_attn_in['Wv_f'], 'L1_attn_Wr_f': _L1_attn_in['Wr_f'], 'L1_ffn_Wg': _L1_ffn_in['Wg'], 'L1_ffn_bg': _L1_ffn_in['bg'], 'L1_ffn_Wqkv': _L1_ffn_in['Wqkv'], 'L1_ffn_bqkv': _L1_ffn_in['bqkv'], 'L1_ffn_Wproj': _L1_ffn_in['Wproj'], 'L1_ffn_bproj': _L1_ffn_in['bproj'], 'L1_ffn_A': _L1_ffn_in['A'], 'L1_ffn_ba': _L1_ffn_in['ba'], 'L1_ffn_Bm': _L1_ffn_in['Bm'], 'L1_ffn_bb': _L1_ffn_in['bb']}

def reference(x, L0_tok_gamma, L0_tok_beta, L0_tok_W, L0_tok_b, L0_attn_qkv_w, L0_attn_qkv_b, L0_attn_out_w, L0_attn_out_b, L0_ffn_router_w, L0_ffn_router_b, L0_ffn_w1, L0_ffn_b1, L0_ffn_w2, L0_ffn_b2, L1_attn_ln1_w, L1_attn_ln1_b, L1_attn_ln2_w, L1_attn_ln2_b, L1_attn_decay, L1_attn_first, L1_attn_Wk_a, L1_attn_Wv_a, L1_attn_Wr_a, L1_attn_Wo_a, L1_attn_Wk_f, L1_attn_Wv_f, L1_attn_Wr_f, L1_ffn_Wg, L1_ffn_bg, L1_ffn_Wqkv, L1_ffn_bqkv, L1_ffn_Wproj, L1_ffn_bproj, L1_ffn_A, L1_ffn_ba, L1_ffn_Bm, L1_ffn_bb):
    import jax
    import jax.numpy as jnp

    def _L0_tok_ref(x, gamma, beta, W, b):
        import jax, jax.numpy as jnp
        import numpy as np
        PATCH = 16

        def _shifted_concat(x):
            B, C, H, W = x.shape
            xp = jnp.pad(x, ((0, 0), (0, 0), (1, 1), (1, 1)))
            right = xp[:, :, 1:1 + H, 0:W]
            left = xp[:, :, 1:1 + H, 2:2 + W]
            down = xp[:, :, 0:H, 1:1 + W]
            up = xp[:, :, 2:2 + H, 1:1 + W]
            return jnp.concatenate([x, right, left, down, up], axis=1)

        def _patchify(x, p):
            B, C, H, W = x.shape
            h, w = (H // p, W // p)
            x = x.reshape(B, C, h, p, w, p)
            x = x.transpose(0, 2, 4, 3, 5, 1)
            return x.reshape(B, h * w, p * p * C)

        def _layernorm(x, gamma, beta, eps=1e-05):
            mu = jnp.mean(x, axis=-1, keepdims=True)
            var = jnp.var(x, axis=-1, keepdims=True)
            return (x - mu) * jax.lax.rsqrt(var + eps) * gamma + beta
        xs = _shifted_concat(x)
        tokens = _patchify(xs, PATCH)
        normed = _layernorm(tokens, gamma, beta)
        return jnp.einsum('bnd,de->bne', normed, W) + b

    def _L0_attn_ref(x, qkv_w, qkv_b, out_w, out_b):
        import jax, jax.numpy as jnp
        import numpy as np
        B, S, D = (2, 512, 192)
        H, STRIDE = (12, 8)
        HD = D // H

        def _stride_mask(S, stride, causal):
            i = jnp.arange(S)[:, None]
            j = jnp.arange(S)[None, :]
            strided = j % stride == 0
            if causal:
                strided = strided & (j <= i)
            return strided | (j == i) | (j == i - 1)
        Bx, Sx, Dx = x.shape
        qkv = x @ qkv_w.T + qkv_b
        qkv = qkv.reshape(Bx, Sx, 3, H, HD)
        q, k, v = jnp.transpose(qkv, (2, 0, 3, 1, 4))
        scale = HD ** (-0.5)
        attn = jnp.einsum('bhid,bhjd->bhij', q, k) * scale
        mask = _stride_mask(Sx, STRIDE, True)
        attn = jnp.where(mask[None, None], attn, -jnp.inf)
        a = jax.nn.softmax(attn, axis=-1)
        a = jnp.nan_to_num(a, nan=0.0)
        out = jnp.einsum('bhij,bhjd->bhid', a, v)
        out = jnp.transpose(out, (0, 2, 1, 3)).reshape(Bx, Sx, Dx)
        return out @ out_w.T + out_b

    def _L0_ffn_ref(x, router_w, router_b, w1, b1, w2, b2):
        import jax, jax.numpy as jnp
        import numpy as np
        EMB = 192
        HID = 288
        NUM_EXPERTS = 8
        TOP_K = 2
        B, N, E = x.shape
        T = B * N
        logits = jnp.einsum('bne,ef->bnf', x, router_w) + router_b
        probs = jax.nn.softmax(logits, axis=-1)
        topk_probs, topk_idx = jax.lax.top_k(probs, TOP_K)
        flat_x = x.reshape(T, E)
        flat_idx = topk_idx.reshape(T, TOP_K)
        flat_w = topk_probs.reshape(T, TOP_K)
        gates = jnp.zeros((T, NUM_EXPERTS), dtype=x.dtype)
        gates = gates.at[jnp.arange(T)[:, None], flat_idx].add(flat_w)
        out = jnp.zeros((T, E), dtype=x.dtype)
        for e in range(NUM_EXPERTS):
            h = jax.nn.gelu(flat_x @ w1[e] + b1[e], approximate=False)
            y = h @ w2[e] + b2[e]
            out = out + y * gates[:, e:e + 1]
        return out.reshape(B, N, E)

    def _L1_attn_ref(x, ln1_w, ln1_b, ln2_w, ln2_b, decay, first, Wk_a, Wv_a, Wr_a, Wo_a, Wk_f, Wv_f, Wr_f):
        import jax, jax.numpy as jnp
        import numpy as np
        EPS = 1e-05
        B, T, C = (8, 512, 192)
        H = 4 * C
        LAYER_ID, N_LAYER = (4, 12)

        def _ln(x, w, b):
            mu = x.mean(-1, keepdims=True)
            var = ((x - mu) ** 2).mean(-1, keepdims=True)
            return (x - mu) / jnp.sqrt(var + EPS) * w + b

        def _wkv_scan(w, k, v):
            a0 = jnp.zeros(k.shape[1:], k.dtype)
            b0 = jnp.zeros_like(a0)
            m0 = jnp.full_like(a0, -1e+38)

            def step(carry, kv):
                a, b, m = carry
                kt, vt = kv
                mm = jnp.maximum(m + w, kt)
                e1 = jnp.exp(m + w - mm)
                e2 = jnp.exp(kt - mm)
                return ((e1 * a + e2 * vt, e1 * b + e2, mm), (a, b, m))
            _, (A, Bd, M) = jax.lax.scan(step, (a0, b0, m0), (k, v))
            return (A, Bd, M)

        def bi_wkv(w, u, k, v):
            kt = jnp.swapaxes(k, 0, 1)
            vt = jnp.swapaxes(v, 0, 1)
            af, bf, mf = _wkv_scan(w, kt, vt)
            ab, bb, mb = _wkv_scan(w, kt[::-1], vt[::-1])
            ab, bb, mb = (ab[::-1], bb[::-1], mb[::-1])
            kk = kt + u
            M = jnp.maximum(jnp.maximum(mf, mb), kk)
            ef = jnp.exp(mf - M)
            eb = jnp.exp(mb - M)
            ec = jnp.exp(kk - M)
            y = (ef * af + eb * ab + ec * vt) / (ef * bf + eb * bb + ec)
            return jnp.swapaxes(y, 0, 1)
        Bn, Tn, Cn = x.shape
        h = _ln(x, ln1_w, ln1_b)
        k = h @ Wk_a.T
        v = h @ Wv_a.T
        sr = jax.nn.sigmoid(h @ Wr_a.T)
        y = bi_wkv(decay / Tn, first / Tn, k, v)
        x = x + sr * y @ Wo_a.T
        h = _ln(x, ln2_w, ln2_b)
        kf = jnp.square(jax.nn.relu(h @ Wk_f.T))
        x = x + jax.nn.sigmoid(h @ Wr_f.T) * (kf @ Wv_f.T)
        return x

    def _L1_ffn_ref(x, Wg, bg, Wqkv, bqkv, Wproj, bproj, A, ba, Bm, bb):
        import jax, jax.numpy as jnp
        import numpy as np
        DIM = 192
        NUM_HEADS = 12
        HEAD_DIM = DIM // NUM_HEADS
        SCALE = HEAD_DIM ** (-0.5)
        NUM_EXPERTS = 8
        RANK = 16
        ALPHA = 32
        TOPK = 2
        SCALING = ALPHA / RANK
        B, S = (8, 256)
        b, s, d = x.shape
        t = b * s
        xf = x.reshape(t, d)
        probs = jax.nn.softmax(xf @ Wg.T + bg, axis=-1)
        top_w, top_idx = jax.lax.top_k(probs, TOPK)
        combine = jnp.zeros((t, NUM_EXPERTS), x.dtype).at[jnp.arange(t)[:, None], top_idx].add(top_w)
        h = jnp.einsum('td,erd->ter', xf, A) + ba
        hw = h * combine[:, :, None]
        delta = jnp.einsum('ter,eor->to', hw, Bm) + combine @ bb
        delta = delta * SCALING
        qkv = xf @ Wqkv.T + bqkv + delta
        qkv = qkv.reshape(b, s, 3, NUM_HEADS, HEAD_DIM)
        qkv = jnp.transpose(qkv, (2, 0, 3, 1, 4))
        q, k, v = (qkv[0], qkv[1], qkv[2])
        attn = jax.nn.softmax(jnp.einsum('bhsd,bhtd->bhst', q, k) * SCALE, axis=-1)
        out = jnp.einsum('bhst,bhtd->bhsd', attn, v)
        out = jnp.transpose(out, (0, 2, 1, 3)).reshape(b, s, d)
        return out @ Wproj.T + bproj
    h = _L0_tok_ref(x, L0_tok_gamma, L0_tok_beta, L0_tok_W, L0_tok_b)
    h = h + _L0_attn_ref(_layernorm(h, axis=-1), L0_attn_qkv_w, L0_attn_qkv_b, L0_attn_out_w, L0_attn_out_b)
    h = h + _L0_ffn_ref(_layernorm(h, axis=-1), L0_ffn_router_w, L0_ffn_router_b, L0_ffn_w1, L0_ffn_b1, L0_ffn_w2, L0_ffn_b2)
    h = h + _L1_attn_ref(_layernorm(h, axis=-1), L1_attn_ln1_w, L1_attn_ln1_b, L1_attn_ln2_w, L1_attn_ln2_b, L1_attn_decay, L1_attn_first, L1_attn_Wk_a, L1_attn_Wv_a, L1_attn_Wr_a, L1_attn_Wo_a, L1_attn_Wk_f, L1_attn_Wv_f, L1_attn_Wr_f)
    h = h + _L1_ffn_ref(_layernorm(h, axis=-1), L1_ffn_Wg, L1_ffn_bg, L1_ffn_Wqkv, L1_ffn_bqkv, L1_ffn_Wproj, L1_ffn_bproj, L1_ffn_A, L1_ffn_ba, L1_ffn_Bm, L1_ffn_bb)
    return h

_drawn_inputs = setup_inputs


def setup_inputs(seed=0):
    import zlib

    import numpy as np

    out = dict(_drawn_inputs(seed))
    spreads = {'L0_tok_gamma': (1.0, 0.2),
     'L0_tok_beta': (0.0, 0.1),
     'L0_tok_b': (0.0, 0.1),
     'L0_attn_qkv_b': (0.0, 0.317),
     'L0_attn_out_b': (0.0, 0.1),
     'L0_ffn_router_b': (0.0, 0.635),
     'L0_ffn_b1': (0.0, 0.8),
     'L0_ffn_b2': (0.0, 0.344),
     'L1_attn_ln1_w': (1.0, 0.6),
     'L1_attn_ln1_b': (0.0, 0.8),
     'L1_attn_ln2_w': (1.0, 0.6),
     'L1_attn_ln2_b': (0.0, 0.8)}
    factors = {'L0_ffn_w1': 4.927,
     'L0_ffn_w2': 4.571,
     'L1_attn_decay': 8.0,
     'L1_attn_first': 8.0,
     'L1_attn_Wk_a': 8.0,
     'L1_attn_Wv_a': 8.0,
     'L1_attn_Wr_a': 8.0,
     'L1_attn_Wo_a': 8.0,
     'L1_attn_Wk_f': 4.425,
     'L1_attn_Wv_f': 4.053,
     'L1_attn_Wr_f': 8.0,
     'L1_ffn_Wg': 8.0,
     'L1_ffn_bg': 8.0,
     'L1_ffn_Wqkv': 4.997,
     'L1_ffn_bqkv': 8.0,
     'L1_ffn_Wproj': 4.728,
     'L1_ffn_bproj': 44.696,
     'L1_ffn_A': 8.0,
     'L1_ffn_ba': 8.0,
     'L1_ffn_Bm': 8.0,
     'L1_ffn_bb': 8.0}
    for name, (base, spread) in spreads.items():
        noise = np.random.default_rng([zlib.crc32(name.encode()), seed]).standard_normal(out[name].shape)
        drawn = base * np.exp(spread * noise) if base else spread * noise
        out[name] = jnp.asarray(drawn.astype(out[name].dtype))
    for name, factor in factors.items():
        out[name] = (out[name] * factor).astype(out[name].dtype)
    return out
```

```python
from contextlib import ExitStack

import numpy as np

import concourse.bass as bass
from concourse import mybir

F32 = mybir.dt.float32
F16 = mybir.dt.float16
ALU = mybir.AluOpType
ACT = mybir.ActivationFunctionType
AX = mybir.AxisListType.X

P = 128
C = 192
CB = C - P
SEQ = 16
NT = 8
TOK = NT * P
HALF = TOK // 2
SH = HALF // SEQ
HD = 16
HA, HB = P // HD, CB // HD
NH = HA + HB
E = 8
HID = 288
NCH = E * HID // P
KF = 768
PIX = 768
FEAT = 960
NCHUNK = 8
PDIM = 3840
WS = 16.0
EPS = 1e-5
BIG = 1e38

GROUPS = ((294, 5), (294, 5), (168, 4), (12, 3), (192, 1))

K_ID = 0
K_HM = K_ID + P
K_HMB = K_HM + HA
K_AM = K_HMB + HB
K_BNW = K_AM + SEQ
K_TRI = K_BNW + 30
K_N = K_TRI + E * E

C_QB0, C_B1, C_LN1WA, C_LN1WB, C_LN1BA, C_LN1BB, C_LN2WA, C_LN2WB, C_LN2BA, C_LN2BB, C_DECA, C_DECB, \
    C_FIRA, C_FIRB, C_BA, C_QB1 = 0, 5, 23, 24, 25, 26, 27, 28, 29, 30, 31, 32, 33, 34, 35, 36
C_N = 41
R_OUT, R_RT, R_PJ, R_GT, R_N = 0, C, C + E, 2 * C + E, 2 * C + 2 * E

LATE = {}
_at = 0
for _name, _width in (("kvr", 3 * C), ("wo", C), ("kf", KF), ("wr", C), ("gate", E), ("la", P),
                      ("qkv1", 3 * C), ("proj", C)):
    LATE[_name] = _at
    _at += _width
LATE_N = _at
EARLY = {"qkv0": 0, "out0": 3 * C, "router": 4 * C}
EARLY_N = 4 * C + E
FULL_N = 6 * C + 3 * C + 3 * C
SLOTS = (("QA", 0, P), ("KA", P, P), ("VA", 2 * P, P), ("KVB", 3 * P, P), ("QB", 4 * P, CB))


UNITS = 2 * E


def unit_chunks(u):
    e = u % E
    n = 2 * u + u // 4
    chunks = []
    if e % 4 == 0:
        chunks.append((n, 2 * E + e // 4, 4 + u // 4 % 2))
        n += 1
    else:
        n += 1
    return chunks + [(n + i, 2 * e + i, (2 * u + i) % 4) for i in range(2)]


class Fills:

    def __init__(self):
        self.bank, self.before, self.done, self.release = {}, {}, {}, {}
        self.latest, self.count, self.total = {}, {}, 0

    def add(self, name, bank=None, by=None, at=None, counted=True):
        if bank is None:
            bank = self.total % 8
        self.bank[name] = bank
        self.before[name] = self.latest.get(bank)
        self.latest[bank] = name
        by = by or f"bank_free{bank}"
        self.count[by] = at or self.count.get(by, 0) + 1
        self.release[name] = (by, self.count[by])
        if counted:
            self.total += 1
            self.done[name] = self.total


def plan_fills():
    f = Fills()
    f.add("beta")
    for t in range(NT + 1):
        if t < NT:
            f.add(("tokT", t, 0))
            f.add(("tokT", t, 1), by="tokx_ready")
        if t:
            f.add(("tok", t - 1))

    def norm(phase):
        for pr in range(4):
            if phase.startswith("mix"):
                f.add(("x", phase, pr), by="xf_ready")
            else:
                f.add(("x", phase, pr), by="x_ready", at=4 * PHASES.index(phase) + pr + 1)

    def attention(a, hf):
        for s in SLOTS:
            f.add(("qkv", a, hf, s[0]), by="qkv_ready")
        for pr in range(2):
            f.add(("st", a, hf, pr), by="st_ready")
        for hl in range(2):
            for g in range(4):
                f.add(("va", a, hf, hl, g), by="v_dve_ready" if g % 2 == 0 else "v_act_ready")
            for g in range(2):
                f.add(("vb", a, hf, hl, g), by="v_act_ready")
            if hl == 0:
                for pr in range(2):
                    f.add(("s", a, hf, pr))
        for pr in range(2):
            f.add(("pt", a, hf, pr), by="pt_ready")
        for pr in range(2):
            f.add(("ot", a, hf, pr), by="ot_ready")
        for pr in range(2):
            f.add(("pj", a, hf, pr))

    norm("attn0")
    for hf in range(2):
        attention(0, hf)
    norm("moe")
    f.add("router0")
    for u in range(UNITS + 1):
        if u < UNITS:
            for n, _, _ in unit_chunks(u):
                f.add(("h", n), bank=n % 4, by="gelu_ready")
        if u:
            for pr in range(2):
                f.add(("y", u - 1, pr), bank=4 + 2 * ((u - 1) % 2) + pr)
    for hf in range(2):
        f.add(("ct", hf), by="ct_ready")
    for pr in range(4):
        f.add(("b2", pr))
    norm("mix1")
    for n in "kvr":
        for part in range(3):
            f.add((n, part), by="kvr_ready")
    for pr in range(4):
        f.add(("wo", pr))
    norm("mix2")
    for hf in range(2):
        for m in range(6):
            f.add(("kf", hf, m), by="relu_ready")
        for pr in range(2):
            f.add(("r", hf, pr), by="tanh_ready")
            f.add(("kv", hf, pr))
    norm("attn1")
    f.add("router1")
    for hf in range(2):
        f.add(("ce", hf))
        f.add(("la", hf), by="hw_ready", at=2 * hf + 1)
        attention(1, hf)
    return f


PHASES = ("attn0", "moe", "mix1", "mix2", "attn1")


def build(nc, tok_x, tok_w, tok_wh, tok_g, tok_bt, tok_b, early, moe1, moe2, moe_b2, late, full, cols, rows, consts,
          out):
    f = plan_fills()
    with ExitStack() as ctx:
        def sb(name, shape, dt=F32):
            return ctx.enter_context(nc.sbuf_tensor(name, shape, dt))

        def sem(name):
            return ctx.enter_context(nc.semaphore(name))

        H = sb("H", [P, NT, C])
        K = sb("K", [P, K_N])
        col = sb("col", [P, C_N])
        col16 = sb("col16", [P, C_N])
        rowr = sb("rowr", [1, R_N])
        rowh = sb("rowh", [1, R_N], F16)
        rowl = sb("rowl", [1, R_N], F16)
        ones = sb("ones", [1, P], F16)
        id16 = sb("id16", [P, P], F16)
        mhalf = sb("mhalf", [P, 1])
        tokb = sb("tokb", [P, C])
        stats = sb("stats", [P, 2, 30])
        wstats = sb("wstats", [P, 2, 30])
        mv = sb("mv", [P, NT, 2])
        ve = sb("ve", [P, NT])
        rstd = sb("rstd", [P, NT])
        xn = sb("xn", [P, NT // 2, 2 * P])
        X_hi = sb("X_hi", [P, NT, 2, P], F16)
        X_lo = sb("X_lo", [P, NT, P], F16)
        gat = sb("gat", [P, 6, NT, E])
        gsum = sb("gsum", [P, 4, NT])
        early_a = sb("early_a", [P, 2, EARLY_N], F16)
        early_b = sb("early_b", [P, 2, EARLY_N], F16)
        late_a = sb("late_a", [P, 2, LATE_N], F16)
        late_b = sb("late_b", [P, 2, LATE_N], F16)
        fullp = sb("fullp", [P, 2, FULL_N], F16)
        b2s = sb("b2s", [E, C])
        T_WORDS = 6144
        T = sb("T", [P, T_WORDS])
        NR = TOK + HALF
        RW = NR + 1
        R = sb("R", [P, 14 * RW])
        Q = sb("Q", [P, 6144])
        PS = ctx.enter_context(nc.psum_tensor("PS", [P, 8, 512], F32))

        def bank(name):
            return PS[:, f.bank[name], :]

        Z = T[:, 0:NT * C].rearrange("p (t n) -> p t n", t=NT)
        raw_w = T[:, 0:5760].rearrange("p (k s n) -> p k s n", k=6, s=5)
        raw_wh = T[:, 5760:6144].rearrange("p (k n) -> p k n", k=2)
        
        tok_in = [R[:, 8192 + 960 * i:8192 + 960 * (i + 1)] for i in range(3)]
        tx_n = [R[:, 1024 * i:1024 * i + 1024] for i in range(2)]
        tx_hi = [R[:, 2048 + 512 * i:2560 + 512 * i].bitcast(F16).rearrange("p (k n) -> p k n", k=8) for i in range(2)]
        tx_lo = [R[:, 3072 + 512 * i:3584 + 512 * i].bitcast(F16).rearrange("p (k n) -> p k n", k=8) for i in range(2)]
        wf = R[:, 4096:4096 + 1536].rearrange("p (k n) -> p k n", k=8)
        wt_hi = R[:, 5632:6400].bitcast(F16).rearrange("p (k n) -> p k n", k=8)
        wt_lo = R[:, 6400:7168].bitcast(F16).rearrange("p (k n) -> p k n", k=8)
        gbt = R[:, 7168:7168 + 64]
        raw_early = R[:, 12416:12416 + 2 * EARLY_N].rearrange("p (k n) -> p k n", k=2)
        KAbd = R[:, 0:4096].bitcast(F16).rearrange("p (l s n) -> p l s n", l=2, s=SH)
        KVBbd = R[:, 4096:6144].bitcast(F16).rearrange("p (l s n) -> p l s n", l=2, s=SH)
        VAbd = R[:, 6144:10240].bitcast(F16).rearrange("p (l s n) -> p l s n", l=2, s=SH)
        VA = R[:, 12288:16384].bitcast(F16).rearrange("p (l s n) -> p l s n", l=2, s=SH)
        VB = R[:, 10240:12288].bitcast(F16).rearrange("p (l s n) -> p l s n", l=2, s=SH)
        M1 = 2304
        raw_m1a = T[:, 0:M1]
        raw_m1b = T[:, M1:2 * M1]
        raw_m2 = T[:, 0:NCH * C]
        m1a = R[:, 16384:16384 + M1].bitcast(F16).rearrange("p (l n) -> p l n", l=2)
        m1b = R[:, 16384 + M1:16384 + 2 * M1].bitcast(F16).rearrange("p (l n) -> p l n", l=2)
        m2 = sb("m2", [P, 2, NCH * C], F16)

        def qv(at, n):
            return Q[:, at:at + n].bitcast(F16)
        pairs = {"QA": qv(0, 512), "KA": qv(512, 512), "VA": qv(1024, 512), "KVB": qv(1536, 512), "QB": qv(2048, 512)}
        pairs = {k: v.rearrange("p (l n) -> p l n", l=2) for k, v in pairs.items()}
        ST = Q[:, 2560:3584].rearrange("p (r t k n) -> p r t k n", r=2, t=2, k=2)
        SM = Q[:, 3584:4352].rearrange("p (r h j) -> p r h j", r=2, j=SEQ)
        PT = Q[:, 4352:5376].bitcast(F16).rearrange("p (l t k n) -> p l t k n", l=2, t=4, k=2)
        O_hi = Q[:, 5376:5888].bitcast(F16).rearrange("p (t k n) -> p t k n", t=4, k=2)
        O_lo = Q[:, 5888:6144].bitcast(F16).rearrange("p (t n) -> p t n", t=4)
        smx = sb("smx", [P, 2, 3, 2 * NH])
        rk = Q[:, 5120:5632].rearrange("p (t e f) -> p t e f", t=NT, e=E)
        rk2 = Q[:, 5632:6144].rearrange("p (t e f) -> p t e f", t=NT, e=E)
        ge = [Q[:, 512 * i:512 * i + 512] for i in range(3)]
        hgh = [Q[:, 1536 + 512 * i:1792 + 512 * i].bitcast(F16) for i in range(6)]
        hgl = [Q[:, 1792 + 512 * i:2048 + 512 * i].bitcast(F16) for i in range(6)]
        ctT = Q[0:E, 4608:5632]
        sy_ah = Q[:, 0:512].bitcast(F16)
        sy_al = Q[:, 512:1024].bitcast(F16)
        sy_bh = Q[:, 1024:1280].bitcast(F16)
        sy_bl = Q[:, 1280:1536].bitcast(F16)
        kfr = [Q[:, 1536 + 512 * i:2048 + 512 * i] for i in range(2)]
        kfs = [R[:, 512 * i:512 + 512 * i] for i in range(2)]
        kfh = Q[:, 3072:4608].bitcast(F16).rearrange("p (m n) -> p m n", m=6)
        kfl = Q[:, 4608:6144].bitcast(F16).rearrange("p (m n) -> p m n", m=6)
        tr_ = R[:, 2048:2048 + 768].rearrange("p (r n) -> p r n", r=2)
        uu = R[:, 3072:3072 + 768].rearrange("p (r n) -> p r n", r=2)
        xt_f = R[:, 4096:4096 + 2048].rearrange("p (r t k n) -> p r t k n", r=4, t=2, k=2)
        crep1 = R[:, 19456:20480].rearrange("p (t n) -> p t n", t=NT)
        ceF = R[:, 16384:17408]
        hwF = R[:, 17408:17920]
        hw_hi = R[:, 17920:18432].bitcast(F16)
        hw_lo = R[:, 18432:18944].bitcast(F16)
        cstack = R[:, 18944:19456].bitcast(F16)
        r_ = [R[:, RW * i:RW * (i + 1)] for i in range(14)]
        rK, rV, rT, rW0, Mf, Mb, E1f, E2f, E1b, E2b, Af, Ab, Bf, Bb = r_

        loaded = {n: sem("in_" + n) for n in ("consts", "cols", "tokw", "tokg", "early", "moe", "late", "full", "b2")}
        x_in = [sem(f"x_in{i}") for i in range(3)]
        out_done = sem("out_done")
        psum_filled = sem("psum_filled")
        bank_free = [sem(f"bank_free{i}") for i in range(8)]
        const_ready = sem("const_ready")
        cols_ready = sem("cols_ready")
        dve_step = sem("dve_step")
        act_step = sem("act_step")
        pool_step = sem("pool_step")
        var_ready = sem("var_ready")
        rstd_ready = sem("rstd_ready")
        xn_ready = sem("xn_ready")
        tokn_ready = sem("tokn_ready")
        hi_ready = sem("hi_ready")
        tokw_ready = sem("tokw_ready")
        tokx_ready = sem("tokx_ready")
        x_ready = sem("x_ready")
        wearly = sem("wearly")
        whi = sem("whi")
        wlo = sem("wlo")
        qkv_ready = sem("qkv_ready")
        bd_ready = sem("bd_ready")
        st_ready = sem("st_ready")
        v_act_ready = sem("v_act_ready")
        v_dve_ready = sem("v_dve_ready")
        smax_ready = sem("smax_ready")
        gmax_ready = sem("gmax_ready")
        exp_ready = sem("exp_ready")
        p_ready = sem("p_ready")
        pt_ready = sem("pt_ready")
        ot_ready = sem("ot_ready")
        gate_ready = sem("gate_ready")
        ct_ready = sem("ct_ready")
        gelu_ready = sem("gelu_ready")
        hp_ready = sem("hp_ready")
        kvr_ready = sem("kvr_ready")
        rd_ready = sem("rd_ready")
        re_ready = sem("re_ready")
        den_in = sem("den_in")
        den_ready = sem("den_ready")
        sy_ready = sem("sy_ready")
        xf_ready = sem("xf_ready")
        relu_ready = sem("relu_ready")
        sq_ready = sem("sq_ready")
        kf_ready = sem("kf_ready")
        tanh_ready = sem("tanh_ready")
        ce_ready = sem("ce_ready")
        hw_ready = sem("hw_ready")
        h_ready = sem("h_ready")

        readers = {"tokx_ready": tokx_ready, "x_ready": x_ready, "xf_ready": xf_ready, "qkv_ready": qkv_ready,
                   "st_ready": st_ready, "v_dve_ready": v_dve_ready, "v_act_ready": v_act_ready, "pt_ready": pt_ready,
                   "ot_ready": ot_ready, "ct_ready": ct_ready, "gelu_ready": gelu_ready,
                   "kvr_ready": kvr_ready, "relu_ready": relu_ready, "tanh_ready": tanh_ready, "hw_ready": hw_ready}
        readers.update({f"bank_free{i}": bank_free[i] for i in range(8)})

        block = ctx.enter_context(nc.Block())

        moe_pieces = []
        for a in range(0, M1, 576):
            moe_pieces.append((raw_m1a[:, a:a + 576], m1a[:, 0, a:a + 576], m1a[:, 1, a:a + 576], WS))
        for a in range(0, M1, 576):
            moe_pieces.append((raw_m1b[:, a:a + 576], m1b[:, 0, a:a + 576], m1b[:, 1, a:a + 576], WS))
        for a in range(0, NCH * C, 576):
            moe_pieces.append((raw_m2[:, a:a + 576], m2[:, 0, a:a + 576], m2[:, 1, a:a + 576], WS))
        late_pieces = []
        raw_la = T[:, 0:LATE_N]
        raw_lb = T[:, LATE_N:2 * LATE_N]
        raw_f = T[:, 0:FULL_N]
        late_cuts = [(a, min(a + 576, LATE_N)) for a in range(0, LATE_N, 576)]
        for a, b in late_cuts:
            late_pieces.append((raw_la[:, a:b], late_a[:, 0, a:b], late_a[:, 1, a:b], WS))
            late_pieces.append((raw_lb[:, a:b], late_b[:, 0, a:b], late_b[:, 1, a:b], WS))
        FW = 6 * C
        for a, b, s in ((0, 576, WS), (576, FW, WS), (FW, FW + 576, 1.0), (FW + 576, FULL_N, WS)):
            late_pieces.append((raw_f[:, a:b], fullp[:, 0, a:b], fullp[:, 1, a:b], s))
        NM, NL, N1 = len(moe_pieces), len(late_pieces), 2 * M1 // 576

        @block.sync
        def _(sp):
            sp.dma_start(K[:], consts).then_inc(loaded["consts"], 16)
            sp.dma_start(gbt[:, 0:32], tok_g).then_inc(loaded["tokg"], 16)
            sp.dma_start(gbt[:, 32:64], tok_bt).then_inc(loaded["tokg"], 16)
            for t in range(2):
                sp.dma_start(tok_in[t], tok_x[t]).then_inc(x_in[t], 16)
            for k in range(6):
                sp.dma_start(raw_w[:, k], tok_w[:, k]).then_inc(loaded["tokw"], 16)
            sp.dma_start(raw_wh, tok_wh).then_inc(loaded["tokw"], 16)
            sp.dma_start(tokb[:], tok_b).then_inc(loaded["cols"], 16)
            sp.dma_start(col[:], cols).then_inc(loaded["cols"], 16)
            sp.dma_start(rowr[:], rows).then_inc(loaded["cols"], 16)
            sp.dma_start(tok_in[2], tok_x[2]).then_inc(x_in[2], 16)
            sp.dma_start(raw_early, early).then_inc(loaded["early"], 16)
            sp.dma_start(b2s[:], moe_b2).then_inc(loaded["b2"], 16)
            for t in range(3, NT):
                sp.wait_ge(tokn_ready, t - 2)
                sp.dma_start(tok_in[t % 3], tok_x[t]).then_inc(x_in[t % 3], 16)
            sp.wait_ge(tokw_ready, 1)
            sp.wait_ge(bank_free[f.bank["beta"]], 1)
            sp.dma_start(T[:, 0:2 * M1], moe1).then_inc(loaded["moe"], 16)
            sp.wait_ge(wlo, N1)
            sp.dma_start(raw_m2, moe2).then_inc(loaded["moe"], 16)
            sp.wait_ge(wlo, NM)
            sp.dma_start(T[:, 0:2 * LATE_N], late).then_inc(loaded["late"], 16)
            sp.wait_ge(wlo, NM + 2 * len(late_cuts))
            sp.dma_start(raw_f, full).then_inc(loaded["full"], 16)
            for pr in range(4):
                sp.wait_ge(h_ready, pr + 1)
                sp.dma_start(out[:, 2 * pr:2 * pr + 2, :], H[:, 2 * pr:2 * pr + 2, :]).then_inc(out_done, 16)
            sp.wait_ge(out_done, 4 * 16)

        @block.gpsimd
        def _(pool):
            nc.gpsimd.memset(mhalf[:], -0.5)
            nc.gpsimd.memset(ones[:], 1.0).then_inc(const_ready, 1)
            steps = [0]

            def one_over_std(n, t):
                pool.wait_ge(var_ready, n + 1)
                nc.gpsimd.tensor_scalar(ve[:, t:t + 1], mv[:, t, 1:2], EPS, None, ALU.add).then_inc(pool_step, 1)
                steps[0] += 1
                pool.wait_ge(pool_step, steps[0])
                nc.gpsimd.tensor_tensor(rstd[:, t:t + 1], ve[:, t:t + 1], mhalf[:], ALU.pow).then_inc(rstd_ready, 1)

            def low_part(n, raw, hi, lo):
                pool.wait_ge(whi, n + 1)
                nc.gpsimd.tensor_tensor(lo, raw, hi, ALU.subtract).then_inc(wlo, 1)

            pool.wait_ge(const_ready, 1)
            n = 0
            for t in range(NT):
                one_over_std(n, t)
                n += 1
            for t in range(NT):
                one_over_std(n, t)
                n += 1
            for i, (raw, hi, lo, _) in enumerate(moe_pieces):
                low_part(i, raw, hi, lo)
            for t in range(NT):
                one_over_std(n, t)
                n += 1
            for i, (raw, hi, lo, _) in enumerate(late_pieces):
                low_part(NM + i, raw, hi, lo)
            pool.wait_ge(wlo, NM + NL)
            nc.gpsimd.tensor_copy(fullp[64:64 + E, 0, FW + 576:FULL_N],
                                  fullp[64:64 + E, 1, FW + 576:FULL_N]).then_inc(wlo, 1)
            pool.wait_ge(wlo, NM + NL + 1)
            for t in range(NT):
                one_over_std(n, t)
                one_over_std(n + 1, t)
                n += 2
            pool.wait_ge(den_in, 1)
            nc.gpsimd.tensor_tensor(E1f[:, 0:NR], E1f[:, 0:NR], Bf[:, 0:NR], ALU.mult).then_inc(pool_step, 1)
            nc.gpsimd.tensor_tensor(E1b[:, 0:NR], E1b[:, 0:NR], Bb[:, 1:NR + 1], ALU.mult).then_inc(pool_step, 1)
            steps[0] += 2
            pool.wait_ge(pool_step, steps[0])
            nc.gpsimd.tensor_tensor(E1f[:, 0:NR], E1f[:, 0:NR], E1b[:, 0:NR], ALU.add).then_inc(pool_step, 1)
            steps[0] += 1
            pool.wait_ge(pool_step, steps[0])
            nc.gpsimd.tensor_tensor(E1f[:, 0:NR], E1f[:, 0:NR], E2f[:, 0:NR], ALU.add).then_inc(den_ready, 1)
            for phase in range(2):
                for t in range(NT):
                    one_over_std(n, t)
                    n += 1

        @block.scalar
        def _(act):
            hn = [0]

            def filled(name):
                act.wait_ge(psum_filled, f.done[name])

            act.wait_ge(loaded["cols"], 48)
            nc.scalar.activation(col16[:], col[:], ACT.Copy, scale=WS).then_inc(cols_ready, 1)
            act.wait_ge(loaded["consts"], 16)
            nc.scalar.activation(id16[:], K[:, K_ID:K_ID + P], ACT.Copy).then_inc(cols_ready, 1)
            for a, b, s in ((R_OUT, C, WS * WS), (R_RT, E, WS), (R_PJ, C, WS * WS), (R_GT, E, WS)):
                nc.scalar.activation(rowh[:, a:a + b], rowr[:, a:a + b], ACT.Copy, scale=s).then_inc(cols_ready, 1)
            act.wait_ge(tokw_ready, 1)
            nc.scalar.activation(wt_hi[:], wf[:], ACT.Copy, scale=WS).then_inc(tokw_ready, 1)
            for t in range(NT):
                for i in range(2):
                    name = ("tokT", t, i)
                    filled(name)
                    if i == 0 and t >= 2:
                        act.wait_ge(psum_filled, f.done[("tok", t - 2)])
                    nc.scalar.activation(tx_hi[t % 2][:, 4 * i:4 * i + 4, :], bank(name), ACT.Copy).then_inc(hi_ready, 1)
                    hn[0] += 1
                if t == 0:
                    act.wait_ge(loaded["early"], 16)
                    nc.scalar.activation(early_a[:, 0, :], raw_early[:, 0], ACT.Copy, scale=WS).then_inc(wearly, 1)
                    nc.scalar.activation(early_b[:, 0, :], raw_early[:, 1], ACT.Copy, scale=WS).then_inc(wearly, 1)

            def high_part(raw, hi, lo, scale):
                nc.scalar.activation(hi, raw, ACT.Copy, scale=scale).then_inc(act_step, 1)
                ast[0] += 1
                nc.scalar.activation(raw, raw, ACT.Copy, scale=scale).then_inc(whi, 1)
            ast = [0]

            def x_high(phase):
                for pr in range(4):
                    name = ("x", phase, pr)
                    filled(name)
                    nc.scalar.activation(X_hi[:, 2 * pr:2 * pr + 2],
                                         bank(name).rearrange("p (t k n) -> p t k n", t=2, k=2),
                                         ACT.Copy).then_inc(hi_ready, 1)
                    hn[0] += 1

            def x_high_affine():
                for pr in range(4):
                    act.wait_ge(xf_ready, xf[0] + 1)
                    xf[0] += 1
                    nc.scalar.activation(X_hi[:, 2 * pr:2 * pr + 2], xt_f[:, pr], ACT.Copy).then_inc(hi_ready, 1)
                    hn[0] += 1
            xf = [0]

            ev = [0]

            def attention(a, hf):
                cb = C_QB0 if a == 0 else C_QB1
                for i, (s, o, m) in enumerate(SLOTS):
                    name = ("qkv", a, hf, s)
                    filled(name)
                    nc.scalar.activation(pairs[s][0:m, 0, :], bank(name)[0:m], ACT.Identity,
                                         bias=col16[0:m, cb + i:cb + i + 1]).then_inc(hi_ready, 1)
                    hn[0] += 1
                for pr in range(2):
                    name = ("st", a, hf, pr)
                    filled(name)
                    v = bank(name).rearrange("p (t k n) -> p t k n", t=2, k=2)
                    nc.scalar.activation(ST[:, pr, :, 0], v[:, :, 0], ACT.Copy).then_inc(act_step, 1)
                    nc.scalar.activation(ST[0:CB, pr, :, 1], v[0:CB, :, 1], ACT.Copy).then_inc(st_ready, 1)
                    ast[0] += 1
                for hl in range(2):
                    for g in range(4):
                        if g % 2 == 0:
                            continue
                        name = ("va", a, hf, hl, g)
                        filled(name)
                        nc.scalar.activation(VA[:, hl, 8 * g:8 * g + 8, :],
                                             bank(name).bitcast(F16).rearrange("p (s n) -> p s n", s=8),
                                             ACT.Copy).then_inc(v_act_ready, 1)
                        ev[0] += 1
                    for g in range(2):
                        name = ("vb", a, hf, hl, g)
                        filled(name)
                        nc.scalar.activation(VB[0:CB, hl, 16 * g:16 * g + 16, :],
                                             bank(name)[0:CB].bitcast(F16).rearrange("p (s n) -> p s n", s=16),
                                             ACT.Copy).then_inc(v_act_ready, 1)
                        ev[0] += 1
                    if hl == 0:
                        for pr in range(2):
                            act.wait_ge(smax_ready, 2 * (2 * a + hf) + pr + 1)
                            nc.scalar.activation(SM[:, pr], SM[:, pr], ACT.Exp).then_inc(exp_ready, 1)
                for pr in range(2):
                    name = ("pt", a, hf, pr)
                    filled(name)
                    v = bank(name).rearrange("p (t k n) -> p t k n", t=2, k=2)
                    nc.scalar.activation(PT[:, 0, 2 * pr:2 * pr + 2, 0], v[:, :, 0], ACT.Copy).then_inc(act_step, 1)
                    ast[0] += 1
                    nc.scalar.activation(PT[0:CB, 0, 2 * pr:2 * pr + 2, 1], v[0:CB, :, 1], ACT.Copy).then_inc(hi_ready, 1)
                    hn[0] += 1
                for pr in range(2):
                    name = ("ot", a, hf, pr)
                    filled(name)
                    v = bank(name).rearrange("p (t k n) -> p t k n", t=2, k=2)
                    nc.scalar.activation(O_hi[:, 2 * pr:2 * pr + 2, 0], v[:, :, 0], ACT.Copy).then_inc(act_step, 1)
                    ast[0] += 1
                    nc.scalar.activation(O_hi[0:CB, 2 * pr:2 * pr + 2, 1], v[0:CB, :, 1], ACT.Copy).then_inc(hi_ready, 1)
                    hn[0] += 1
            x_high("attn0")
            act.wait_ge(loaded["moe"], 16)
            for piece in moe_pieces[:N1]:
                high_part(*piece)
            attention(0, 0)
            act.wait_ge(loaded["moe"], 32)
            for piece in moe_pieces[N1:]:
                high_part(*piece)
            attention(0, 1)
            x_high("moe")
            act.wait_ge(gmax_ready, 1)
            nc.scalar.activation(gat[:, 1], gat[:, 1], ACT.Exp).then_inc(exp_ready, 1)
            lp = [0]

            def late_high():
                if lp[0] < NL:
                    if lp[0] == 0:
                        act.wait_ge(loaded["late"], 16)
                    if lp[0] == 2 * len(late_cuts):
                        act.wait_ge(loaded["full"], 16)
                    high_part(*late_pieces[lp[0]])
                    lp[0] += 1
            for u in range(UNITS):
                for n, c, slot in unit_chunks(u):
                    filled(("h", n))
                    if n >= 3:
                        act.wait_ge(hp_ready, n - 2)
                    b = col[:, C_B1 + c:C_B1 + c + 1]
                    nc.scalar.activation(ge[n % 3], bank(("h", n)), ACT.Gelu, bias=b,
                                         scale=1.0 / WS).then_inc(act_step, 1)
                    ast[0] += 1
                    if u >= 2:
                        filled(("y", u - 2, 1))
                    nc.scalar.activation(hgh[slot], bank(("h", n)), ACT.Gelu, bias=b,
                                         scale=1.0 / WS).then_inc(gelu_ready, 1)
                if u > 1:
                    late_high()
                    late_high()
            for hf in range(2):
                name = ("ct", hf)
                filled(name)
                nc.scalar.activation(ctT[:, HALF * hf:HALF * (hf + 1)], bank(name)[0:E], ACT.Copy).then_inc(ct_ready, 1)
            while lp[0] < NL:
                late_high()
            x_high_affine()
            for i, n in enumerate("kvr"):
                dst, fn, sc = ((rK, ACT.Copy, 1 / WS), (rV, ACT.Copy, 1 / WS), (rT, ACT.Tanh, 0.5 / WS))[i]
                for part in range(3):
                    name = (n, part)
                    filled(name)
                    nc.scalar.activation(dst[:, 512 * part:512 * part + 512], bank(name), fn, scale=sc).then_inc(kvr_ready, 1)
            for i, (e1, e2) in enumerate(((E1f, E2f), (E1b, E2b))):
                act.wait_ge(rd_ready, i + 1)
                nc.scalar.activation(e2[:, 0:NR], e1[:, 0:NR], ACT.Relu).then_inc(act_step, 1)
                ast[0] += 1
                act.wait_ge(act_step, ast[0])
                nc.scalar.activation(e1[:, 0:NR], e1[:, 0:NR], ACT.Relu, scale=-1.0).then_inc(act_step, 1)
                nc.scalar.activation(e2[:, 0:NR], e2[:, 0:NR], ACT.Exp, scale=-1.0).then_inc(re_ready, 1)
                ast[0] += 1
                act.wait_ge(act_step, ast[0])
                nc.scalar.activation(e1[:, 0:NR], e1[:, 0:NR], ACT.Exp, scale=-1.0).then_inc(re_ready, 1)
            for i, e in enumerate((E1f, E1b, E2f)):
                act.wait_ge(rd_ready, i + 3)
                nc.scalar.activation(e[:, 0:NR], e[:, 0:NR], ACT.Exp).then_inc(re_ready, 1)
            act.wait_ge(sy_ready, 1)
            nc.scalar.activation(sy_ah, E1b[:, 0:TOK], ACT.Copy).then_inc(hi_ready, 1)
            nc.scalar.activation(sy_bh, E1b[:, TOK:NR], ACT.Copy).then_inc(hi_ready, 1)
            hn[0] += 2
            x_high_affine()
            for hf in range(2):
                for m in range(6):
                    n = 6 * hf + m
                    name = ("kf", hf, m)
                    filled(name)
                    if n >= 2:
                        act.wait_ge(sq_ready, n - 1)
                    nc.scalar.activation(kfr[m % 2], bank(name), ACT.Relu, scale=1 / WS).then_inc(relu_ready, 1)
                    act.wait_ge(sq_ready, n + 1)
                    if hf and m == 0:
                        act.wait_ge(psum_filled, f.done[("kv", 0, 1)])
                    nc.scalar.activation(kfh[:, m], kfs[m % 2], ACT.Copy).then_inc(hi_ready, 1)
                    hn[0] += 1
                for pr in range(2):
                    name = ("r", hf, pr)
                    filled(name)
                    nc.scalar.activation(tr_[:, pr], bank(name)[:, 0:2 * C], ACT.Tanh, scale=0.5 / WS).then_inc(tanh_ready, 1)
            x_high("attn1")
            act.wait_ge(gmax_ready, 2)
            nc.scalar.activation(gat[:, 1], gat[:, 1], ACT.Exp).then_inc(exp_ready, 1)
            for hf in range(2):
                sl = slice(HALF * hf, HALF * (hf + 1))
                name = ("ce", hf)
                filled(name)
                nc.scalar.activation(ceF[:, sl], bank(name), ACT.Copy).then_inc(ce_ready, 1)
                nc.scalar.activation(cstack[0:E, sl], bank(name)[0:E], ACT.Copy).then_inc(act_step, 1)
                nc.scalar.activation(cstack[64:64 + E, sl], bank(name)[0:E], ACT.Copy).then_inc(hi_ready, 1)
                ast[0] += 1
                hn[0] += 1
                act.wait_ge(hw_ready, 2 * hf + 1)
                nc.scalar.activation(hw_hi[:, sl], hwF, ACT.Copy).then_inc(hi_ready, 1)
                hn[0] += 1
                attention(1, hf)

        @block.vector
        def _(dve):
            V = nc.vector
            chain = [0]
            hn = [0]
            nn = [0]
            ev = [0]

            def link(ins):
                ins.then_inc(dve_step, 1)
                chain[0] += 1
                dve.wait_ge(dve_step, chain[0])

            def filled(name):
                dve.wait_ge(psum_filled, f.done[name])

            def released(name):
                dve.wait_ge(bank_free[f.bank[name]], f.release[name][1])

            def next_high():
                hn[0] += 1
                dve.wait_ge(hi_ready, hn[0])

            dve.wait_ge(loaded["consts"], 16)
            wgt = K[:, K_BNW:K_BNW + 30]

            def tok_stats(t):
                dve.wait_ge(x_in[t % 3], 16 * (t // 3 + 1))
                a = 0
                for i, (n, _) in enumerate(GROUPS):
                    ins = V.bn_stats(stats[:, t % 2, 6 * i:6 * i + 6], tok_in[t % 3][:, a:a + n])
                    a += n
                link(ins)
                link(V.tensor_tensor(wstats[:, t % 2], stats[:, t % 2], wgt, ALU.mult))
                V.bn_aggr(mv[:, t], wstats[:, t % 2]).then_inc(var_ready, 1)

            def tok_norm(t):
                dve.wait_ge(rstd_ready, t + 1)
                if t >= 2:
                    dve.wait_ge(psum_filled, f.done[("tokT", t - 2, 1)])
                dst = tx_n[t % 2]
                V.tensor_scalar(dst[:, 0:FEAT], tok_in[t % 3], mv[:, t, 0:1], rstd[:, t:t + 1],
                                ALU.subtract, ALU.mult).then_inc(dve_step, 1)
                chain[0] += 1
                V.tensor_scalar(dst[:, FEAT:1024], tok_in[t % 3][:, FEAT - 64:FEAT], mv[:, t, 0:1], rstd[:, t:t + 1],
                                ALU.subtract, ALU.mult).then_inc(tokn_ready, 1)

            def tok_low(t):
                for i in range(2):
                    name = ("tokT", t, i)
                    next_high()
                    b = bank(name).rearrange("p (k n) -> p k n", k=4)
                    if i == 0:
                        V.tensor_tensor(tx_lo[t % 2][:, 0:4, :], b, tx_hi[t % 2][:, 0:4, :],
                                        ALU.subtract).then_inc(bank_free[f.bank[name]], 1)
                    else:
                        V.tensor_tensor(tx_lo[t % 2][:, 4:7, :], b[:, 0:3], tx_hi[t % 2][:, 4:7, :], ALU.subtract)
                        V.tensor_tensor(tx_hi[t % 2][64:P, 7, :], b[64:P, 3], tx_hi[t % 2][64:P, 7, :],
                                        ALU.subtract).then_inc(tokx_ready, 1)

            def tok_out(t):
                name = ("tok", t)
                filled(name)
                V.scalar_tensor_tensor(H[:, t], bank(name)[:, 0:C], 1.0 / WS, tokb[:], ALU.mult,
                                       ALU.add).then_inc(bank_free[f.bank[name]], 1)
                dve.wait_ge(bank_free[f.bank[name]], f.release[name][1])

            tok_stats(0)
            dve.wait_ge(loaded["tokg"], 32)
            dve.wait_ge(const_ready, 1)
            for k in range(6):
                dve.wait_ge(loaded["tokw"], 16 * 7)
                for s in range(5):
                    g = gbt[:, 5 * k + s:5 * k + s + 1]
                    if s == 0:
                        link(V.tensor_scalar(wf[:, k], raw_w[:, k, 0], g, None, ALU.mult))
                    elif s < 4 or k < 5:
                        link(V.scalar_tensor_tensor(wf[:, k], raw_w[:, k, s], g, wf[:, k], ALU.mult, ALU.add))
                    else:
                        link(V.scalar_tensor_tensor(wf[:, k], raw_w[:, k, s], g, wf[:, k], ALU.mult, ALU.add))
                if k == 0:
                    tok_norm(0)
                if k == 2:
                    tok_stats(1)
            link(V.tensor_scalar(wf[:, 6], raw_wh[:, 0], gbt[:, 30:31], None, ALU.mult))
            V.tensor_scalar(wf[:, 7], raw_wh[:, 1], gbt[:, 31:32], None, ALU.mult).then_inc(tokw_ready, 1)
            tok_norm(1)
            tok_low(0)
            dve.wait_ge(tokw_ready, 2)
            V.scalar_tensor_tensor(wt_lo[:], wf[:], WS, wt_hi[:], ALU.mult, ALU.subtract).then_inc(tokw_ready, 1)
            dve.wait_ge(cols_ready, 6)
            for a, b, s in ((R_OUT, C, WS * WS), (R_RT, E, WS), (R_PJ, C, WS * WS), (R_GT, E, WS)):
                V.scalar_tensor_tensor(rowl[:, a:a + b], rowr[:, a:a + b], s, rowh[:, a:a + b], ALU.mult,
                                       ALU.subtract).then_inc(cols_ready, 1)
            filled("beta")
            V.tensor_tensor(tokb[:], tokb[:], bank("beta")[:, 0:C], ALU.add).then_inc(bank_free[f.bank["beta"]], 1)
            dve.wait_ge(bank_free[f.bank["beta"]], 1)
            dve.wait_ge(wearly, 2)
            V.scalar_tensor_tensor(early_a[:, 1], raw_early[:, 0], WS, early_a[:, 0], ALU.mult,
                                   ALU.subtract).then_inc(wearly, 1)
            V.scalar_tensor_tensor(early_b[0:CB, 1], raw_early[0:CB, 1], WS, early_b[0:CB, 0], ALU.mult,
                                   ALU.subtract).then_inc(wearly, 1)
            nn[0] = NT

            def ln_stats(t, src):
                link(V.bn_stats(stats[:, t % 2, 0:6], src[:, t]))
                V.bn_aggr(mv[:, t], stats[:, t % 2, 0:6]).then_inc(var_ready, 1)
                nn[0] += 1
                return nn[0]

            def ln_norm(t, src, n, k):
                dve.wait_ge(rstd_ready, n)
                if k >= 4:
                    dve.wait_ge(psum_filled, x_fill(k - 4))
                V.tensor_scalar(xn[:, t % 4, 0:C], src[:, t], mv[:, t, 0:1], rstd[:, t:t + 1], ALU.subtract,
                                ALU.mult).then_inc(dve_step, 1)
                chain[0] += 1
                V.tensor_scalar(xn[:, t % 4, C:2 * P], src[:, t, P:C], mv[:, t, 0:1], rstd[:, t:t + 1], ALU.subtract,
                                ALU.mult).then_inc(xn_ready, 1)

            def x_fill(k):
                return f.done[("x", PHASES[k // NT], k % NT // 2)]

            xc = [0]
            xr = [0]

            def norm_tiles(src, ready=None):
                last = None
                for t in range(NT + 1):
                    if t < NT:
                        if ready:
                            ready(t)
                        now = ln_stats(t, src)
                    if t:
                        ln_norm(t - 1, src, last, xc[0])
                        xc[0] += 1
                    last = now

            def x_low(phase):
                for pr in range(4):
                    name = ("x", phase, pr)
                    next_high()
                    b = bank(name).rearrange("p (t k n) -> p t k n", t=2, k=2)
                    V.tensor_tensor(X_lo[:, 2 * pr:2 * pr + 2], b[:, :, 0], X_hi[:, 2 * pr:2 * pr + 2, 0], ALU.subtract)
                    xr[0] += 1
                    V.tensor_tensor(X_hi[64:P, 2 * pr:2 * pr + 2, 1], b[64:P, :, 1], X_hi[64:P, 2 * pr:2 * pr + 2, 1],
                                    ALU.subtract).then_inc(x_ready, 1)

            def x_affine(phase, wa, wb, ba, bb):
                for pr in range(4):
                    name = ("x", phase, pr)
                    filled(name)
                    b = bank(name).rearrange("p (t k n) -> p t k n", t=2, k=2)
                    V.tensor_scalar(xt_f[:, pr, :, 0], b[:, :, 0], col[:, wa:wa + 1], col[:, ba:ba + 1],
                                    ALU.mult, ALU.add).then_inc(dve_step, 1)
                    chain[0] += 1
                    V.tensor_scalar(xt_f[:, pr, :, 1], b[:, :, 1], col[:, wb:wb + 1], col[:, bb:bb + 1],
                                    ALU.mult, ALU.add).then_inc(xf_ready, 1)
                    xfc[0] += 1
                for pr in range(4):
                    next_high()
                    V.tensor_tensor(X_lo[:, 2 * pr:2 * pr + 2], xt_f[:, pr, :, 0], X_hi[:, 2 * pr:2 * pr + 2, 0],
                                    ALU.subtract)
                    xr[0] += 1
                    V.tensor_tensor(X_hi[64:P, 2 * pr:2 * pr + 2, 1], xt_f[64:P, pr, :, 1],
                                    X_hi[64:P, 2 * pr:2 * pr + 2, 1], ALU.subtract).then_inc(x_ready, 1)
            xfc = [0]

            def attention(a, hf, after_pair):
                cb = C_QB0 if a == 0 else C_QB1
                n0 = 2 * a + hf

                def low(i):
                    s, o, m = SLOTS[i]
                    name = ("qkv", a, hf, s)
                    next_high()
                    V.scalar_tensor_tensor(pairs[s][0:m, 1, :], bank(name)[0:m], col16[0:m, cb + i:cb + i + 1],
                                           pairs[s][0:m, 0, :], ALU.add, ALU.subtract).then_inc(qkv_ready, 1)

                def spread(dst, src, nh, mask, i):
                    dve.wait_ge(qkv_ready, 5 * n0 + i + 1)
                    for l in range(2):
                        v = dst[:, l].rearrange("p s (h j) -> p s h j", h=nh)
                        w = src[:, l].rearrange("p (s j) -> p s j", j=SEQ)
                        for h in range(nh):
                            ins = V.tensor_scalar(v[:, :, h], w, K[:, mask + h:mask + h + 1], None, ALU.mult)
                    ins.then_inc(bd_ready, 1)

                low(0)
                low(1)
                spread(KAbd, pairs["KA"], HA, K_HM, 1)
                low(2)
                low(3)
                spread(KVBbd, pairs["KVB"], HB, K_HMB, 3)
                low(4)
                spread(VAbd, pairs["VA"], HA, K_HM, 2)

                def softmax_in(pr):
                    name = ("s", a, hf, pr)
                    filled(name)
                    s = bank(name)[:, 0:2 * C].rearrange("p (h j) -> p h j", j=SEQ)
                    sc = HD ** -0.5 / (WS * WS)
                    if a == 0:
                        am = K[:, K_AM:K_AM + SEQ][:, None, :].broadcast_to([P, 2 * NH, SEQ])
                        V.scalar_tensor_tensor(SM[:, pr], s, sc, am, ALU.mult, ALU.add).then_inc(
                            bank_free[f.bank[name]], 1)
                    else:
                        V.tensor_scalar(SM[:, pr], s, sc, None, ALU.mult).then_inc(bank_free[f.bank[name]], 1)
                    dve.wait_ge(bank_free[f.bank[name]], f.release[name][1])
                    link(V.tensor_reduce(smx[:, pr, 0], SM[:, pr], AX, ALU.max))
                    V.tensor_tensor(SM[:, pr], SM[:, pr], smx[:, pr, 0][:, :, None].broadcast_to([P, 2 * NH, SEQ]),
                                    ALU.subtract).then_inc(smax_ready, 1)

                def softmax_out(pr):
                    dve.wait_ge(exp_ready, en[0] + 1)
                    en[0] += 1
                    link(V.tensor_reduce(smx[:, pr, 1], SM[:, pr], AX, ALU.add))
                    link(V.reciprocal(smx[:, pr, 2], smx[:, pr, 1]))
                    V.tensor_tensor(SM[:, pr], SM[:, pr], smx[:, pr, 2][:, :, None].broadcast_to([P, 2 * NH, SEQ]),
                                    ALU.mult).then_inc(p_ready, 1)

                def values(hl):
                    for g in (0, 2):
                        name = ("va", a, hf, hl, g)
                        filled(name)
                        V.tensor_copy(VA[:, hl, 8 * g:8 * g + 8, :],
                                      bank(name).bitcast(F16).rearrange("p (s n) -> p s n", s=8)).then_inc(v_dve_ready, 1)
                        ev[0] += 1

                values(0)
                softmax_in(0)
                softmax_in(1)
                softmax_out(0)
                softmax_out(1)
                values(1)
                for pr in range(2):
                    name = ("pt", a, hf, pr)
                    next_high()
                    v = bank(name).rearrange("p (t k n) -> p t k n", t=2, k=2)
                    sl = slice(2 * pr, 2 * pr + 2)
                    V.tensor_tensor(PT[:, 1, sl, 0], v[:, :, 0], PT[:, 0, sl, 0], ALU.subtract)
                    V.tensor_tensor(PT[0:CB, 1, sl, 1], v[0:CB, :, 1], PT[0:CB, 0, sl, 1],
                                    ALU.subtract).then_inc(pt_ready, 1)
                for pr in range(2):
                    name = ("ot", a, hf, pr)
                    next_high()
                    v = bank(name).rearrange("p (t k n) -> p t k n", t=2, k=2)
                    sl = slice(2 * pr, 2 * pr + 2)
                    V.tensor_tensor(O_lo[:, sl], v[:, :, 0], O_hi[:, sl, 0], ALU.subtract)
                    V.tensor_tensor(O_hi[64:P, sl, 1], v[0:CB, :, 1], O_hi[0:CB, sl, 1],
                                    ALU.subtract).then_inc(ot_ready, 1)
                for pr in range(2):
                    name = ("pj", a, hf, pr)
                    filled(name)
                    t = 4 * hf + 2 * pr
                    V.scalar_tensor_tensor(H[:, t:t + 2], bank(name)[:, 0:2 * C].rearrange("p (t n) -> p t n", t=2),
                                           1.0 / (WS * WS), H[:, t:t + 2], ALU.mult,
                                           ALU.add).then_inc(bank_free[f.bank[name]], 1)
                    dve.wait_ge(bank_free[f.bank[name]], f.release[name][1])
                    after_pair(2 * hf + pr)
            en = [0]

            def gates(which, twice):
                name = f"router{which}"
                filled(name)
                lg = bank(name)[:, 0:NT * E].rearrange("p (t e) -> p t e", t=NT)
                V.tensor_scalar(gat[:, 0], lg, 1.0 / WS, None, ALU.mult).then_inc(bank_free[f.bank[name]], 1)
                dve.wait_ge(bank_free[f.bank[name]], f.release[name][1])
                link(V.tensor_reduce(gsum[:, 0], gat[:, 0], AX, ALU.max))
                V.tensor_tensor(gat[:, 1], gat[:, 0], gsum[:, 0][:, :, None].broadcast_to([P, NT, E]),
                                ALU.subtract).then_inc(gmax_ready, 1)
                dve.wait_ge(exp_ready, en[0] + 1)
                en[0] += 1
                link(V.tensor_reduce(gsum[:, 1], gat[:, 1], AX, ALU.add))
                link(V.reciprocal(gsum[:, 2], gsum[:, 1]))
                link(V.tensor_tensor(gat[:, 2], gat[:, 1], gsum[:, 2][:, :, None].broadcast_to([P, NT, E]), ALU.mult))
                full4 = [P, NT, E, E]
                of = gat[:, 2][:, :, None, :].broadcast_to(full4)
                oe = gat[:, 2][:, :, :, None].broadcast_to(full4)
                tri = K[:, K_TRI:K_TRI + E * E].rearrange("p (e f) -> p e f", e=E)[:, None].broadcast_to(full4)
                link(V.tensor_tensor(rk[:], of, oe, ALU.is_equal))
                link(V.tensor_tensor(rk[:], rk[:], tri, ALU.mult))
                link(V.tensor_tensor(rk2[:], of, oe, ALU.is_gt))
                link(V.tensor_tensor(rk[:], rk[:], rk2[:], ALU.add))
                link(V.tensor_reduce(gat[:, 3], rk[:], AX, ALU.add))
                link(V.scalar_tensor_tensor(gat[:, 4], gat[:, 3], 1.5, gat[:, 2], ALU.is_lt, ALU.mult))
                if twice:
                    link(V.tensor_scalar(gat[:, 5], gat[:, 4], 2.0, None, ALU.mult))

            norm_now = []
            tok_stats(2)
            for t in range(NT):
                if t + 2 < NT:
                    tok_norm(t + 2)
                if t + 3 < NT:
                    tok_stats(t + 3)
                if t + 1 < NT:
                    tok_low(t + 1)
                tok_out(t)
            norm_tiles(H)
            x_low("attn0")
            attention(0, 0, lambda pr: None)
            attention(0, 1, lambda pr: None)
            norm_tiles(H)
            x_low("moe")
            dve.wait_ge(loaded["b2"], 16)
            link(V.tensor_scalar(b2s[:], b2s[:], WS, None, ALU.mult))
            gates(0, False)
            V.tensor_scalar(gat[:, 5], gat[:, 4], 1.0 / WS, None, ALU.mult).then_inc(gate_ready, 1)
            dve.wait_ge(gate_ready, 1)
            for u in range(UNITS + 1):
                if u < UNITS:
                    for n, _, slot in unit_chunks(u):
                        dve.wait_ge(gelu_ready, n + 1)
                        V.tensor_tensor(hgl[slot], ge[n % 3], hgh[slot], ALU.subtract).then_inc(hp_ready, 1)
                if u:
                    hf, e = divmod(u - 1, E)
                    for pr in range(2):
                        name = ("y", u - 1, pr)
                        filled(name)
                        if e:
                            released(("y", u - 2, pr))
                        for j in range(2):
                            t = 4 * hf + 2 * pr + j
                            ins = V.scalar_tensor_tensor(H[:, t], bank(name)[:, C * j:C * j + C], gat[:, 5, t, e:e + 1],
                                                         H[:, t], ALU.mult, ALU.add)
                        ins.then_inc(bank_free[f.bank[name]], 1)
            for pr in range(4):
                name = ("b2", pr)
                filled(name)
                released(("y", E * (pr // 2) + E - 1, pr % 2))
                V.scalar_tensor_tensor(H[:, 2 * pr:2 * pr + 2], bank(name)[:, 0:2 * C].rearrange("p (t n) -> p t n", t=2),
                                       1.0 / WS, H[:, 2 * pr:2 * pr + 2], ALU.mult,
                                       ALU.add).then_inc(bank_free[f.bank[name]], 1)
                dve.wait_ge(bank_free[f.bank[name]], f.release[name][1])
            for t in range(NT):
                n = ln_stats(t, H)
                dve.wait_ge(rstd_ready, n)
                link(V.tensor_scalar(Z[:, t], H[:, t], mv[:, t, 0:1], rstd[:, t:t + 1], ALU.subtract, ALU.mult))
                n = ln_stats(t, Z)
                ln_norm(t, Z, n, xc[0])
                xc[0] += 1
            x_affine("mix1", C_LN1WA, C_LN1WB, C_LN1BA, C_LN1BB)
            link(V.tensor_scalar(col[:, C_DECA:C_FIRB + 1], col[:, C_DECA:C_FIRB + 1], 1.0 / SEQ, None, ALU.mult))
            link(V.memset(rW0[:, 0:NR], 0.0))
            link(V.tensor_scalar(rW0[:, 0:TOK], rW0[:, 0:TOK], col[:, C_DECA:C_DECA + 1], None, ALU.add))
            link(V.tensor_scalar(rW0[:, TOK:NR], rW0[:, TOK:NR], col[:, C_DECB:C_DECB + 1], None, ALU.add))
            link(V.memset(rW0[:, 0:NR:SEQ], -BIG))
            parts = ((0, TOK, C_DECA, C_FIRA), (TOK, NR, C_DECB, C_FIRB))
            dve.wait_ge(kvr_ready, 3)

            def scan(dst, d0, d1, back, op0, op1, d0_flip=True):
                for a, b, _, _ in parts:
                    if back:
                        x = d0[:, a:b][:, ::-1] if d0_flip else d0[:, a:b]
                        ins = V.tensor_tensor_scan(dst[:, a:b][:, ::-1], x, d1[:, a:b][:, ::-1], 0.0, op0, op1)
                    else:
                        ins = V.tensor_tensor_scan(dst[:, a + 1:b + 1], d0[:, a:b], d1[:, a:b], 0.0, op0, op1)
                    link(ins)

            def before(buf, back):
                return buf[:, 1:NR + 1] if back else buf[:, 0:NR]

            for i, (M, D) in enumerate(((Mf, E1f), (Mb, E1b))):
                scan(M, rW0, rK, i, ALU.add, ALU.max, d0_flip=False)
                link(V.memset(M[:, 0:RW:SEQ], -BIG))
                m = before(M, i)
                for a, b, w, _ in parts:
                    ins = V.scalar_tensor_tensor(D[:, a:b], m[:, a:b], col[:, w:w + 1], rK[:, a:b], ALU.add,
                                                 ALU.subtract)
                    if a == 0:
                        link(ins)
                ins.then_inc(rd_ready, 1)
            dve.wait_ge(kvr_ready, 9)
            for i, (e1, e2, A, B) in enumerate(((E1f, E2f, Af, Bf), (E1b, E2b, Ab, Bb))):
                dve.wait_ge(re_ready, 2 * i + 2)
                scan(B, e1, e2, i, ALU.mult, ALU.add)
                link(V.tensor_tensor(e2[:, 0:NR], e2[:, 0:NR], rV[:, 0:NR], ALU.mult))
                scan(A, e1, e2, i, ALU.mult, ALU.add)
                link(V.memset(A[:, 0:RW:SEQ], 0.0))
                link(V.memset(B[:, 0:RW:SEQ], 0.0))
            mf, mb = before(Mf, 0), before(Mb, 1)
            link(V.tensor_tensor(E2b[:, 0:NR], mf, mb, ALU.max))
            for a, b, _, u in parts:
                link(V.scalar_tensor_tensor(E2b[:, a:b], rK[:, a:b], col[:, u:u + 1], E2b[:, a:b], ALU.add, ALU.max))
            V.tensor_tensor(E1f[:, 0:NR], mf, E2b[:, 0:NR], ALU.subtract).then_inc(rd_ready, 1)
            V.tensor_tensor(E1b[:, 0:NR], mb, E2b[:, 0:NR], ALU.subtract).then_inc(rd_ready, 1)
            for a, b, _, u in parts:
                ins = V.scalar_tensor_tensor(E2f[:, a:b], rK[:, a:b], col[:, u:u + 1], E2b[:, a:b], ALU.add,
                                             ALU.subtract)
                if a == 0:
                    link(ins)
            ins.then_inc(rd_ready, 1)
            dve.wait_ge(re_ready, 7)
            link(V.tensor_tensor(Mf[:, 0:NR], E1f[:, 0:NR], before(Af, 0), ALU.mult))
            V.tensor_tensor(Mb[:, 0:NR], E1b[:, 0:NR], before(Ab, 1), ALU.mult).then_inc(den_in, 1)
            dve.wait_ge(den_in, 1)
            link(V.tensor_tensor(Mf[:, 0:NR], Mf[:, 0:NR], Mb[:, 0:NR], ALU.add))
            link(V.tensor_tensor(rV[:, 0:NR], E2f[:, 0:NR], rV[:, 0:NR], ALU.mult))
            link(V.tensor_tensor(Mf[:, 0:NR], Mf[:, 0:NR], rV[:, 0:NR], ALU.add))
            link(V.scalar_tensor_tensor(Mf[:, 0:NR], rT[:, 0:NR], 1.0, Mf[:, 0:NR], ALU.add, ALU.mult))
            dve.wait_ge(den_ready, 1)
            link(V.reciprocal(E2b[:, 0:NR], E1f[:, 0:NR]))
            V.tensor_tensor(E1b[:, 0:NR], Mf[:, 0:NR], E2b[:, 0:NR], ALU.mult).then_inc(sy_ready, 1)
            next_high()
            V.tensor_tensor(sy_al, E1b[:, 0:TOK], sy_ah, ALU.subtract).then_inc(sy_ready, 1)
            next_high()
            V.tensor_tensor(sy_bl, E1b[:, TOK:NR], sy_bh, ALU.subtract).then_inc(sy_ready, 1)

            def wo_out(t):
                if t % 2 == 0:
                    name = ("wo", t // 2)
                    filled(name)
                    V.scalar_tensor_tensor(Z[:, t:t + 2], bank(name)[:, 0:2 * C].rearrange("p (t n) -> p t n", t=2),
                                           0.5 / WS, Z[:, t:t + 2], ALU.mult, ALU.add).then_inc(
                                               bank_free[f.bank[name]], 1)
                    dve.wait_ge(bank_free[f.bank[name]], f.release[name][1])
            norm_tiles(Z, wo_out)
            x_affine("mix2", C_LN2WA, C_LN2WB, C_LN2BA, C_LN2BB)
            for hf in range(2):
                for m in range(6):
                    n = 6 * hf + m
                    dve.wait_ge(relu_ready, n + 1)
                    if n >= 2:
                        dve.wait_ge(kf_ready, n - 1)
                    V.tensor_tensor(kfs[m % 2], kfr[m % 2], kfr[m % 2], ALU.mult).then_inc(sq_ready, 1)
                    next_high()
                    V.tensor_tensor(kfl[:, m], kfs[m % 2], kfh[:, m], ALU.subtract).then_inc(kf_ready, 1)
                for pr in range(2):
                    name = ("kv", hf, pr)
                    t = 4 * hf + 2 * pr
                    filled(name)
                    dve.wait_ge(tanh_ready, 2 * hf + pr + 1)
                    V.scalar_tensor_tensor(uu[:, pr], tr_[:, pr], 1.0, bank(name)[:, 0:2 * C], ALU.add,
                                           ALU.mult).then_inc(bank_free[f.bank[name]], 1)
                    dve.wait_ge(bank_free[f.bank[name]], f.release[name][1])
                    u = uu[:, pr].rearrange("p (t n) -> p t n", t=2)
                    link(V.scalar_tensor_tensor(Z[:, t:t + 2], u, 0.5 / WS, Z[:, t:t + 2], ALU.mult, ALU.add))
                    link(V.tensor_tensor(H[:, t:t + 2], H[:, t:t + 2], Z[:, t:t + 2], ALU.add))
            norm_tiles(H)
            x_low("attn1")
            gates(1, True)
            V.tensor_copy(crep1.rearrange("p t (r e) -> p t r e", e=E),
                          gat[:, 5][:, :, None, :].broadcast_to([P, NT, 16, E])).then_inc(gate_ready, 1)
            link(V.memset(cstack[0:96, :], 0.0))
            dve.sem_inc(gate_ready, 1)
            for hf in range(2):
                sl = slice(HALF * hf, HALF * (hf + 1))
                name = ("ce", hf)
                next_high()
                V.tensor_tensor(cstack[32:32 + E, sl], bank(name)[0:E], cstack[0:E, sl],
                                ALU.subtract).then_inc(bank_free[f.bank[name]], 1)
                name = ("la", hf)
                filled(name)
                dve.wait_ge(ce_ready, hf + 1)
                V.scalar_tensor_tensor(hwF, bank(name), col16[:, C_BA:C_BA + 1], ceF[:, sl], ALU.add,
                                       ALU.mult).then_inc(hw_ready, 1)
                next_high()
                V.tensor_tensor(hw_lo[:, sl], hwF, hw_hi[:, sl], ALU.subtract).then_inc(hw_ready, 1)
                attention(1, hf, lambda pr: dve.sem_inc(h_ready, 1))

        @block.tensor
        def _(pe):
            T_ = nc.tensor

            def free(name):
                if f.before[name]:
                    by, count = f.release[f.before[name]]
                    pe.wait_ge(readers[by], count)

            def mm(o, w, x, start, stop):
                return T_.matmul(o, w, x, start=start, stop=stop, skip_group_check=True)

            ident = K[:, K_ID:K_ID + P]

            pe.wait_ge(loaded["consts"], 16)
            pe.wait_ge(loaded["tokg"], 32)
            pe.wait_ge(loaded["tokw"], 16 * 7)

            def beta():
                b = bank("beta")[:, 0:C]
                n = 0
                for k in range(8):
                    for s in range(5 if k < 6 else 1):
                        w = raw_w[:, k, s] if k < 6 else raw_wh[:, k - 6]
                        c = 32 + n
                        last = mm(b, gbt[:, c:c + 1].broadcast_to([P, P]), w, n == 0, n == 31)
                        n += 1
                last.then_inc(psum_filled, 1)
            beta()

            def tok_turn(t):
                pe.wait_ge(tokn_ready, t + 1)
                for i in range(2):
                    name = ("tokT", t, i)
                    free(name)
                    for k in range(4):
                        last = T_.transpose(bank(name)[:, P * k:P * k + P],
                                            tx_n[t % 2][:, P * (4 * i + k):P * (4 * i + k + 1)], ident)
                    last.then_inc(psum_filled, 1)

            def tok_product(t):
                name = ("tok", t)
                pe.wait_ge(tokx_ready, t + 1)
                if t == 0:
                    pe.wait_ge(tokw_ready, 3)
                free(name)
                o = bank(name)[:, 0:C]
                hi, lo = tx_hi[t % 2], tx_lo[t % 2]
                for k in range(7):
                    mm(o, hi[:, k], wt_hi[:, k], k == 0, False)
                    mm(o, lo[:, k], wt_hi[:, k], False, False)
                    mm(o, hi[:, k], wt_lo[:, k], False, False)
                mm(o, hi[:, 7], wt_hi[:, 7], False, False)
                mm(o, hi[0:64, 7], wt_lo[0:64, 7], False, True).then_inc(psum_filled, 1)

            for t in range(NT + 1):
                if t < NT:
                    tok_turn(t)
                if t:
                    tok_product(t - 1)

            xc = [0]
            xr = [0]

            def turn(phase):
                for pr in range(4):
                    name = ("x", phase, pr)
                    free(name)
                    for j in range(2):
                        xc[0] += 1
                        pe.wait_ge(xn_ready, xc[0])
                        t = 2 * pr + j
                        for k in range(2):
                            last = T_.transpose(bank(name)[:, 256 * j + P * k:256 * j + P * k + P],
                                                xn[:, t % 4, P * k:P * k + P], ident)
                    last.then_inc(psum_filled, 1)

            def by_rows(o, wa, wb, col0, m, hf, more=()):
                xa, xb = X_hi[:, 4 * hf:4 * hf + 4, 0], X_hi[:, 4 * hf:4 * hf + 4, 1]
                xl = X_lo[:, 4 * hf:4 * hf + 4]
                s = slice(col0, col0 + m)
                mm(o, wa[:, 0, s], xa, True, False)
                mm(o, wa[:, 0, s], xl, False, False)
                mm(o, wa[:, 1, s], xa, False, False)
                mm(o, wb[:, 0, s], xb, False, False)
                for w, x in more:
                    mm(o, w, x, False, False)
                return mm(o, wb[0:64, 1, s], xb[0:64], False, True)

            def by_tokens(o, ah, al, b, wa, wb, s, bias=None, start=True):
                mm(o, ah, wa[:, 0, s], start, False)
                mm(o, al, wa[:, 0, s], False, False)
                mm(o, ah, wa[:, 1, s], False, False)
                mm(o, b, wb[:, 0, s], False, False)
                if bias is not None:
                    mm(o, ones[:], rowh[:, bias:bias + (s.stop - s.start)], False, False)
                    mm(o, ones[:], rowl[:, bias:bias + (s.stop - s.start)], False, False)
                return mm(o, b[0:64], wb[0:64, 1, s], False, True)

            vw = [0, 0]

            def attention(a, hf):
                wa, wb = (early_a, early_b) if a == 0 else (late_a, late_b)
                c0 = 0 if a == 0 else LATE["qkv1"]
                n0 = 2 * a + hf
                for i, (s, o, m) in enumerate(SLOTS):
                    name = ("qkv", a, hf, s)
                    free(name)
                    more = ()
                    if a == 1:
                        sl = slice(HALF * hf, HALF * (hf + 1))
                        bh, bl = fullp[:, 0, FW + o:FW + o + m], fullp[:, 1, FW + o:FW + o + m]
                        bb = fullp[0:72, 0, FW + 576 + o:FW + 576 + o + m]
                        more = ((bh, hw_hi[:, sl]), (bh, hw_lo[:, sl]), (bl, hw_hi[:, sl]), (bb, cstack[0:72, sl]))
                    by_rows(bank(name)[0:m], wa, wb, c0 + o, m, hf, more).then_inc(psum_filled, 1)
                pe.wait_ge(bd_ready, 3 * n0 + 2)
                pe.wait_ge(qkv_ready, 5 * n0 + 5)
                qa, qb = pairs["QA"], pairs["QB"]
                for pr in range(2):
                    name = ("st", a, hf, pr)
                    free(name)
                    for s in range(16):
                        g = 16 * pr + s
                        o = bank(name)[:, 256 * (s // 8) + 16 * (s % 8):256 * (s // 8) + 16 * (s % 8) + 16]
                        q = slice(16 * g, 16 * g + 16)
                        mm(o, KAbd[:, 0, g], qa[:, 0, q], True, False)
                        mm(o, KAbd[:, 0, g], qa[:, 1, q], False, False)
                        mm(o, KAbd[:, 1, g], qa[:, 0, q], False, True)
                        o = bank(name)[0:CB, 256 * (s // 8) + P + 16 * (s % 8):256 * (s // 8) + P + 16 * (s % 8) + 16]
                        mm(o, KVBbd[0:CB, 0, g], qb[0:CB, 0, q], True, False)
                        mm(o, KVBbd[0:CB, 0, g], qb[0:CB, 1, q], False, False)
                        last = mm(o, KVBbd[0:CB, 1, g], qb[0:CB, 0, q], False, True)
                    last.then_inc(psum_filled, 1)
                pe.wait_ge(bd_ready, 3 * n0 + 3)
                for hl in range(2):
                    for g in range(4):
                        name = ("va", a, hf, hl, g)
                        free(name)
                        o = bank(name).bitcast(F16)
                        for s in range(8):
                            last = T_.transpose(o[:, P * s:P * s + P], VAbd[:, hl, 8 * g + s], id16[:])
                        last.then_inc(psum_filled, 1)
                    for g in range(2):
                        name = ("vb", a, hf, hl, g)
                        free(name)
                        o = bank(name)[0:CB].bitcast(F16)
                        for s in range(16):
                            last = T_.transpose(o[:, CB * s:CB * s + CB], KVBbd[64:P, hl, 16 * g + s], id16[64:P, 64:P])
                        last.then_inc(psum_filled, 1)
                    if hl == 0:
                        for pr in range(2):
                            name = ("s", a, hf, pr)
                            free(name)
                            pe.wait_ge(st_ready, 2 * n0 + pr + 1)
                            for j in range(2):
                                T_.transpose(bank(name)[:, C * j:C * j + P], ST[:, pr, j, 0], ident)
                                last = T_.transpose(bank(name)[:, C * j + P:C * j + C], ST[0:CB, pr, j, 1],
                                                    ident[0:CB, 0:CB])
                            last.then_inc(psum_filled, 1)
                for pr in range(2):
                    name = ("pt", a, hf, pr)
                    free(name)
                    pe.wait_ge(p_ready, 2 * n0 + pr + 1)
                    sm = SM[:, pr].rearrange("p h j -> p (h j)")
                    for j in range(2):
                        T_.transpose(bank(name)[:, 256 * j:256 * j + P], sm[:, C * j:C * j + P], ident)
                        last = T_.transpose(bank(name)[0:CB, 256 * j + P:256 * j + 2 * P], sm[:, C * j + P:C * j + C],
                                            ident)
                    last.then_inc(psum_filled, 1)
                vw[0] += 8
                vw[1] += 4
                pe.wait_ge(v_act_ready, vw[0])
                pe.wait_ge(v_dve_ready, vw[1])
                for pr in range(2):
                    name = ("ot", a, hf, pr)
                    free(name)
                    pe.wait_ge(pt_ready, 2 * n0 + pr + 1)
                    for s in range(16):
                        g = 16 * pr + s
                        t, q = 2 * pr + s // 8, slice(16 * (s % 8), 16 * (s % 8) + 16)
                        o = bank(name)[:, 256 * (s // 8) + 16 * (s % 8):256 * (s // 8) + 16 * (s % 8) + 16]
                        mm(o, VA[:, 0, g], PT[:, 0, t, 0, q], True, False)
                        mm(o, VA[:, 0, g], PT[:, 1, t, 0, q], False, False)
                        mm(o, VA[:, 1, g], PT[:, 0, t, 0, q], False, True)
                        o = bank(name)[0:CB, 256 * (s // 8) + P + 16 * (s % 8):256 * (s // 8) + P + 16 * (s % 8) + 16]
                        mm(o, VB[0:CB, 0, g], PT[0:CB, 0, t, 1, q], True, False)
                        mm(o, VB[0:CB, 0, g], PT[0:CB, 1, t, 1, q], False, False)
                        last = mm(o, VB[0:CB, 1, g], PT[0:CB, 0, t, 1, q], False, True)
                    last.then_inc(psum_filled, 1)
                c1 = EARLY["out0"] if a == 0 else LATE["proj"]
                for pr in range(2):
                    name = ("pj", a, hf, pr)
                    free(name)
                    pe.wait_ge(ot_ready, 2 * n0 + pr + 1)
                    for j in range(2):
                        t = 2 * pr + j
                        last = by_tokens(bank(name)[:, C * j:C * j + C], O_hi[:, t, 0], O_lo[:, t], O_hi[:, t, 1],
                                         wa, wb, slice(c1, c1 + C), R_OUT if a == 0 else R_PJ)
                    last.then_inc(psum_filled, 1)

            turn("attn0")
            pe.wait_ge(wearly, 4)
            pe.wait_ge(cols_ready, 10)
            for hf in range(2):
                pe.wait_ge(x_ready, 2 * hf + 2)
                attention(0, hf)
            turn("moe")
            pe.wait_ge(x_ready, 8)
            free("router0")
            for t in range(NT):
                last = by_tokens(bank("router0")[:, E * t:E * t + E], X_hi[:, t, 0], X_lo[:, t], X_hi[:, t, 1],
                                 early_a, early_b, slice(EARLY["router"], EARLY_N), R_RT)
            last.then_inc(psum_filled, 1)
            pe.wait_ge(wlo, NM)
            for u in range(UNITS + 1):
                if u < UNITS:
                    for n, c, _ in unit_chunks(u):
                        free(("h", n))
                        by_rows(bank(("h", n)), m1a, m1b, P * c, P, u // E).then_inc(psum_filled, 1)
                if u:
                    v = u - 1
                    q = v // 4
                    r = slice(32 * (v % 4), 32 * (v % 4) + 32)
                    terms = [(r, 4 + q % 2, 2 * E + q % 2)] + [(slice(0, P), s_, c) for n, c, s_ in unit_chunks(v)[-2:]]
                    pe.wait_ge(hp_ready, unit_chunks(v)[-1][0] + 1)
                    for pr in range(2):
                        free(("y", v, pr))
                        for j in range(2):
                            o = bank(("y", v, pr))[:, C * j:C * j + C]
                            x = slice(P * (2 * pr + j), P * (2 * pr + j) + P)
                            for i, (rows_, slot, c) in enumerate(terms):
                                w = slice(C * c, C * c + C)
                                mm(o, hgh[slot][rows_, x], m2[rows_, 0, w], i == 0, False)
                                mm(o, hgl[slot][rows_, x], m2[rows_, 0, w], False, False)
                                last = mm(o, hgh[slot][rows_, x], m2[rows_, 1, w], False, i == 2)
                        last.then_inc(psum_filled, 1)
            pe.wait_ge(gate_ready, 1)
            for hf in range(2):
                name = ("ct", hf)
                free(name)
                for i in range(4):
                    last = T_.transpose(bank(name)[0:E, P * i:P * i + P], gat[:, 4, 4 * hf + i], ident)
                last.then_inc(psum_filled, 1)
            pe.wait_ge(ct_ready, 2)
            for pr in range(4):
                name = ("b2", pr)
                free(name)
                for j in range(2):
                    t = 2 * pr + j
                    last = mm(bank(name)[:, C * j:C * j + C], ctT[:, P * t:P * t + P], b2s[:], True, True)
                last.then_inc(psum_filled, 1)
            turn("mix1")
            pe.wait_ge(x_ready, 12)
            pe.wait_ge(wlo, NM + NL + 1)
            for i in range(3):
                n = "kvr"[i]
                c0 = LATE["kvr"] + C * i
                for hf in range(2):
                    free((n, hf))
                    by_rows(bank((n, hf)), late_a, late_b, c0, P, hf).then_inc(psum_filled, 1)
                free((n, 2))
                for hf in range(2):
                    last = by_rows(bank((n, 2))[64 * hf:64 * hf + 64], late_a, late_b, c0 + P, CB, hf)
                last.then_inc(psum_filled, 1)
            pe.wait_ge(sy_ready, 3)
            c0 = slice(LATE["wo"], LATE["wo"] + C)
            for pr in range(4):
                name = ("wo", pr)
                free(name)
                for j in range(2):
                    t = 2 * pr + j
                    o = bank(name)[:, C * j:C * j + C]
                    x = slice(P * t, P * t + P)
                    y = slice(P * (t % 4), P * (t % 4) + P)
                    r = slice(64 * (t // 4), 64 * (t // 4) + 64)
                    mm(o, sy_ah[:, x], late_a[:, 0, c0], True, False)
                    mm(o, sy_al[:, x], late_a[:, 0, c0], False, False)
                    mm(o, sy_ah[:, x], late_a[:, 1, c0], False, False)
                    mm(o, sy_bh[r, y], late_b[r, 0, c0], False, False)
                    mm(o, sy_bl[r, y], late_b[r, 0, c0], False, False)
                    last = mm(o, sy_bh[r, y], late_b[r, 1, c0], False, True)
                last.then_inc(psum_filled, 1)
            turn("mix2")
            for hf in range(2):
                pe.wait_ge(x_ready, 12 + 2 * hf + 2)
                for m in range(6):
                    name = ("kf", hf, m)
                    free(name)
                    by_rows(bank(name), late_a, late_b, LATE["kf"] + P * m, P, hf).then_inc(psum_filled, 1)
                for pr in range(2):
                    name = ("r", hf, pr)
                    free(name)
                    for j in range(2):
                        t = 4 * hf + 2 * pr + j
                        last = by_tokens(bank(name)[:, C * j:C * j + C], X_hi[:, t, 0], X_lo[:, t], X_hi[:, t, 1],
                                         late_a, late_b, slice(LATE["wr"], LATE["wr"] + C))
                    last.then_inc(psum_filled, 1)
                    name = ("kv", hf, pr)
                    free(name)
                    for j in range(2):
                        o = bank(name)[:, C * j:C * j + C]
                        x = slice(P * (2 * pr + j), P * (2 * pr + j) + P)
                        for m in range(6):
                            if pr == 0 and j == 0:
                                pe.wait_ge(kf_ready, 6 * hf + m + 1)
                            w = slice(C * m, C * m + C)
                            mm(o, kfh[:, m, x], fullp[:, 0, w], m == 0, False)
                            mm(o, kfl[:, m, x], fullp[:, 0, w], False, False)
                            last = mm(o, kfh[:, m, x], fullp[:, 1, w], False, m == 5)
                    last.then_inc(psum_filled, 1)
            turn("attn1")
            pe.wait_ge(x_ready, 20)
            free("router1")
            for t in range(NT):
                last = by_tokens(bank("router1")[:, E * t:E * t + E], X_hi[:, t, 0], X_lo[:, t], X_hi[:, t, 1],
                                 late_a, late_b, slice(LATE["gate"], LATE["gate"] + E), R_GT)
            last.then_inc(psum_filled, 1)
            pe.wait_ge(gate_ready, 3)
            for hf in range(2):
                name = ("ce", hf)
                free(name)
                for i in range(4):
                    last = T_.transpose(bank(name)[:, P * i:P * i + P], crep1[:, 4 * hf + i], ident)
                last.then_inc(psum_filled, 1)
                name = ("la", hf)
                free(name)
                by_rows(bank(name), late_a, late_b, LATE["la"], P, hf).then_inc(psum_filled, 1)
                pe.wait_ge(hw_ready, 2 * hf + 2)
                attention(1, hf)


def _patch_order():
    inner, edge, corner, halo = [], [], [], []
    for i in range(-1, 17):
        for j in range(-1, 17):
            a, b = i in (-1, 16), j in (-1, 16)
            if a and b:
                continue
            where = halo if a or b else (corner, edge, inner)[2 - (i in (0, 15)) - (j in (0, 15))]
            where += [(i, j, c) for c in range(3)]
    return inner + edge + corner + halo


def _weight_rows(order):
    rows = np.full((FEAT, 5), PDIM)
    for n, (i, j, c) in enumerate(order):
        for s, (di, dj) in enumerate(((0, 0), (0, 1), (0, -1), (1, 0), (-1, 0))):
            p, q = i + di, j + dj
            if 0 <= p < 16 and 0 <= q < 16:
                rows[n, s] = (p * 16 + q) * 15 + 3 * s + c
    return rows


def _constants():
    k = np.zeros((P, K_N), np.float32)
    p = np.arange(P)
    k[:, K_ID:K_ID + P] = np.eye(P)
    k[:, K_HM:K_HM + HA] = p[:, None] // HD == np.arange(HA)
    k[:, K_HMB:K_HMB + HB] = p[:, None] % CB // HD == np.arange(HB)
    i, j = p[:, None] % SEQ, np.arange(SEQ)
    k[:, K_AM:K_AM + SEQ] = np.where(((j % 8 == 0) & (j <= i)) | (j == i) | (j == i - 1), 0.0, -1e30)
    k[:, K_BNW:K_BNW + 30] = [x for _, w in GROUPS for x in (w, 1, w) * 2]
    k[:, K_TRI:K_TRI + E * E] = (np.arange(E)[None, :] < np.arange(E)[:, None]).reshape(-1)
    return k


def kernel(**inputs):
    import concourse.bacc as bacc
    from concourse.bass_utils import run_bass_kernel_spmd

    g = {k: np.asarray(v) for k, v in inputs.items()}
    f32 = np.float32
    order = _patch_order()
    rows = _weight_rows(order)
    x = np.pad(g["x"], ((0, 0), (0, 0), (1, 1), (1, 1)))
    oi, oj, oc = (np.array(v) for v in zip(*order))
    tok = np.stack([x[:, oc, 16 * a + 1 + oi, 16 * b + 1 + oj] for a in range(4) for b in range(4)], axis=1)
    tok_x = tok.reshape(NT, P, FEAT)
    wz = np.concatenate([g["L0_tok_W"], np.zeros((1, C), f32)])
    tok_w = wz[rows[:PIX]].reshape(6, P, 5, C).transpose(1, 0, 2, 3)
    live = rows[PIX:].min(axis=1)
    live = np.concatenate([live, np.full(64, PDIM)])
    tok_wh = wz[live].reshape(2, P, C).transpose(1, 0, 2).copy()
    tok_wh[64:, 1] = tok_wh[:64, 1]

    def spread(v):
        z = np.concatenate([v, np.zeros(1, f32)])
        a = z[rows[:PIX]].reshape(6, P, 5).transpose(1, 0, 2).reshape(P, 30)
        b = z[live].reshape(2, P).T.copy()
        return a, b
    ga, gb = spread(g["L0_tok_gamma"])
    gb[64:, 1] = gb[:64, 1]
    ba, bb = spread(g["L0_tok_beta"])
    tok_g = np.concatenate([ga, gb], 1)
    tok_bt = np.concatenate([ba, bb], 1)

    def two(ws):
        w = np.concatenate(ws, 1)
        return np.stack([w[:P], np.concatenate([w[P:], w[P:]])], 1)

    def slots(w):
        q, k, v = w[..., :C], w[..., C:2 * C], w[..., 2 * C:]
        return np.concatenate([q[..., :P], k[..., :P], v[..., :P], k[..., P:], v[..., P:], q[..., P:]], -1)

    early = two([slots(g["L0_attn_qkv_w"].T), g["L0_attn_out_w"].T, g["L0_ffn_router_w"]])
    w1, w2, b1 = g["L0_ffn_w1"], g["L0_ffn_w2"], g["L0_ffn_b1"]
    w1c = np.concatenate([w1[:, :, :256].transpose(1, 0, 2).reshape(C, -1), w1[:, :, 256:].transpose(1, 0, 2).reshape(C, -1)], 1)
    moe1 = two([w1c]).reshape(P, -1)
    w2c = np.concatenate([w2[:, :256].reshape(-1, C), w2[:, 256:].reshape(-1, C)])
    moe2 = w2c.reshape(NCH, P, C).transpose(1, 0, 2).reshape(P, -1)
    b1c = np.concatenate([b1[:, :256].reshape(-1), b1[:, 256:].reshape(-1)]).reshape(NCH, P).T
    la = g["L1_ffn_A"].transpose(2, 1, 0).reshape(C, P)
    bm = slots(g["L1_ffn_Bm"].transpose(2, 0, 1).reshape(P, 3 * C))
    bbs = np.zeros((P, 3 * C), f32)
    for r in (0, 32, 64):
        bbs[r:r + E] = slots(g["L1_ffn_bb"])
    late = two([g["L1_attn_Wk_a"].T, g["L1_attn_Wv_a"].T, g["L1_attn_Wr_a"].T, g["L1_attn_Wo_a"].T, g["L1_attn_Wk_f"].T,
                g["L1_attn_Wr_f"].T, g["L1_ffn_Wg"].T, la, slots(g["L1_ffn_Wqkv"].T), g["L1_ffn_Wproj"].T])
    wv = g["L1_attn_Wv_f"].T.reshape(6, P, C).transpose(1, 0, 2).reshape(P, -1)
    full = np.concatenate([wv, bm, bbs], 1)

    def qcols(b):
        s = slots(b)
        return [s[:128], s[128:256], s[256:384], s[384:512], np.concatenate([s[512:], s[512:]])]

    def ab(v):
        return [v[:P], np.concatenate([v[P:], v[P:]])]
    cols = qcols(g["L0_attn_qkv_b"]) + list(b1c.T) + ab(g["L1_attn_ln1_w"]) + ab(g["L1_attn_ln1_b"]) \
        + ab(g["L1_attn_ln2_w"]) + ab(g["L1_attn_ln2_b"]) + ab(g["L1_attn_decay"]) + ab(g["L1_attn_first"]) \
        + [g["L1_ffn_ba"].T.reshape(P)] + qcols(g["L1_ffn_bqkv"])
    cols = np.stack(cols, 1)
    brow = np.concatenate([g["L0_attn_out_b"], g["L0_ffn_router_b"], g["L1_ffn_bproj"], g["L1_ffn_bg"]])[None]
    tok_b = np.broadcast_to(g["L0_tok_b"], (P, C))

    nc = bacc.Bacc("TRN2", target_bir_lowering=False, num_devices=1)
    arrays, args = {}, []
    for name, a in (("tok_x", tok_x), ("tok_w", tok_w), ("tok_wh", tok_wh), ("tok_g", tok_g), ("tok_bt", tok_bt),
                    ("tok_b", tok_b), ("early", early), ("moe1", moe1), ("moe2", moe2), ("moe_b2", g["L0_ffn_b2"]),
                    ("late", late.reshape(P, -1)), ("full", full), ("cols", cols), ("rows", brow),
                    ("consts", _constants())):
        a = np.ascontiguousarray(a)
        arrays[name] = a
        args.append(nc.dram_tensor(name, a.shape, F32, kind="ExternalInput").ap())
    args.append(nc.dram_tensor("out", (P, NT, C), F32, kind="ExternalOutput").ap())
    build(nc, *args)
    r = run_bass_kernel_spmd(nc, [arrays], core_ids=[0])
    return r.results[0]["out"].transpose(1, 0, 2).reshape(64, SEQ, C)
```

```python
from contextlib import ExitStack

import numpy as np

import concourse.bass as bass
from concourse import mybir

F32 = mybir.dt.float32
F16 = mybir.dt.float16
ALU = mybir.AluOpType
ACT = mybir.ActivationFunctionType
AX = mybir.AxisListType.X

P = 128
C = 192
CB = C - P
SEQ = 16
NT = 8
TOK = NT * P
HALF = TOK // 2
SH = HALF // SEQ
HD = 16
HA, HB = P // HD, CB // HD
NH = HA + HB
E = 8
HID = 288
NCH = E * HID // P
KF = 768
PIX = 768
FEAT = 960
NCHUNK = 8
PDIM = 3840
WS = 16.0
EPS = 1e-5
BIG = 1e38

GROUPS = ((294, 5), (294, 5), (168, 4), (12, 3), (192, 1))

K_ID = 0
K_HM = K_ID + P
K_HMB = K_HM + HA
K_AM = K_HMB + HB
K_BNW = K_AM + SEQ
K_TRI = K_BNW + 30
K_N = K_TRI + E * E

C_QB0, C_B1, C_LN1WA, C_LN1WB, C_LN1BA, C_LN1BB, C_LN2WA, C_LN2WB, C_LN2BA, C_LN2BB, C_DECA, C_DECB, \
    C_FIRA, C_FIRB, C_BA, C_QB1 = 0, 5, 23, 24, 25, 26, 27, 28, 29, 30, 31, 32, 33, 34, 35, 36
C_N = 41
R_OUT, R_RT, R_PJ, R_GT, R_N = 0, C, C + E, 2 * C + E, 2 * C + 2 * E

LATE = {}
_at = 0
for _name, _width in (("kvr", 3 * C), ("wo", C), ("kf", KF), ("wr", C), ("gate", E), ("la", P),
                      ("qkv1", 3 * C), ("proj", C)):
    LATE[_name] = _at
    _at += _width
LATE_N = _at
EARLY = {"qkv0": 0, "out0": 3 * C, "router": 4 * C}
EARLY_N = 4 * C + E
FULL_N = 6 * C + 3 * C + 3 * C
SLOTS = (("QA", 0, P), ("KA", P, P), ("VA", 2 * P, P), ("KVB", 3 * P, P), ("QB", 4 * P, CB))


UNITS = 2 * E


def unit_chunks(u):
    e = u % E
    n = 2 * u + u // 4
    chunks = []
    if e % 4 == 0:
        chunks.append((n, 2 * E + e // 4, 4 + u // 4 % 2))
        n += 1
    else:
        n += 1
    return chunks + [(n + i, 2 * e + i, (2 * u + i) % 4) for i in range(2)]


class Fills:

    def __init__(self):
        self.bank, self.before, self.done, self.release = {}, {}, {}, {}
        self.latest, self.count, self.total = {}, {}, 0

    def add(self, name, bank=None, by=None, at=None, counted=True):
        if bank is None:
            bank = self.total % 8
        self.bank[name] = bank
        self.before[name] = self.latest.get(bank)
        self.latest[bank] = name
        by = by or f"bank_free{bank}"
        self.count[by] = at or self.count.get(by, 0) + 1
        self.release[name] = (by, self.count[by])
        if counted:
            self.total += 1
            self.done[name] = self.total


def plan_fills():
    f = Fills()
    f.add("beta")
    for t in range(NT + 1):
        if t < NT:
            f.add(("tokT", t, 0))
            f.add(("tokT", t, 1), by="tokx_ready")
        if t:
            f.add(("tok", t - 1))

    def norm(phase, pairs=range(4)):
        for pr in pairs:
            if phase.startswith("mix"):
                f.add(("x", phase, pr), by="xf_ready")
            else:
                f.add(("x", phase, pr), by="x_ready", at=4 * PHASES.index(phase) + pr + 1)

    def attention(a):
        for step, hf in ATTENTION_ORDER:
            if step == "qkv":
                for s in SLOTS:
                    f.add(("qkv", a, hf, s[0]), by="qkv_ready")
            elif step in ("values0", "values1"):
                for g in range(4):
                    f.add(("va", a, hf, int(step[-1]), g), by="v_dve_ready" if g % 2 == 0 else "v_act_ready")
                for g in range(2):
                    f.add(("vb", a, hf, int(step[-1]), g), by="v_act_ready")
            else:
                for pr in range(2):
                    f.add((step, a, hf, pr), by={"st": "st_ready", "pt": "pt_ready", "ot": "ot_ready"}.get(step))

    norm("attn0")
    attention(0)
    norm("moe")
    f.add("router0")
    for u in range(UNITS + 1):
        if u < UNITS:
            for n, _, _ in unit_chunks(u):
                f.add(("h", n), bank=n % 4, by="gelu_ready")
        if u:
            for pr in range(2):
                f.add(("y", u - 1, pr), bank=4 + 2 * ((u - 1) % 2) + pr)
            if u == 1:
                for hf in range(2):
                    f.add(("ct", hf), bank=6 + hf, by="ct_ready")
            if u % E == 0:
                for pr in range(2):
                    f.add(("b2", 2 * (u // E - 1) + pr), bank=4 + 2 * (u % 2) + pr)
    norm("mix1", (0, 1))
    for n in "kvr":
        f.add((n, 0), by="kvr_ready")
    norm("mix1", (2, 3))
    for block in (1, 2):
        for n in "kvr":
            f.add((n, block), by="kvr_ready")
    for pr in range(4):
        f.add(("wo", pr))
    norm("mix2", (0, 1))
    for m in range(6):
        f.add(("kf", 0, m), by="relu_ready")
    norm("mix2", (2, 3))
    for pr in range(2):
        f.add(("r", 0, pr), by="tanh_ready")
    for m in range(6):
        f.add(("kf", 1, m), by="relu_ready")
    for pr in range(2):
        f.add(("kv", 0, pr))
    for pr in range(2):
        f.add(("r", 1, pr), by="tanh_ready")
    for pr in range(2):
        f.add(("kv", 1, pr))
    norm("attn1")
    f.add("router1")
    for hf in range(2):
        f.add(("ce", hf))
        f.add(("la", hf), by="hw_ready", at=2 * hf + 1)
    attention(1)
    return f


ATTENTION_ORDER = (("qkv", 0), ("st", 0), ("values0", 0), ("s", 0), ("values1", 0), ("qkv", 1), ("pt", 0), ("ot", 0),
                   ("st", 1), ("pj", 0), ("values0", 1), ("s", 1), ("values1", 1), ("pt", 1), ("ot", 1), ("pj", 1))
RECURRENCE_ORDER = (("maxima", 0), ("maxima", 1), ("states", 0), ("maxima", 2), ("states", 1), ("sums", 0),
                    ("states", 2), ("sums", 1), ("outputs", 0), ("sums", 2), ("outputs", 1), ("outputs", 2))
PHASES = ("attn0", "moe", "mix1", "mix2", "attn1")


def build(nc, tok_x, tok_w, tok_wh, tok_g, tok_bt, tok_b, early, moe1, moe2, moe_b2, late, full, cols, rows, consts,
          out):
    f = plan_fills()
    with ExitStack() as ctx:
        def sb(name, shape, dt=F32):
            return ctx.enter_context(nc.sbuf_tensor(name, shape, dt))

        def sem(name):
            return ctx.enter_context(nc.semaphore(name))

        H = sb("H", [P, NT, C])
        K = sb("K", [P, K_N])
        col = sb("col", [P, C_N])
        col16 = sb("col16", [P, C_N])
        rowr = sb("rowr", [1, R_N])
        rowh = sb("rowh", [1, R_N], F16)
        rowl = sb("rowl", [1, R_N], F16)
        ones = sb("ones", [1, P], F16)
        id16 = sb("id16", [P, P], F16)
        mhalf = sb("mhalf", [P, 1])
        tokb = sb("tokb", [P, C])
        stats = sb("stats", [P, 2, 30])
        wstats = sb("wstats", [P, 2, 30])
        mv = sb("mv", [P, NT, 2])
        ve = sb("ve", [P, NT])
        rstd = sb("rstd", [P, NT])
        xn = sb("xn", [P, NT // 2, 2 * P])
        X_hi = sb("X_hi", [P, NT, 2, P], F16)
        X_lo = sb("X_lo", [P, NT, P], F16)
        gat = sb("gat", [P, 6, NT, E])
        gsum = sb("gsum", [P, 4, NT])
        early_a = sb("early_a", [P, 2, EARLY_N], F16)
        early_b = sb("early_b", [P, 2, EARLY_N], F16)
        late_a = sb("late_a", [P, 2, LATE_N], F16)
        late_b = sb("late_b", [P, 2, LATE_N], F16)
        fullp = sb("fullp", [P, 2, FULL_N], F16)
        b2s = sb("b2s", [E, C])
        T_WORDS = 6144
        T = sb("T", [P, T_WORDS])
        BW = HALF + 1
        RW = 3 * BW
        R = sb("R", [P, 14 * RW])
        Q = sb("Q", [P, 6144])
        PS = ctx.enter_context(nc.psum_tensor("PS", [P, 8, 512], F32))

        def bank(name):
            return PS[:, f.bank[name], :]

        Z = T[:, 0:NT * C].rearrange("p (t n) -> p t n", t=NT)
        raw_w = T[:, 0:5760].rearrange("p (k s n) -> p k s n", k=6, s=5)
        raw_wh = T[:, 5760:6144].rearrange("p (k n) -> p k n", k=2)
        
        tok_in = [R[:, 8192 + 960 * i:8192 + 960 * (i + 1)] for i in range(3)]
        tx_n = [R[:, 1024 * i:1024 * i + 1024] for i in range(2)]
        tx_hi = [R[:, 2048 + 512 * i:2560 + 512 * i].bitcast(F16).rearrange("p (k n) -> p k n", k=8) for i in range(2)]
        tx_lo = [R[:, 3072 + 512 * i:3584 + 512 * i].bitcast(F16).rearrange("p (k n) -> p k n", k=8) for i in range(2)]
        wf = R[:, 4096:4096 + 1536].rearrange("p (k n) -> p k n", k=8)
        wt_hi = R[:, 5632:6400].bitcast(F16).rearrange("p (k n) -> p k n", k=8)
        wt_lo = R[:, 6400:7168].bitcast(F16).rearrange("p (k n) -> p k n", k=8)
        gbt = R[:, 7168:7168 + 64]
        raw_early = R[:, 12416:12416 + 2 * EARLY_N].rearrange("p (k n) -> p k n", k=2)
        KAbd = R[:, 0:4096].bitcast(F16).rearrange("p (l s n) -> p l s n", l=2, s=SH)
        KVBbd = R[:, 4096:6144].bitcast(F16).rearrange("p (l s n) -> p l s n", l=2, s=SH)
        VAbd = R[:, 6144:10240].bitcast(F16).rearrange("p (l s n) -> p l s n", l=2, s=SH)
        VA = R[:, 12288:16384].bitcast(F16).rearrange("p (l s n) -> p l s n", l=2, s=SH)
        VB = R[:, 10240:12288].bitcast(F16).rearrange("p (l s n) -> p l s n", l=2, s=SH)
        M1 = 2304
        raw_m1a = T[:, 0:M1]
        raw_m1b = T[:, M1:2 * M1]
        raw_m2 = T[:, 0:NCH * C]
        m1a = R[:, 16384:16384 + M1].bitcast(F16).rearrange("p (l n) -> p l n", l=2)
        m1b = R[:, 16384 + M1:16384 + 2 * M1].bitcast(F16).rearrange("p (l n) -> p l n", l=2)
        m2 = sb("m2", [P, 2, NCH * C], F16)

        def qv(at, n):
            return Q[:, at:at + n].bitcast(F16)
        pairs = {"QA": qv(0, 512), "KA": qv(512, 512), "VA": qv(1024, 512), "KVB": qv(1536, 512), "QB": qv(2048, 512)}
        pairs = {k: v.rearrange("p (l n) -> p l n", l=2) for k, v in pairs.items()}
        ST = Q[:, 2560:3584].rearrange("p (r t k n) -> p r t k n", r=2, t=2, k=2)
        SM = Q[:, 3584:4352].rearrange("p (r h j) -> p r h j", r=2, j=SEQ)
        PT = Q[:, 4352:5376].bitcast(F16).rearrange("p (l t k n) -> p l t k n", l=2, t=4, k=2)
        O_hi = Q[:, 5376:5888].bitcast(F16).rearrange("p (t k n) -> p t k n", t=4, k=2)
        O_lo = Q[:, 5888:6144].bitcast(F16).rearrange("p (t n) -> p t n", t=4)
        smx = sb("smx", [P, 2, 3, 2 * NH])
        rk = Q[:, 5120:5632].rearrange("p (t e f) -> p t e f", t=NT, e=E)
        rk2 = Q[:, 5632:6144].rearrange("p (t e f) -> p t e f", t=NT, e=E)
        ge = [Q[:, 512 * i:512 * i + 512] for i in range(3)]
        hgh = [Q[:, 1536 + 512 * i:1792 + 512 * i].bitcast(F16) for i in range(6)]
        hgl = [Q[:, 1792 + 512 * i:2048 + 512 * i].bitcast(F16) for i in range(6)]
        ctT = Q[0:E, 4608:5632]
        sy_ah = Q[:, 0:512].bitcast(F16)
        sy_al = Q[:, 512:1024].bitcast(F16)
        sy_bh = Q[:, 1024:1280].bitcast(F16)
        sy_bl = Q[:, 1280:1536].bitcast(F16)
        sy_hi = (sy_ah[:, 0:HALF], sy_bh, sy_ah[:, HALF:TOK])
        sy_lo = (sy_al[:, 0:HALF], sy_bl, sy_al[:, HALF:TOK])
        kfr = [Q[:, 1536 + 512 * i:2048 + 512 * i] for i in range(2)]
        kfs = [R[:, 512 * i:512 + 512 * i] for i in range(2)]
        kfh = Q[:, 3072:4608].bitcast(F16).rearrange("p (m n) -> p m n", m=6)
        kfl = Q[:, 4608:6144].bitcast(F16).rearrange("p (m n) -> p m n", m=6)
        tr_ = R[:, 2048:2048 + 4 * 2 * C].rearrange("p (r n) -> p r n", r=4)
        uu = R[:, 6144:6144 + 4 * C].rearrange("p (r n) -> p r n", r=2)
        xt_f = {n: v.rearrange("p (r t k n) -> p r t k n", r=4, t=2, k=2)
                for n, v in (("mix1", Q[:, 0:2048]), ("mix2", R[:, 4096:6144]))}
        EV = Q[:, 2048:2048 + 3 * HALF]
        crep1 = R[:, 19456:20480].rearrange("p (t n) -> p t n", t=NT)
        ceF = R[:, 16384:17408]
        hwF = R[:, 17408:17920]
        hw_hi = R[:, 17920:18432].bitcast(F16)
        hw_lo = R[:, 18432:18944].bitcast(F16)
        cstack = R[:, 18944:19456].bitcast(F16)
        r_ = [R[:, RW * i:RW * (i + 1)] for i in range(14)]
        rK, rV, rT, rW0, Mf, Mb, E1f, E2f, E1b, E2b, Af, Ab, Bf, Bb = r_

        def start(buf, b, shift=0):
            return buf[:, BW * b + shift:BW * b + shift + HALF]

        loaded = {n: sem("in_" + n) for n in ("consts", "cols", "tokw", "tokg", "early", "moe", "late", "full", "b2")}
        x_in = [sem(f"x_in{i}") for i in range(3)]
        out_done = sem("out_done")
        psum_filled = sem("psum_filled")
        bank_free = [sem(f"bank_free{i}") for i in range(8)]
        const_ready = sem("const_ready")
        cols_ready = sem("cols_ready")
        dve_step = sem("dve_step")
        act_step = sem("act_step")
        pool_step = sem("pool_step")
        var_ready = sem("var_ready")
        rstd_ready = sem("rstd_ready")
        xn_ready = sem("xn_ready")
        tokn_ready = sem("tokn_ready")
        hi_ready = sem("hi_ready")
        tokw_ready = sem("tokw_ready")
        tokx_ready = sem("tokx_ready")
        x_ready = sem("x_ready")
        wearly = sem("wearly")
        whi = sem("whi")
        wlo = sem("wlo")
        qkv_ready = sem("qkv_ready")
        bd_ready = sem("bd_ready")
        st_ready = sem("st_ready")
        v_act_ready = sem("v_act_ready")
        v_dve_ready = sem("v_dve_ready")
        smax_ready = sem("smax_ready")
        gmax_ready = sem("gmax_ready")
        exp_ready = sem("exp_ready")
        p_ready = sem("p_ready")
        pt_ready = sem("pt_ready")
        ot_ready = sem("ot_ready")
        gate_ready = sem("gate_ready")
        ct_ready = sem("ct_ready")
        gelu_ready = sem("gelu_ready")
        hp_ready = sem("hp_ready")
        kvr_ready = sem("kvr_ready")
        rd_ready = sem("rd_ready")
        re_ready = sem("re_ready")
        M_ready = sem("M_ready")
        mm_ready = sem("mm_ready")
        ev_ready = sem("ev_ready")
        ew_ready = sem("ew_ready")
        state_ready = sem("state_ready")
        num_ready = sem("num_ready")
        den_ready = sem("den_ready")
        sy_ready = sem("sy_ready")
        xf_ready = sem("xf_ready")
        relu_ready = sem("relu_ready")
        sq_ready = sem("sq_ready")
        kf_ready = sem("kf_ready")
        tanh_ready = sem("tanh_ready")
        ce_ready = sem("ce_ready")
        hw_ready = sem("hw_ready")
        h_ready = sem("h_ready")

        readers = {"tokx_ready": tokx_ready, "x_ready": x_ready, "xf_ready": xf_ready, "qkv_ready": qkv_ready,
                   "st_ready": st_ready, "v_dve_ready": v_dve_ready, "v_act_ready": v_act_ready, "pt_ready": pt_ready,
                   "ot_ready": ot_ready, "ct_ready": ct_ready, "gelu_ready": gelu_ready,
                   "kvr_ready": kvr_ready, "relu_ready": relu_ready, "tanh_ready": tanh_ready, "hw_ready": hw_ready}
        readers.update({f"bank_free{i}": bank_free[i] for i in range(8)})

        block = ctx.enter_context(nc.Block())

        moe_pieces = []
        for a in range(0, M1, 576):
            moe_pieces.append((raw_m1a[:, a:a + 576], m1a[:, 0, a:a + 576], m1a[:, 1, a:a + 576], WS))
        for a in range(0, M1, 576):
            moe_pieces.append((raw_m1b[:, a:a + 576], m1b[:, 0, a:a + 576], m1b[:, 1, a:a + 576], WS))
        for a in range(0, NCH * C, 576):
            moe_pieces.append((raw_m2[:, a:a + 576], m2[:, 0, a:a + 576], m2[:, 1, a:a + 576], WS))
        late_pieces = []
        raw_la = T[:, 0:LATE_N]
        raw_lb = T[:, LATE_N:2 * LATE_N]
        raw_f = T[:, 0:FULL_N]
        late_cuts = [(a, min(a + 576, LATE_N)) for a in range(0, LATE_N, 576)]
        for a, b in late_cuts:
            late_pieces.append((raw_la[:, a:b], late_a[:, 0, a:b], late_a[:, 1, a:b], WS))
            late_pieces.append((raw_lb[:, a:b], late_b[:, 0, a:b], late_b[:, 1, a:b], WS))
        FW = 6 * C
        for a, b, s in ((0, 576, WS), (576, FW, WS), (FW, FW + 576, 1.0), (FW + 576, FULL_N, WS)):
            late_pieces.append((raw_f[:, a:b], fullp[:, 0, a:b], fullp[:, 1, a:b], s))
        NM, NL, N1 = len(moe_pieces), len(late_pieces), 2 * M1 // 576

        @block.sync
        def _(sp):
            sp.dma_start(K[:], consts).then_inc(loaded["consts"], 16)
            sp.dma_start(gbt[:, 0:32], tok_g).then_inc(loaded["tokg"], 16)
            sp.dma_start(gbt[:, 32:64], tok_bt).then_inc(loaded["tokg"], 16)
            for t in range(2):
                sp.dma_start(tok_in[t], tok_x[t]).then_inc(x_in[t], 16)
            for k in range(6):
                sp.dma_start(raw_w[:, k], tok_w[:, k]).then_inc(loaded["tokw"], 16)
            sp.dma_start(raw_wh, tok_wh).then_inc(loaded["tokw"], 16)
            sp.dma_start(tokb[:], tok_b).then_inc(loaded["cols"], 16)
            sp.dma_start(col[:], cols).then_inc(loaded["cols"], 16)
            sp.dma_start(rowr[:], rows).then_inc(loaded["cols"], 16)
            sp.dma_start(tok_in[2], tok_x[2]).then_inc(x_in[2], 16)
            sp.dma_start(raw_early, early).then_inc(loaded["early"], 16)
            sp.dma_start(b2s[:], moe_b2).then_inc(loaded["b2"], 16)
            for t in range(3, NT):
                sp.wait_ge(tokn_ready, t - 2)
                sp.dma_start(tok_in[t % 3], tok_x[t]).then_inc(x_in[t % 3], 16)
            sp.wait_ge(tokw_ready, 1)
            sp.wait_ge(bank_free[f.bank["beta"]], 1)
            sp.dma_start(T[:, 0:2 * M1], moe1).then_inc(loaded["moe"], 16)
            sp.wait_ge(wlo, N1)
            sp.dma_start(raw_m2, moe2).then_inc(loaded["moe"], 16)
            sp.wait_ge(wlo, NM)
            sp.dma_start(T[:, 0:2 * LATE_N], late).then_inc(loaded["late"], 16)
            sp.wait_ge(wlo, NM + 2 * len(late_cuts))
            sp.dma_start(raw_f, full).then_inc(loaded["full"], 16)
            for pr in range(4):
                sp.wait_ge(h_ready, pr + 1)
                sp.dma_start(out[:, 2 * pr:2 * pr + 2, :], H[:, 2 * pr:2 * pr + 2, :]).then_inc(out_done, 16)
            sp.wait_ge(out_done, 4 * 16)

        @block.gpsimd
        def _(pool):
            nc.gpsimd.memset(mhalf[:], -0.5)
            nc.gpsimd.memset(ones[:], 1.0).then_inc(const_ready, 1)
            steps = [0]

            def one_over_std(n, t):
                pool.wait_ge(var_ready, n + 1)
                nc.gpsimd.tensor_scalar(ve[:, t:t + 1], mv[:, t, 1:2], EPS, None, ALU.add).then_inc(pool_step, 1)
                steps[0] += 1
                pool.wait_ge(pool_step, steps[0])
                nc.gpsimd.tensor_tensor(rstd[:, t:t + 1], ve[:, t:t + 1], mhalf[:], ALU.pow).then_inc(rstd_ready, 1)

            def low_part(n, raw, hi, lo):
                pool.wait_ge(whi, n + 1)
                nc.gpsimd.tensor_tensor(lo, raw, hi, ALU.subtract).then_inc(wlo, 1)

            pool.wait_ge(const_ready, 1)
            n = 0
            for t in range(NT):
                one_over_std(n, t)
                n += 1
            for t in range(NT):
                one_over_std(n, t)
                n += 1
            for i, (raw, hi, lo, _) in enumerate(moe_pieces):
                low_part(i, raw, hi, lo)
            for t in range(NT):
                one_over_std(n, t)
                n += 1
            for i, (raw, hi, lo, _) in enumerate(late_pieces):
                low_part(NM + i, raw, hi, lo)
            pool.wait_ge(wlo, NM + NL)
            nc.gpsimd.tensor_copy(fullp[64:64 + E, 0, FW + 576:FULL_N],
                                  fullp[64:64 + E, 1, FW + 576:FULL_N]).then_inc(wlo, 1)
            pool.wait_ge(wlo, NM + NL + 1)
            for hf in range(2):
                for k in range(5):
                    if k:
                        one_over_std(n, 4 * hf + k - 1)
                        n += 1
                    if k < 4:
                        one_over_std(n, 4 * hf + k)
                        n += 1

            def link(ins):
                ins.then_inc(pool_step, 1)
                steps[0] += 1
                pool.wait_ge(pool_step, steps[0])

            def exponents(b):
                pool.wait_ge(M_ready, b + 1)
                mf, mb, m = start(Mf, b), start(Mb, b, 1), start(rW0, b)
                nc.gpsimd.tensor_tensor(mf, mf, m, ALU.subtract).then_inc(pool_step, 1)
                nc.gpsimd.tensor_tensor(mb, mb, m, ALU.subtract).then_inc(mm_ready, 1)
                steps[0] += 1

            def weighted(b):
                pool.wait_ge(re_ready, 4 * b + 4)
                nc.gpsimd.tensor_tensor(EV[:, HALF * b:HALF * b + HALF], start(E2b, b), start(rV, b),
                                        ALU.mult).then_inc(ev_ready, 1)

            def denominator(b):
                pool.wait_ge(ew_ready, b + 1)
                pool.wait_ge(state_ready, b + 1)
                v, ec, ef, eb = start(rV, b), start(rK, b), start(Mf, b), start(Mb, b, 1)
                af, ab, bf, bb = start(Af, b), start(Ab, b, 1), start(Bf, b), start(Bb, b, 1)
                nc.gpsimd.tensor_tensor(v, v, ec, ALU.mult).then_inc(pool_step, 1)
                nc.gpsimd.tensor_tensor(ab, ab, eb, ALU.mult).then_inc(num_ready, 1)
                nc.gpsimd.tensor_tensor(bf, bf, ef, ALU.mult).then_inc(pool_step, 1)
                steps[0] += 2
                link(nc.gpsimd.tensor_tensor(bb, bb, eb, ALU.mult))
                link(nc.gpsimd.tensor_tensor(bf, bf, bb, ALU.add))
                nc.gpsimd.tensor_tensor(bf, bf, ec, ALU.add).then_inc(den_ready, 1)

            for step, b in RECURRENCE_ORDER:
                if step == "maxima":
                    exponents(b)
                elif step == "states":
                    weighted(b)
                elif step == "sums":
                    denominator(b)
            for phase in range(2):
                for t in range(NT):
                    one_over_std(n, t)
                    n += 1

        @block.scalar
        def _(act):
            hn = [0]

            def filled(name):
                act.wait_ge(psum_filled, f.done[name])

            act.wait_ge(loaded["cols"], 48)
            nc.scalar.activation(col16[:], col[:], ACT.Copy, scale=WS).then_inc(cols_ready, 1)
            act.wait_ge(loaded["consts"], 16)
            nc.scalar.activation(id16[:], K[:, K_ID:K_ID + P], ACT.Copy).then_inc(cols_ready, 1)
            for a, b, s in ((R_OUT, C, WS * WS), (R_RT, E, WS), (R_PJ, C, WS * WS), (R_GT, E, WS)):
                nc.scalar.activation(rowh[:, a:a + b], rowr[:, a:a + b], ACT.Copy, scale=s).then_inc(cols_ready, 1)
            act.wait_ge(tokw_ready, 1)
            nc.scalar.activation(wt_hi[:], wf[:], ACT.Copy, scale=WS).then_inc(tokw_ready, 1)
            for t in range(NT):
                for i in range(2):
                    name = ("tokT", t, i)
                    filled(name)
                    if i == 0 and t >= 2:
                        act.wait_ge(psum_filled, f.done[("tok", t - 2)])
                    nc.scalar.activation(tx_hi[t % 2][:, 4 * i:4 * i + 4, :], bank(name), ACT.Copy).then_inc(hi_ready, 1)
                    hn[0] += 1
                if t == 0:
                    act.wait_ge(loaded["early"], 16)
                    nc.scalar.activation(early_a[:, 0, :], raw_early[:, 0], ACT.Copy, scale=WS).then_inc(wearly, 1)
                    nc.scalar.activation(early_b[:, 0, :], raw_early[:, 1], ACT.Copy, scale=WS).then_inc(wearly, 1)

            def high_part(raw, hi, lo, scale):
                nc.scalar.activation(hi, raw, ACT.Copy, scale=scale).then_inc(act_step, 1)
                ast[0] += 1
                nc.scalar.activation(raw, raw, ACT.Copy, scale=scale).then_inc(whi, 1)
            ast = [0]

            def x_high(phase):
                for pr in range(4):
                    name = ("x", phase, pr)
                    filled(name)
                    nc.scalar.activation(X_hi[:, 2 * pr:2 * pr + 2],
                                         bank(name).rearrange("p (t k n) -> p t k n", t=2, k=2),
                                         ACT.Copy).then_inc(hi_ready, 1)
                    hn[0] += 1

            def x_high_affine(phase, pairs_):
                for pr in pairs_:
                    act.wait_ge(xf_ready, xf[0] + 1)
                    xf[0] += 1
                    nc.scalar.activation(X_hi[:, 2 * pr:2 * pr + 2], xt_f[phase][:, pr], ACT.Copy).then_inc(hi_ready, 1)
                    hn[0] += 1
            xf = [0]

            ev = [0]

            def attention(a, spare=lambda: None):
                cb = C_QB0 if a == 0 else C_QB1

                def values(hf, hl):
                    for g in (1, 3):
                        name = ("va", a, hf, hl, g)
                        filled(name)
                        nc.scalar.activation(VA[:, hl, 8 * g:8 * g + 8, :],
                                             bank(name).bitcast(F16).rearrange("p (s n) -> p s n", s=8),
                                             ACT.Copy).then_inc(v_act_ready, 1)
                    for g in range(2):
                        name = ("vb", a, hf, hl, g)
                        filled(name)
                        nc.scalar.activation(VB[0:CB, hl, 16 * g:16 * g + 16, :],
                                             bank(name)[0:CB].bitcast(F16).rearrange("p (s n) -> p s n", s=16),
                                             ACT.Copy).then_inc(v_act_ready, 1)

                for step, hf in ATTENTION_ORDER:
                    if step == "qkv":
                        n0 = 2 * a + hf
                        if n0:
                            act.wait_ge(bd_ready, 3 * n0)
                        for i, (s, o, m) in enumerate(SLOTS):
                            name = ("qkv", a, hf, s)
                            filled(name)
                            nc.scalar.activation(pairs[s][0:m, 0, :], bank(name)[0:m], ACT.Identity,
                                                 bias=col16[0:m, cb + i:cb + i + 1]).then_inc(hi_ready, 1)
                            hn[0] += 1
                    elif step == "st":
                        for pr in range(2):
                            name = ("st", a, hf, pr)
                            filled(name)
                            v = bank(name).rearrange("p (t k n) -> p t k n", t=2, k=2)
                            nc.scalar.activation(ST[:, pr, :, 0], v[:, :, 0], ACT.Copy).then_inc(act_step, 1)
                            nc.scalar.activation(ST[0:CB, pr, :, 1], v[0:CB, :, 1], ACT.Copy).then_inc(st_ready, 1)
                            ast[0] += 1
                    elif step in ("values0", "values1"):
                        values(hf, int(step[-1]))
                    elif step == "s":
                        for pr in range(2):
                            act.wait_ge(smax_ready, 2 * (2 * a + hf) + pr + 1)
                            nc.scalar.activation(SM[:, pr], SM[:, pr], ACT.Exp).then_inc(exp_ready, 1)
                    elif step in ("pt", "ot"):
                        for pr in range(2):
                            name = (step, a, hf, pr)
                            filled(name)
                            v = bank(name).rearrange("p (t k n) -> p t k n", t=2, k=2)
                            d = PT[:, 0] if step == "pt" else O_hi
                            nc.scalar.activation(d[:, 2 * pr:2 * pr + 2, 0], v[:, :, 0], ACT.Copy).then_inc(act_step, 1)
                            ast[0] += 1
                            nc.scalar.activation(d[0:CB, 2 * pr:2 * pr + 2, 1], v[0:CB, :, 1],
                                                 ACT.Copy).then_inc(hi_ready, 1)
                            hn[0] += 1
                    if step != "pj":
                        spare()
            x_high("attn0")
            mp = [0]

            def moe_high():
                for _ in range(2 if mp[0] < 2 * N1 // 4 else 1):
                    if mp[0] < NM:
                        if mp[0] in (0, N1):
                            act.wait_ge(loaded["moe"], 16 if mp[0] == 0 else 32)
                        high_part(*moe_pieces[mp[0]])
                        mp[0] += 1
            attention(0, moe_high)
            while mp[0] < NM:
                moe_high()
            x_high("moe")
            act.wait_ge(gmax_ready, 1)
            nc.scalar.activation(gat[:, 1], gat[:, 1], ACT.Exp).then_inc(exp_ready, 1)
            lp = [0]

            def late_high():
                if lp[0] < NL:
                    if lp[0] == 0:
                        act.wait_ge(loaded["late"], 16)
                    if lp[0] == 2 * len(late_cuts):
                        act.wait_ge(loaded["full"], 16)
                    high_part(*late_pieces[lp[0]])
                    lp[0] += 1
            for u in range(UNITS):
                for n, c, slot in unit_chunks(u):
                    filled(("h", n))
                    if n >= 3:
                        act.wait_ge(hp_ready, n - 2)
                    b = col[:, C_B1 + c:C_B1 + c + 1]
                    nc.scalar.activation(ge[n % 3], bank(("h", n)), ACT.Gelu, bias=b,
                                         scale=1.0 / WS).then_inc(act_step, 1)
                    ast[0] += 1
                    if u >= 2:
                        filled(("y", u - 2, 1))
                    nc.scalar.activation(hgh[slot], bank(("h", n)), ACT.Gelu, bias=b,
                                         scale=1.0 / WS).then_inc(gelu_ready, 1)
                if u == 2:
                    for hf in range(2):
                        name = ("ct", hf)
                        filled(name)
                        nc.scalar.activation(ctT[:, HALF * hf:HALF * (hf + 1)], bank(name)[0:E],
                                             ACT.Copy).then_inc(ct_ready, 1)
                if u > 1:
                    late_high()
                    late_high()
            while lp[0] < NL:
                late_high()
            x_high_affine("mix1", (0, 1))
            for block in range(3):
                if block == 1:
                    x_high_affine("mix1", (2, 3))
                for i, n in enumerate("kvr"):
                    dst, fn, sc = ((rK, ACT.Copy, 1 / WS), (rV, ACT.Copy, 1 / WS), (rT, ACT.Tanh, 0.5 / WS))[i]
                    name = (n, block)
                    filled(name)
                    nc.scalar.activation(start(dst, block), bank(name), fn, scale=sc).then_inc(kvr_ready, 1)

            def decays(b):
                for i, (e1, e2) in enumerate(((start(E1f, b), start(E2f, b)), (start(E1b, b), start(E2b, b)))):
                    act.wait_ge(rd_ready, 2 * b + i + 1)
                    nc.scalar.activation(e2, e1, ACT.Relu).then_inc(act_step, 1)
                    ast[0] += 1
                    act.wait_ge(act_step, ast[0])
                    nc.scalar.activation(e1, e1, ACT.Relu, scale=-1.0).then_inc(act_step, 1)
                    nc.scalar.activation(e2, e2, ACT.Exp, scale=-1.0).then_inc(re_ready, 1)
                    ast[0] += 1
                    act.wait_ge(act_step, ast[0])
                    nc.scalar.activation(e1, e1, ACT.Exp, scale=-1.0).then_inc(re_ready, 1)

            def weights(b):
                act.wait_ge(mm_ready, b + 1)
                for e in (start(Mf, b), start(Mb, b, 1)):
                    nc.scalar.activation(e, e, ACT.Exp).then_inc(act_step, 1)
                    ast[0] += 1
                e = start(rK, b)
                nc.scalar.activation(e, e, ACT.Exp).then_inc(ew_ready, 1)

            def sy_high(b):
                act.wait_ge(sy_ready, 2 * b + 1)
                nc.scalar.activation(sy_hi[b], start(E1b, b), ACT.Copy).then_inc(hi_ready, 1)
                hn[0] += 1

            for step, b in RECURRENCE_ORDER:
                if step == "maxima":
                    decays(b)
                elif step == "states":
                    weights(b)
                elif step == "outputs":
                    sy_high(b)
            x_high_affine("mix2", range(4))

            def ffn_high(hf):
                for m in range(6):
                    n = 6 * hf + m
                    filled(("kf", hf, m))
                    if n >= 2:
                        act.wait_ge(sq_ready, n - 1)
                    nc.scalar.activation(kfr[m % 2], bank(("kf", hf, m)), ACT.Relu, scale=1 / WS).then_inc(relu_ready, 1)
                    act.wait_ge(relu_ready, n + 1)
                    if hf and m == 0:
                        filled(("kv", 0, 1))
                    nc.scalar.activation(kfh[:, m], kfr[m % 2], ACT.Square).then_inc(hi_ready, 1)
                    hn[0] += 1

            def receptance(hf):
                for pr in range(2):
                    name = ("r", hf, pr)
                    filled(name)
                    nc.scalar.activation(tr_[:, 2 * hf + pr], bank(name)[:, 0:2 * C], ACT.Tanh,
                                         scale=0.5 / WS).then_inc(tanh_ready, 1)
            ffn_high(0)
            receptance(0)
            ffn_high(1)
            receptance(1)
            x_high("attn1")
            act.wait_ge(gmax_ready, 2)
            nc.scalar.activation(gat[:, 1], gat[:, 1], ACT.Exp).then_inc(exp_ready, 1)
            for hf in range(2):
                sl = slice(HALF * hf, HALF * (hf + 1))
                name = ("ce", hf)
                filled(name)
                nc.scalar.activation(ceF[:, sl], bank(name), ACT.Copy).then_inc(ce_ready, 1)
                nc.scalar.activation(cstack[0:E, sl], bank(name)[0:E], ACT.Copy).then_inc(act_step, 1)
                nc.scalar.activation(cstack[64:64 + E, sl], bank(name)[0:E], ACT.Copy).then_inc(hi_ready, 1)
                ast[0] += 1
                hn[0] += 1
                act.wait_ge(hw_ready, 2 * hf + 1)
                nc.scalar.activation(hw_hi[:, sl], hwF, ACT.Copy).then_inc(hi_ready, 1)
                hn[0] += 1
            attention(1)

        @block.vector
        def _(dve):
            V = nc.vector
            chain = [0]
            hn = [0]
            nn = [0]
            ev = [0]

            def link(ins):
                ins.then_inc(dve_step, 1)
                chain[0] += 1
                dve.wait_ge(dve_step, chain[0])

            def filled(name):
                dve.wait_ge(psum_filled, f.done[name])

            def released(name):
                dve.wait_ge(bank_free[f.bank[name]], f.release[name][1])

            deca = [col[:, c:c + 1] for c in (C_DECA, C_DECB, C_DECA)]
            fira = [col[:, c:c + 1] for c in (C_FIRA, C_FIRB, C_FIRA)]

            def next_high():
                hn[0] += 1
                dve.wait_ge(hi_ready, hn[0])

            dve.wait_ge(loaded["consts"], 16)
            wgt = K[:, K_BNW:K_BNW + 30]

            def tok_stats(t):
                dve.wait_ge(x_in[t % 3], 16 * (t // 3 + 1))
                a = 0
                for i, (n, _) in enumerate(GROUPS):
                    ins = V.bn_stats(stats[:, t % 2, 6 * i:6 * i + 6], tok_in[t % 3][:, a:a + n])
                    a += n
                link(ins)
                link(V.tensor_tensor(wstats[:, t % 2], stats[:, t % 2], wgt, ALU.mult))
                V.bn_aggr(mv[:, t], wstats[:, t % 2]).then_inc(var_ready, 1)

            def tok_norm(t):
                dve.wait_ge(rstd_ready, t + 1)
                if t >= 2:
                    dve.wait_ge(psum_filled, f.done[("tokT", t - 2, 1)])
                dst = tx_n[t % 2]
                V.tensor_scalar(dst[:, 0:FEAT], tok_in[t % 3], mv[:, t, 0:1], rstd[:, t:t + 1],
                                ALU.subtract, ALU.mult).then_inc(dve_step, 1)
                chain[0] += 1
                V.tensor_scalar(dst[:, FEAT:1024], tok_in[t % 3][:, FEAT - 64:FEAT], mv[:, t, 0:1], rstd[:, t:t + 1],
                                ALU.subtract, ALU.mult).then_inc(tokn_ready, 1)

            def tok_low(t):
                for i in range(2):
                    name = ("tokT", t, i)
                    next_high()
                    b = bank(name).rearrange("p (k n) -> p k n", k=4)
                    if i == 0:
                        V.tensor_tensor(tx_lo[t % 2][:, 0:4, :], b, tx_hi[t % 2][:, 0:4, :],
                                        ALU.subtract).then_inc(bank_free[f.bank[name]], 1)
                    else:
                        V.tensor_tensor(tx_lo[t % 2][:, 4:7, :], b[:, 0:3], tx_hi[t % 2][:, 4:7, :], ALU.subtract)
                        V.tensor_tensor(tx_hi[t % 2][64:P, 7, :], b[64:P, 3], tx_hi[t % 2][64:P, 7, :],
                                        ALU.subtract).then_inc(tokx_ready, 1)

            def tok_out(t):
                name = ("tok", t)
                filled(name)
                V.scalar_tensor_tensor(H[:, t], bank(name)[:, 0:C], 1.0 / WS, tokb[:], ALU.mult,
                                       ALU.add).then_inc(bank_free[f.bank[name]], 1)
                dve.wait_ge(bank_free[f.bank[name]], f.release[name][1])

            tok_stats(0)
            dve.wait_ge(loaded["tokg"], 32)
            dve.wait_ge(const_ready, 1)
            for k in range(6):
                dve.wait_ge(loaded["tokw"], 16 * 7)
                for s in range(5):
                    g = gbt[:, 5 * k + s:5 * k + s + 1]
                    if s == 0:
                        link(V.tensor_scalar(wf[:, k], raw_w[:, k, 0], g, None, ALU.mult))
                    elif s < 4 or k < 5:
                        link(V.scalar_tensor_tensor(wf[:, k], raw_w[:, k, s], g, wf[:, k], ALU.mult, ALU.add))
                    else:
                        link(V.scalar_tensor_tensor(wf[:, k], raw_w[:, k, s], g, wf[:, k], ALU.mult, ALU.add))
                if k == 0:
                    tok_norm(0)
                if k == 2:
                    tok_stats(1)
            link(V.tensor_scalar(wf[:, 6], raw_wh[:, 0], gbt[:, 30:31], None, ALU.mult))
            V.tensor_scalar(wf[:, 7], raw_wh[:, 1], gbt[:, 31:32], None, ALU.mult).then_inc(tokw_ready, 1)
            tok_norm(1)
            tok_low(0)
            dve.wait_ge(tokw_ready, 2)
            V.scalar_tensor_tensor(wt_lo[:], wf[:], WS, wt_hi[:], ALU.mult, ALU.subtract).then_inc(tokw_ready, 1)
            dve.wait_ge(cols_ready, 6)
            for a, b, s in ((R_OUT, C, WS * WS), (R_RT, E, WS), (R_PJ, C, WS * WS), (R_GT, E, WS)):
                V.scalar_tensor_tensor(rowl[:, a:a + b], rowr[:, a:a + b], s, rowh[:, a:a + b], ALU.mult,
                                       ALU.subtract).then_inc(cols_ready, 1)
            filled("beta")
            V.tensor_tensor(tokb[:], tokb[:], bank("beta")[:, 0:C], ALU.add).then_inc(bank_free[f.bank["beta"]], 1)
            dve.wait_ge(bank_free[f.bank["beta"]], 1)
            dve.wait_ge(wearly, 2)
            V.scalar_tensor_tensor(early_a[:, 1], raw_early[:, 0], WS, early_a[:, 0], ALU.mult,
                                   ALU.subtract).then_inc(wearly, 1)
            V.scalar_tensor_tensor(early_b[0:CB, 1], raw_early[0:CB, 1], WS, early_b[0:CB, 0], ALU.mult,
                                   ALU.subtract).then_inc(wearly, 1)
            nn[0] = NT

            def ln_stats(t, src):
                link(V.bn_stats(stats[:, t % 2, 0:6], src[:, t]))
                V.bn_aggr(mv[:, t], stats[:, t % 2, 0:6]).then_inc(var_ready, 1)
                nn[0] += 1
                return nn[0]

            def ln_norm(t, src, n, k):
                dve.wait_ge(rstd_ready, n)
                if k >= 4:
                    dve.wait_ge(psum_filled, x_fill(k - 4))
                V.tensor_scalar(xn[:, t % 4, 0:C], src[:, t], mv[:, t, 0:1], rstd[:, t:t + 1], ALU.subtract,
                                ALU.mult).then_inc(dve_step, 1)
                chain[0] += 1
                V.tensor_scalar(xn[:, t % 4, C:2 * P], src[:, t, P:C], mv[:, t, 0:1], rstd[:, t:t + 1], ALU.subtract,
                                ALU.mult).then_inc(xn_ready, 1)

            def x_fill(k):
                return f.done[("x", PHASES[k // NT], k % NT // 2)]

            xc = [0]

            def norm_tiles(src, ready=None, tiles=range(NT)):
                last = None
                for t in range(tiles[0], tiles[-1] + 2):
                    if t in tiles:
                        if ready:
                            ready(t)
                        now = ln_stats(t, src)
                    if last:
                        ln_norm(t - 1, src, last, xc[0])
                        xc[0] += 1
                    last = now

            def norm_twice(hf, k):
                if k >= 2:
                    ln_norm(4 * hf + k - 2, Z, second[k - 2], xc[0])
                    xc[0] += 1
                if 1 <= k < 5:
                    t = 4 * hf + k - 1
                    dve.wait_ge(rstd_ready, first[k - 1])
                    link(V.tensor_scalar(Z[:, t], H[:, t], mv[:, t, 0:1], rstd[:, t:t + 1], ALU.subtract, ALU.mult))
                    second[k - 1] = ln_stats(t, Z)
                if k < 4:
                    first[k] = ln_stats(4 * hf + k, H)
            first, second = {}, {}

            def x_low(phase):
                for pr in range(4):
                    name = ("x", phase, pr)
                    next_high()
                    b = bank(name).rearrange("p (t k n) -> p t k n", t=2, k=2)
                    V.tensor_tensor(X_lo[:, 2 * pr:2 * pr + 2], b[:, :, 0], X_hi[:, 2 * pr:2 * pr + 2, 0], ALU.subtract)
                    V.tensor_tensor(X_hi[64:P, 2 * pr:2 * pr + 2, 1], b[64:P, :, 1], X_hi[64:P, 2 * pr:2 * pr + 2, 1],
                                    ALU.subtract).then_inc(x_ready, 1)

            def x_affine(phase, pairs_):
                wa, wb, ba, bb = {"mix1": (C_LN1WA, C_LN1WB, C_LN1BA, C_LN1BB),
                                  "mix2": (C_LN2WA, C_LN2WB, C_LN2BA, C_LN2BB)}[phase]
                for pr in pairs_:
                    name = ("x", phase, pr)
                    filled(name)
                    b = bank(name).rearrange("p (t k n) -> p t k n", t=2, k=2)
                    V.tensor_scalar(xt_f[phase][:, pr, :, 0], b[:, :, 0], col[:, wa:wa + 1], col[:, ba:ba + 1],
                                    ALU.mult, ALU.add).then_inc(dve_step, 1)
                    chain[0] += 1
                    V.tensor_scalar(xt_f[phase][:, pr, :, 1], b[:, :, 1], col[:, wb:wb + 1], col[:, bb:bb + 1],
                                    ALU.mult, ALU.add).then_inc(xf_ready, 1)

            def x_affine_low(phase, pairs_):
                for pr in pairs_:
                    next_high()
                    x = xt_f[phase]
                    V.tensor_tensor(X_lo[:, 2 * pr:2 * pr + 2], x[:, pr, :, 0], X_hi[:, 2 * pr:2 * pr + 2, 0],
                                    ALU.subtract)
                    V.tensor_tensor(X_hi[64:P, 2 * pr:2 * pr + 2, 1], x[64:P, pr, :, 1],
                                    X_hi[64:P, 2 * pr:2 * pr + 2, 1], ALU.subtract).then_inc(x_ready, 1)

            def attention(a, after_pair):
                cb = C_QB0 if a == 0 else C_QB1

                def low(hf, i):
                    s, o, m = SLOTS[i]
                    name = ("qkv", a, hf, s)
                    next_high()
                    V.scalar_tensor_tensor(pairs[s][0:m, 1, :], bank(name)[0:m], col16[0:m, cb + i:cb + i + 1],
                                           pairs[s][0:m, 0, :], ALU.add, ALU.subtract).then_inc(qkv_ready, 1)

                def spread(hf, i):
                    dst, src, nh, mask = ((KAbd, "KA", HA, K_HM), (VAbd, "VA", HA, K_HM), (KVBbd, "KVB", HB, K_HMB))[i - 1]
                    dve.wait_ge(qkv_ready, 5 * (2 * a + hf) + i + 1)
                    for l in range(2):
                        v = dst[:, l].rearrange("p s (h j) -> p s h j", h=nh)
                        w = pairs[src][:, l].rearrange("p (s j) -> p s j", j=SEQ)
                        for h in range(nh):
                            ins = V.tensor_scalar(v[:, :, h], w, K[:, mask + h:mask + h + 1], None, ALU.mult)
                    ins.then_inc(bd_ready, 1)

                def softmax_in(hf, pr):
                    name = ("s", a, hf, pr)
                    filled(name)
                    s = bank(name)[:, 0:2 * C].rearrange("p (h j) -> p h j", j=SEQ)
                    sc = HD ** -0.5 / (WS * WS)
                    if a == 0:
                        am = K[:, K_AM:K_AM + SEQ][:, None, :].broadcast_to([P, 2 * NH, SEQ])
                        V.scalar_tensor_tensor(SM[:, pr], s, sc, am, ALU.mult, ALU.add).then_inc(
                            bank_free[f.bank[name]], 1)
                    else:
                        V.tensor_scalar(SM[:, pr], s, sc, None, ALU.mult).then_inc(bank_free[f.bank[name]], 1)
                    released(name)
                    link(V.tensor_reduce(smx[:, pr, 0], SM[:, pr], AX, ALU.max))
                    V.tensor_tensor(SM[:, pr], SM[:, pr], smx[:, pr, 0][:, :, None].broadcast_to([P, 2 * NH, SEQ]),
                                    ALU.subtract).then_inc(smax_ready, 1)

                def softmax_out(pr):
                    dve.wait_ge(exp_ready, en[0] + 1)
                    en[0] += 1
                    link(V.tensor_reduce(smx[:, pr, 1], SM[:, pr], AX, ALU.add))
                    link(V.reciprocal(smx[:, pr, 2], smx[:, pr, 1]))
                    V.tensor_tensor(SM[:, pr], SM[:, pr], smx[:, pr, 2][:, :, None].broadcast_to([P, 2 * NH, SEQ]),
                                    ALU.mult).then_inc(p_ready, 1)

                def values(hf, hl):
                    for g in (0, 2):
                        name = ("va", a, hf, hl, g)
                        filled(name)
                        V.tensor_copy(VA[:, hl, 8 * g:8 * g + 8, :],
                                      bank(name).bitcast(F16).rearrange("p (s n) -> p s n", s=8)).then_inc(v_dve_ready, 1)

                def low_rows(hf, step):
                    for pr in range(2):
                        name = (step, a, hf, pr)
                        next_high()
                        v = bank(name).rearrange("p (t k n) -> p t k n", t=2, k=2)
                        sl = slice(2 * pr, 2 * pr + 2)
                        if step == "pt":
                            V.tensor_tensor(PT[:, 1, sl, 0], v[:, :, 0], PT[:, 0, sl, 0], ALU.subtract)
                            V.tensor_tensor(PT[0:CB, 1, sl, 1], v[0:CB, :, 1], PT[0:CB, 0, sl, 1],
                                            ALU.subtract).then_inc(pt_ready, 1)
                        else:
                            V.tensor_tensor(O_lo[:, sl], v[:, :, 0], O_hi[:, sl, 0], ALU.subtract)
                            V.tensor_tensor(O_hi[64:P, sl, 1], v[0:CB, :, 1], O_hi[0:CB, sl, 1],
                                            ALU.subtract).then_inc(ot_ready, 1)

                def project(hf):
                    for pr in range(2):
                        name = ("pj", a, hf, pr)
                        filled(name)
                        t = 4 * hf + 2 * pr
                        V.scalar_tensor_tensor(H[:, t:t + 2],
                                               bank(name)[:, 0:2 * C].rearrange("p (t n) -> p t n", t=2),
                                               1.0 / (WS * WS), H[:, t:t + 2], ALU.mult,
                                               ALU.add).then_inc(bank_free[f.bank[name]], 1)
                        released(name)
                        after_pair(2 * hf + pr)

                def probabilities(hf):
                    values(hf, 0)
                    softmax_in(hf, 0)
                    softmax_in(hf, 1)
                    values(hf, 1)
                    softmax_out(0)
                    softmax_out(1)

                low(0, 0)
                low(0, 1)
                spread(0, 1)
                low(0, 2)
                low(0, 3)
                spread(0, 3)
                low(0, 4)
                spread(0, 2)
                probabilities(0)
                for i in range(5):
                    low(1, i)
                low_rows(0, "pt")
                spread(1, 1)
                spread(1, 3)
                low_rows(0, "ot")
                spread(1, 2)
                project(0)
                probabilities(1)
                low_rows(1, "pt")
                low_rows(1, "ot")
                project(1)
            en = [0]

            def gates(which, twice):
                name = f"router{which}"
                filled(name)
                lg = bank(name)[:, 0:NT * E].rearrange("p (t e) -> p t e", t=NT)
                V.tensor_scalar(gat[:, 0], lg, 1.0 / WS, None, ALU.mult).then_inc(bank_free[f.bank[name]], 1)
                dve.wait_ge(bank_free[f.bank[name]], f.release[name][1])
                link(V.tensor_reduce(gsum[:, 0], gat[:, 0], AX, ALU.max))
                V.tensor_tensor(gat[:, 1], gat[:, 0], gsum[:, 0][:, :, None].broadcast_to([P, NT, E]),
                                ALU.subtract).then_inc(gmax_ready, 1)
                dve.wait_ge(exp_ready, en[0] + 1)
                en[0] += 1
                link(V.tensor_reduce(gsum[:, 1], gat[:, 1], AX, ALU.add))
                link(V.reciprocal(gsum[:, 2], gsum[:, 1]))
                link(V.tensor_tensor(gat[:, 2], gat[:, 1], gsum[:, 2][:, :, None].broadcast_to([P, NT, E]), ALU.mult))
                full4 = [P, NT, E, E]
                of = gat[:, 2][:, :, None, :].broadcast_to(full4)
                oe = gat[:, 2][:, :, :, None].broadcast_to(full4)
                tri = K[:, K_TRI:K_TRI + E * E].rearrange("p (e f) -> p e f", e=E)[:, None].broadcast_to(full4)
                link(V.tensor_tensor(rk[:], of, oe, ALU.is_equal))
                link(V.tensor_tensor(rk[:], rk[:], tri, ALU.mult))
                link(V.tensor_tensor(rk2[:], of, oe, ALU.is_gt))
                link(V.tensor_tensor(rk[:], rk[:], rk2[:], ALU.add))
                link(V.tensor_reduce(gat[:, 3], rk[:], AX, ALU.add))
                link(V.scalar_tensor_tensor(gat[:, 4], gat[:, 3], 1.5, gat[:, 2], ALU.is_lt, ALU.mult))
                if twice:
                    link(V.tensor_scalar(gat[:, 5], gat[:, 4], 2.0, None, ALU.mult))

            norm_now = []
            tok_stats(2)
            for t in range(NT):
                if t + 2 < NT:
                    tok_norm(t + 2)
                if t + 3 < NT:
                    tok_stats(t + 3)
                if t + 1 < NT:
                    tok_low(t + 1)
                tok_out(t)
            norm_tiles(H)
            x_low("attn0")
            attention(0, lambda pr: None)
            norm_tiles(H)
            x_low("moe")
            dve.wait_ge(loaded["b2"], 16)
            link(V.tensor_scalar(b2s[:], b2s[:], WS, None, ALU.mult))
            gates(0, False)
            V.tensor_scalar(gat[:, 5], gat[:, 4], 1.0 / WS, None, ALU.mult).then_inc(gate_ready, 1)
            dve.wait_ge(gate_ready, 1)
            for u in range(UNITS + 1):
                if u < UNITS:
                    for n, _, slot in unit_chunks(u):
                        dve.wait_ge(gelu_ready, n + 1)
                        V.tensor_tensor(hgl[slot], ge[n % 3], hgh[slot], ALU.subtract).then_inc(hp_ready, 1)
                if u:
                    hf, e = divmod(u - 1, E)
                    for pr in range(2):
                        name = ("y", u - 1, pr)
                        filled(name)
                        if e:
                            released(("y", u - 2, pr))
                        for j in range(2):
                            t = 4 * hf + 2 * pr + j
                            ins = V.scalar_tensor_tensor(H[:, t], bank(name)[:, C * j:C * j + C], gat[:, 5, t, e:e + 1],
                                                         H[:, t], ALU.mult, ALU.add)
                        ins.then_inc(bank_free[f.bank[name]], 1)
                    if e == E - 1:
                        for pr in range(2):
                            name = ("b2", 2 * hf + pr)
                            filled(name)
                            released(("y", u - 1, pr))
                            t = 4 * hf + 2 * pr
                            V.scalar_tensor_tensor(H[:, t:t + 2],
                                                   bank(name)[:, 0:2 * C].rearrange("p (t n) -> p t n", t=2), 1.0 / WS,
                                                   H[:, t:t + 2], ALU.mult, ALU.add).then_inc(bank_free[f.bank[name]], 1)
                            released(name)
                if u == E:
                    link(V.tensor_scalar(col[:, C_DECA:C_FIRB + 1], col[:, C_DECA:C_FIRB + 1], 1.0 / SEQ, None, ALU.mult))
                    link(V.memset(rW0[:], 0.0))
                    for b in range(3):
                        w = start(rW0, b)
                        link(V.tensor_scalar(w, w, deca[b], None, ALU.add))
                        link(V.memset(w[:, ::SEQ], -BIG))
                if E < u < E + 7:
                    norm_twice(0, u - E - 1)
            norm_twice(1, 0)
            norm_twice(1, 1)
            x_affine("mix1", (0, 1))
            norm_twice(1, 2)
            norm_twice(1, 3)
            x_affine_low("mix1", (0, 1))
            norm_twice(1, 4)
            norm_twice(1, 5)
            x_affine("mix1", (2, 3))
            x_affine_low("mix1", (2, 3))

            def scan(dst, d0, d1, back, op0, op1):
                if back:
                    link(V.tensor_tensor_scan(dst[:, 0:HALF][:, ::-1], d0, d1[:, ::-1], 0.0, op0, op1))
                else:
                    link(V.tensor_tensor_scan(dst[:, 1:BW], d0, d1, 0.0, op0, op1))

            def block(buf, b):
                return buf[:, BW * b:BW * b + BW]

            def maxima(b):
                dve.wait_ge(kvr_ready, 3 * b + 1)
                k = start(rK, b)
                for i, (M, D) in enumerate(((Mf, E1f), (Mb, E1b))):
                    scan(block(M, b), start(rW0, b), k, i, ALU.add, ALU.max)
                    link(V.memset(block(M, b)[:, ::SEQ], -BIG))
                    V.scalar_tensor_tensor(start(D, b), start(M, b, i), deca[b], k, ALU.add,
                                           ALU.subtract).then_inc(rd_ready, 1)
                m = start(rW0, b)
                link(V.tensor_tensor(m, start(Mf, b), start(Mb, b, 1), ALU.max))
                link(V.scalar_tensor_tensor(m, k, fira[b], m, ALU.add, ALU.max))
                dve.wait_ge(rd_ready, 2 * b + 2)
                V.scalar_tensor_tensor(k, k, fira[b], m, ALU.add, ALU.subtract).then_inc(M_ready, 1)

            def states(b):
                dve.wait_ge(kvr_ready, 3 * b + 2)
                dve.wait_ge(re_ready, 4 * b + 2)
                e1, e2 = start(E1f, b), start(E2f, b)
                scan(block(Bf, b), e1, e2, 0, ALU.mult, ALU.add)
                link(V.tensor_tensor(e2, e2, start(rV, b), ALU.mult))
                scan(block(Af, b), e1, e2, 0, ALU.mult, ALU.add)
                dve.wait_ge(re_ready, 4 * b + 4)
                e1, e2 = start(E1b, b)[:, ::-1], start(E2b, b)
                scan(block(Bb, b), e1, e2, 1, ALU.mult, ALU.add)
                dve.wait_ge(ev_ready, b + 1)
                scan(block(Ab, b), e1, EV[:, HALF * b:HALF * b + HALF], 1, ALU.mult, ALU.add)
                for A in (Af, Ab, Bf, Bb):
                    ins = V.memset(block(A, b)[:, ::SEQ], 0.0)
                ins.then_inc(state_ready, 1)

            def sums(b):
                dve.wait_ge(ew_ready, b + 1)
                dve.wait_ge(state_ready, b + 1)
                n = start(Af, b)
                link(V.tensor_tensor(n, n, start(Mf, b), ALU.mult))
                dve.wait_ge(num_ready, b + 1)
                link(V.tensor_tensor(n, n, start(Ab, b, 1), ALU.add))
                link(V.tensor_tensor(n, n, start(rV, b), ALU.add))
                dve.wait_ge(kvr_ready, 3 * b + 3)
                link(V.scalar_tensor_tensor(n, start(rT, b), 1.0, n, ALU.add, ALU.mult))

            def outputs(b):
                dve.wait_ge(den_ready, b + 1)
                link(V.reciprocal(start(E2b, b), start(Bf, b)))
                V.tensor_tensor(start(E1b, b), start(Af, b), start(E2b, b), ALU.mult).then_inc(sy_ready, 1)
                next_high()
                V.tensor_tensor(sy_lo[b], start(E1b, b), sy_hi[b], ALU.subtract).then_inc(sy_ready, 1)

            for step, b in RECURRENCE_ORDER:
                {"maxima": maxima, "states": states, "sums": sums, "outputs": outputs}[step](b)

            def wo_out(t):
                if t % 2 == 0:
                    name = ("wo", t // 2)
                    filled(name)
                    V.scalar_tensor_tensor(Z[:, t:t + 2], bank(name)[:, 0:2 * C].rearrange("p (t n) -> p t n", t=2),
                                           0.5 / WS, Z[:, t:t + 2], ALU.mult, ALU.add).then_inc(
                                               bank_free[f.bank[name]], 1)
                    released(name)
            norm_tiles(Z, wo_out, range(0, 4))
            x_affine("mix2", (0, 1))
            norm_tiles(Z, wo_out, range(4, 8))
            x_affine_low("mix2", (0, 1))
            x_affine("mix2", (2, 3))
            x_affine_low("mix2", (2, 3))

            def ffn_low(hf):
                for m in range(6):
                    n = 6 * hf + m
                    dve.wait_ge(relu_ready, n + 1)
                    if n >= 2:
                        dve.wait_ge(kf_ready, n - 1)
                    V.tensor_tensor(kfs[m % 2], kfr[m % 2], kfr[m % 2], ALU.mult).then_inc(sq_ready, 1)
                    dve.wait_ge(sq_ready, n + 1)
                    next_high()
                    V.tensor_tensor(kfl[:, m], kfs[m % 2], kfh[:, m], ALU.subtract).then_inc(kf_ready, 1)

            def ffn_out(hf):
                for pr in range(2):
                    name = ("kv", hf, pr)
                    t = 4 * hf + 2 * pr
                    filled(name)
                    dve.wait_ge(tanh_ready, 2 * hf + pr + 1)
                    V.scalar_tensor_tensor(uu[:, pr], tr_[:, 2 * hf + pr], 1.0, bank(name)[:, 0:2 * C], ALU.add,
                                           ALU.mult).then_inc(bank_free[f.bank[name]], 1)
                    released(name)
                    u = uu[:, pr].rearrange("p (t n) -> p t n", t=2)
                    link(V.scalar_tensor_tensor(Z[:, t:t + 2], u, 0.5 / WS, Z[:, t:t + 2], ALU.mult, ALU.add))
                    link(V.tensor_tensor(H[:, t:t + 2], H[:, t:t + 2], Z[:, t:t + 2], ALU.add))
            ffn_low(0)
            ffn_out(0)
            ffn_low(1)
            ffn_out(1)
            norm_tiles(H)
            x_low("attn1")
            gates(1, True)
            V.tensor_copy(crep1.rearrange("p t (r e) -> p t r e", e=E),
                          gat[:, 5][:, :, None, :].broadcast_to([P, NT, 16, E])).then_inc(gate_ready, 1)
            link(V.memset(cstack[0:96, :], 0.0))
            dve.sem_inc(gate_ready, 1)
            for hf in range(2):
                sl = slice(HALF * hf, HALF * (hf + 1))
                name = ("ce", hf)
                next_high()
                V.tensor_tensor(cstack[32:32 + E, sl], bank(name)[0:E], cstack[0:E, sl],
                                ALU.subtract).then_inc(bank_free[f.bank[name]], 1)
                name = ("la", hf)
                filled(name)
                dve.wait_ge(ce_ready, hf + 1)
                if hf:
                    dve.wait_ge(hw_ready, 2)
                V.scalar_tensor_tensor(hwF, bank(name), col16[:, C_BA:C_BA + 1], ceF[:, sl], ALU.add,
                                       ALU.mult).then_inc(hw_ready, 1)
                next_high()
                V.tensor_tensor(hw_lo[:, sl], hwF, hw_hi[:, sl], ALU.subtract).then_inc(hw_ready, 1)
            attention(1, lambda pr: dve.sem_inc(h_ready, 1))

        @block.tensor
        def _(pe):
            T_ = nc.tensor

            def free(name):
                if f.before[name]:
                    by, count = f.release[f.before[name]]
                    pe.wait_ge(readers[by], count)

            def mm(o, w, x, start, stop):
                return T_.matmul(o, w, x, start=start, stop=stop, skip_group_check=True)

            ident = K[:, K_ID:K_ID + P]

            pe.wait_ge(loaded["consts"], 16)
            pe.wait_ge(loaded["tokg"], 32)
            pe.wait_ge(loaded["tokw"], 16 * 7)

            def beta():
                b = bank("beta")[:, 0:C]
                n = 0
                for k in range(8):
                    for s in range(5 if k < 6 else 1):
                        w = raw_w[:, k, s] if k < 6 else raw_wh[:, k - 6]
                        c = 32 + n
                        last = mm(b, gbt[:, c:c + 1].broadcast_to([P, P]), w, n == 0, n == 31)
                        n += 1
                last.then_inc(psum_filled, 1)
            beta()

            def tok_turn(t):
                pe.wait_ge(tokn_ready, t + 1)
                for i in range(2):
                    name = ("tokT", t, i)
                    free(name)
                    for k in range(4):
                        last = T_.transpose(bank(name)[:, P * k:P * k + P],
                                            tx_n[t % 2][:, P * (4 * i + k):P * (4 * i + k + 1)], ident)
                    last.then_inc(psum_filled, 1)

            def tok_product(t):
                name = ("tok", t)
                pe.wait_ge(tokx_ready, t + 1)
                if t == 0:
                    pe.wait_ge(tokw_ready, 3)
                free(name)
                o = bank(name)[:, 0:C]
                hi, lo = tx_hi[t % 2], tx_lo[t % 2]
                for k in range(7):
                    mm(o, hi[:, k], wt_hi[:, k], k == 0, False)
                    mm(o, lo[:, k], wt_hi[:, k], False, False)
                    mm(o, hi[:, k], wt_lo[:, k], False, False)
                mm(o, hi[:, 7], wt_hi[:, 7], False, False)
                mm(o, hi[0:64, 7], wt_lo[0:64, 7], False, True).then_inc(psum_filled, 1)

            for t in range(NT + 1):
                if t < NT:
                    tok_turn(t)
                if t:
                    tok_product(t - 1)

            xc = [0]

            def turn(phase, pairs_=range(4)):
                for pr in pairs_:
                    name = ("x", phase, pr)
                    free(name)
                    for j in range(2):
                        xc[0] += 1
                        pe.wait_ge(xn_ready, xc[0])
                        t = 2 * pr + j
                        for k in range(2):
                            last = T_.transpose(bank(name)[:, 256 * j + P * k:256 * j + P * k + P],
                                                xn[:, t % 4, P * k:P * k + P], ident)
                    last.then_inc(psum_filled, 1)

            def by_rows(o, wa, wb, col0, m, hf, more=()):
                xa, xb = X_hi[:, 4 * hf:4 * hf + 4, 0], X_hi[:, 4 * hf:4 * hf + 4, 1]
                xl = X_lo[:, 4 * hf:4 * hf + 4]
                s = slice(col0, col0 + m)
                mm(o, wa[:, 0, s], xa, True, False)
                mm(o, wa[:, 0, s], xl, False, False)
                mm(o, wa[:, 1, s], xa, False, False)
                mm(o, wb[:, 0, s], xb, False, False)
                for w, x in more:
                    mm(o, w, x, False, False)
                return mm(o, wb[0:64, 1, s], xb[0:64], False, True)

            def by_tokens(o, ah, al, b, wa, wb, s, bias=None, start=True):
                mm(o, ah, wa[:, 0, s], start, False)
                mm(o, al, wa[:, 0, s], False, False)
                mm(o, ah, wa[:, 1, s], False, False)
                mm(o, b, wb[:, 0, s], False, False)
                if bias is not None:
                    mm(o, ones[:], rowh[:, bias:bias + (s.stop - s.start)], False, False)
                    mm(o, ones[:], rowl[:, bias:bias + (s.stop - s.start)], False, False)
                return mm(o, b[0:64], wb[0:64, 1, s], False, True)

            def attention(a, x_pairs):
                wa, wb = (early_a, early_b) if a == 0 else (late_a, late_b)

                def qkv(hf):
                    c0 = 0 if a == 0 else LATE["qkv1"]
                    if x_pairs:
                        pe.wait_ge(x_ready, x_pairs + 2 * hf)
                    for i, (s, o, m) in enumerate(SLOTS):
                        name = ("qkv", a, hf, s)
                        free(name)
                        more = ()
                        if a == 1:
                            sl = slice(HALF * hf, HALF * (hf + 1))
                            bh, bl = fullp[:, 0, FW + o:FW + o + m], fullp[:, 1, FW + o:FW + o + m]
                            bb = fullp[0:72, 0, FW + 576 + o:FW + 576 + o + m]
                            more = ((bh, hw_hi[:, sl]), (bh, hw_lo[:, sl]), (bl, hw_hi[:, sl]), (bb, cstack[0:72, sl]))
                        by_rows(bank(name)[0:m], wa, wb, c0 + o, m, hf, more).then_inc(psum_filled, 1)

                def scores(hf):
                    n0 = 2 * a + hf
                    pe.wait_ge(bd_ready, 3 * n0 + 2)
                    pe.wait_ge(qkv_ready, 5 * n0 + 5)
                    qa, qb = pairs["QA"], pairs["QB"]
                    for pr in range(2):
                        name = ("st", a, hf, pr)
                        free(name)
                        for s in range(16):
                            g = 16 * pr + s
                            at = 256 * (s // 8) + 16 * (s % 8)
                            o = bank(name)[:, at:at + 16]
                            q = slice(16 * g, 16 * g + 16)
                            mm(o, KAbd[:, 0, g], qa[:, 0, q], True, False)
                            mm(o, KAbd[:, 0, g], qa[:, 1, q], False, False)
                            mm(o, KAbd[:, 1, g], qa[:, 0, q], False, True)
                            o = bank(name)[0:CB, at + P:at + P + 16]
                            mm(o, KVBbd[0:CB, 0, g], qb[0:CB, 0, q], True, False)
                            mm(o, KVBbd[0:CB, 0, g], qb[0:CB, 1, q], False, False)
                            last = mm(o, KVBbd[0:CB, 1, g], qb[0:CB, 0, q], False, True)
                        last.then_inc(psum_filled, 1)

                def values(hf, hl):
                    pe.wait_ge(bd_ready, 3 * (2 * a + hf) + 3)
                    for g in range(4):
                        name = ("va", a, hf, hl, g)
                        free(name)
                        o = bank(name).bitcast(F16)
                        for s in range(8):
                            last = T_.transpose(o[:, P * s:P * s + P], VAbd[:, hl, 8 * g + s], id16[:])
                        last.then_inc(psum_filled, 1)
                    for g in range(2):
                        name = ("vb", a, hf, hl, g)
                        free(name)
                        o = bank(name)[0:CB].bitcast(F16)
                        for s in range(16):
                            last = T_.transpose(o[:, CB * s:CB * s + CB], KVBbd[64:P, hl, 16 * g + s], id16[64:P, 64:P])
                        last.then_inc(psum_filled, 1)

                def turn_scores(hf):
                    for pr in range(2):
                        name = ("s", a, hf, pr)
                        free(name)
                        pe.wait_ge(st_ready, 2 * (2 * a + hf) + pr + 1)
                        for j in range(2):
                            T_.transpose(bank(name)[:, C * j:C * j + P], ST[:, pr, j, 0], ident)
                            last = T_.transpose(bank(name)[:, C * j + P:C * j + C], ST[0:CB, pr, j, 1],
                                                ident[0:CB, 0:CB])
                        last.then_inc(psum_filled, 1)

                def turn_probabilities(hf):
                    for pr in range(2):
                        name = ("pt", a, hf, pr)
                        free(name)
                        pe.wait_ge(p_ready, 2 * (2 * a + hf) + pr + 1)
                        sm = SM[:, pr].rearrange("p h j -> p (h j)")
                        for j in range(2):
                            T_.transpose(bank(name)[:, 256 * j:256 * j + P], sm[:, C * j:C * j + P], ident)
                            last = T_.transpose(bank(name)[0:CB, 256 * j + P:256 * j + 2 * P],
                                                sm[:, C * j + P:C * j + C], ident)
                        last.then_inc(psum_filled, 1)

                def outputs(hf):
                    n0 = 2 * a + hf
                    pe.wait_ge(v_act_ready, 8 * (n0 + 1))
                    pe.wait_ge(v_dve_ready, 4 * (n0 + 1))
                    for pr in range(2):
                        name = ("ot", a, hf, pr)
                        free(name)
                        pe.wait_ge(pt_ready, 2 * n0 + pr + 1)
                        for s in range(16):
                            g = 16 * pr + s
                            t, q = 2 * pr + s // 8, slice(16 * (s % 8), 16 * (s % 8) + 16)
                            at = 256 * (s // 8) + 16 * (s % 8)
                            o = bank(name)[:, at:at + 16]
                            mm(o, VA[:, 0, g], PT[:, 0, t, 0, q], True, False)
                            mm(o, VA[:, 0, g], PT[:, 1, t, 0, q], False, False)
                            mm(o, VA[:, 1, g], PT[:, 0, t, 0, q], False, True)
                            o = bank(name)[0:CB, at + P:at + P + 16]
                            mm(o, VB[0:CB, 0, g], PT[0:CB, 0, t, 1, q], True, False)
                            mm(o, VB[0:CB, 0, g], PT[0:CB, 1, t, 1, q], False, False)
                            last = mm(o, VB[0:CB, 1, g], PT[0:CB, 0, t, 1, q], False, True)
                        last.then_inc(psum_filled, 1)

                def project(hf):
                    c1 = EARLY["out0"] if a == 0 else LATE["proj"]
                    for pr in range(2):
                        name = ("pj", a, hf, pr)
                        free(name)
                        pe.wait_ge(ot_ready, 2 * (2 * a + hf) + pr + 1)
                        for j in range(2):
                            t = 2 * pr + j
                            last = by_tokens(bank(name)[:, C * j:C * j + C], O_hi[:, t, 0], O_lo[:, t], O_hi[:, t, 1],
                                             wa, wb, slice(c1, c1 + C), R_OUT if a == 0 else R_PJ)
                        last.then_inc(psum_filled, 1)

                for step, hf in ATTENTION_ORDER:
                    if step == "qkv":
                        qkv(hf)
                    elif step == "st":
                        scores(hf)
                    elif step in ("values0", "values1"):
                        values(hf, int(step[-1]))
                    elif step == "s":
                        turn_scores(hf)
                    elif step == "pt":
                        turn_probabilities(hf)
                    elif step == "ot":
                        outputs(hf)
                    else:
                        project(hf)

            turn("attn0")
            pe.wait_ge(wearly, 4)
            pe.wait_ge(cols_ready, 10)
            attention(0, 2)
            turn("moe")
            pe.wait_ge(x_ready, 8)
            free("router0")
            for t in range(NT):
                last = by_tokens(bank("router0")[:, E * t:E * t + E], X_hi[:, t, 0], X_lo[:, t], X_hi[:, t, 1],
                                 early_a, early_b, slice(EARLY["router"], EARLY_N), R_RT)
            last.then_inc(psum_filled, 1)
            pe.wait_ge(wlo, NM)
            for u in range(UNITS + 1):
                if u < UNITS:
                    for n, c, _ in unit_chunks(u):
                        free(("h", n))
                        by_rows(bank(("h", n)), m1a, m1b, P * c, P, u // E).then_inc(psum_filled, 1)
                if u:
                    v = u - 1
                    q = v // 4
                    r = slice(32 * (v % 4), 32 * (v % 4) + 32)
                    terms = [(r, 4 + q % 2, 2 * E + q % 2)] + [(slice(0, P), s_, c) for n, c, s_ in unit_chunks(v)[-2:]]
                    pe.wait_ge(hp_ready, unit_chunks(v)[-1][0] + 1)
                    for pr in range(2):
                        free(("y", v, pr))
                        for j in range(2):
                            o = bank(("y", v, pr))[:, C * j:C * j + C]
                            x = slice(P * (2 * pr + j), P * (2 * pr + j) + P)
                            for i, (rows_, slot, c) in enumerate(terms):
                                w = slice(C * c, C * c + C)
                                mm(o, hgh[slot][rows_, x], m2[rows_, 0, w], i == 0, False)
                                mm(o, hgl[slot][rows_, x], m2[rows_, 0, w], False, False)
                                last = mm(o, hgh[slot][rows_, x], m2[rows_, 1, w], False, i == 2)
                        last.then_inc(psum_filled, 1)
                    if u == 1:
                        pe.wait_ge(gate_ready, 1)
                        for hf in range(2):
                            name = ("ct", hf)
                            free(name)
                            for i in range(4):
                                last = T_.transpose(bank(name)[0:E, P * i:P * i + P], gat[:, 4, 4 * hf + i], ident)
                            last.then_inc(psum_filled, 1)
                    if u % E == 0:
                        pe.wait_ge(ct_ready, 2)
                        for pr in range(2):
                            name = ("b2", 2 * (u // E - 1) + pr)
                            free(name)
                            for j in range(2):
                                t = 2 * name[1] + j
                                last = mm(bank(name)[:, C * j:C * j + C], ctT[:, P * t:P * t + P], b2s[:], True, True)
                            last.then_inc(psum_filled, 1)
            pe.wait_ge(wlo, NM + NL + 1)

            def kvr(block):
                for i in range(3):
                    name = ("kvr"[i], block)
                    c0 = LATE["kvr"] + C * i
                    free(name)
                    if block == 1:
                        for hf in range(2):
                            last = by_rows(bank(name)[64 * hf:64 * hf + 64], late_a, late_b, c0 + P, CB, hf)
                    else:
                        last = by_rows(bank(name), late_a, late_b, c0, P, block // 2)
                    last.then_inc(psum_filled, 1)

            turn("mix1", (0, 1))
            pe.wait_ge(x_ready, 10)
            kvr(0)
            turn("mix1", (2, 3))
            pe.wait_ge(x_ready, 12)
            kvr(1)
            kvr(2)
            c0 = slice(LATE["wo"], LATE["wo"] + C)
            for pr in range(4):
                name = ("wo", pr)
                free(name)
                pe.wait_ge(sy_ready, 4 + 2 * (pr // 2))
                for j in range(2):
                    t = 2 * pr + j
                    o = bank(name)[:, C * j:C * j + C]
                    x = slice(P * t, P * t + P)
                    y = slice(P * (t % 4), P * (t % 4) + P)
                    r = slice(64 * (t // 4), 64 * (t // 4) + 64)
                    mm(o, sy_ah[:, x], late_a[:, 0, c0], True, False)
                    mm(o, sy_al[:, x], late_a[:, 0, c0], False, False)
                    mm(o, sy_ah[:, x], late_a[:, 1, c0], False, False)
                    mm(o, sy_bh[r, y], late_b[r, 0, c0], False, False)
                    mm(o, sy_bl[r, y], late_b[r, 0, c0], False, False)
                    last = mm(o, sy_bh[r, y], late_b[r, 1, c0], False, True)
                last.then_inc(psum_filled, 1)

            def ffn_keys(hf):
                for m in range(6):
                    name = ("kf", hf, m)
                    free(name)
                    by_rows(bank(name), late_a, late_b, LATE["kf"] + P * m, P, hf).then_inc(psum_filled, 1)

            def receptance(hf):
                for pr in range(2):
                    name = ("r", hf, pr)
                    free(name)
                    for j in range(2):
                        t = 4 * hf + 2 * pr + j
                        last = by_tokens(bank(name)[:, C * j:C * j + C], X_hi[:, t, 0], X_lo[:, t], X_hi[:, t, 1],
                                         late_a, late_b, slice(LATE["wr"], LATE["wr"] + C))
                    last.then_inc(psum_filled, 1)

            def ffn_values(hf):
                for pr in range(2):
                    name = ("kv", hf, pr)
                    free(name)
                    for j in range(2):
                        o = bank(name)[:, C * j:C * j + C]
                        x = slice(P * (2 * pr + j), P * (2 * pr + j) + P)
                        for m in range(6):
                            if pr == 0 and j == 0:
                                pe.wait_ge(kf_ready, 6 * hf + m + 1)
                            w = slice(C * m, C * m + C)
                            mm(o, kfh[:, m, x], fullp[:, 0, w], m == 0, False)
                            mm(o, kfl[:, m, x], fullp[:, 0, w], False, False)
                            last = mm(o, kfh[:, m, x], fullp[:, 1, w], False, m == 5)
                    last.then_inc(psum_filled, 1)

            turn("mix2", (0, 1))
            pe.wait_ge(x_ready, 14)
            ffn_keys(0)
            turn("mix2", (2, 3))
            receptance(0)
            pe.wait_ge(x_ready, 16)
            ffn_keys(1)
            ffn_values(0)
            receptance(1)
            ffn_values(1)
            turn("attn1")
            pe.wait_ge(x_ready, 20)
            free("router1")
            for t in range(NT):
                last = by_tokens(bank("router1")[:, E * t:E * t + E], X_hi[:, t, 0], X_lo[:, t], X_hi[:, t, 1],
                                 late_a, late_b, slice(LATE["gate"], LATE["gate"] + E), R_GT)
            last.then_inc(psum_filled, 1)
            pe.wait_ge(gate_ready, 3)
            for hf in range(2):
                name = ("ce", hf)
                free(name)
                for i in range(4):
                    last = T_.transpose(bank(name)[:, P * i:P * i + P], crep1[:, 4 * hf + i], ident)
                last.then_inc(psum_filled, 1)
                name = ("la", hf)
                free(name)
                by_rows(bank(name), late_a, late_b, LATE["la"], P, hf).then_inc(psum_filled, 1)
            pe.wait_ge(hw_ready, 4)
            attention(1, None)


def _patch_order():
    inner, edge, corner, halo = [], [], [], []
    for i in range(-1, 17):
        for j in range(-1, 17):
            a, b = i in (-1, 16), j in (-1, 16)
            if a and b:
                continue
            where = halo if a or b else (corner, edge, inner)[2 - (i in (0, 15)) - (j in (0, 15))]
            where += [(i, j, c) for c in range(3)]
    return inner + edge + corner + halo


def _weight_rows(order):
    rows = np.full((FEAT, 5), PDIM)
    for n, (i, j, c) in enumerate(order):
        for s, (di, dj) in enumerate(((0, 0), (0, 1), (0, -1), (1, 0), (-1, 0))):
            p, q = i + di, j + dj
            if 0 <= p < 16 and 0 <= q < 16:
                rows[n, s] = (p * 16 + q) * 15 + 3 * s + c
    return rows


def _constants():
    k = np.zeros((P, K_N), np.float32)
    p = np.arange(P)
    k[:, K_ID:K_ID + P] = np.eye(P)
    k[:, K_HM:K_HM + HA] = p[:, None] // HD == np.arange(HA)
    k[:, K_HMB:K_HMB + HB] = p[:, None] % CB // HD == np.arange(HB)
    i, j = p[:, None] % SEQ, np.arange(SEQ)
    k[:, K_AM:K_AM + SEQ] = np.where(((j % 8 == 0) & (j <= i)) | (j == i) | (j == i - 1), 0.0, -1e30)
    k[:, K_BNW:K_BNW + 30] = [x for _, w in GROUPS for x in (w, 1, w) * 2]
    k[:, K_TRI:K_TRI + E * E] = (np.arange(E)[None, :] < np.arange(E)[:, None]).reshape(-1)
    return k


def kernel(**inputs):
    import concourse.bacc as bacc
    from concourse.bass_utils import run_bass_kernel_spmd

    g = {k: np.asarray(v) for k, v in inputs.items()}
    f32 = np.float32
    order = _patch_order()
    rows = _weight_rows(order)
    x = np.pad(g["x"], ((0, 0), (0, 0), (1, 1), (1, 1)))
    oi, oj, oc = (np.array(v) for v in zip(*order))
    tok = np.stack([x[:, oc, 16 * a + 1 + oi, 16 * b + 1 + oj] for a in range(4) for b in range(4)], axis=1)
    tok_x = tok.reshape(NT, P, FEAT)
    wz = np.concatenate([g["L0_tok_W"], np.zeros((1, C), f32)])
    tok_w = wz[rows[:PIX]].reshape(6, P, 5, C).transpose(1, 0, 2, 3)
    live = rows[PIX:].min(axis=1)
    live = np.concatenate([live, np.full(64, PDIM)])
    tok_wh = wz[live].reshape(2, P, C).transpose(1, 0, 2).copy()
    tok_wh[64:, 1] = tok_wh[:64, 1]

    def spread(v):
        z = np.concatenate([v, np.zeros(1, f32)])
        a = z[rows[:PIX]].reshape(6, P, 5).transpose(1, 0, 2).reshape(P, 30)
        b = z[live].reshape(2, P).T.copy()
        return a, b
    ga, gb = spread(g["L0_tok_gamma"])
    gb[64:, 1] = gb[:64, 1]
    ba, bb = spread(g["L0_tok_beta"])
    tok_g = np.concatenate([ga, gb], 1)
    tok_bt = np.concatenate([ba, bb], 1)

    def two(ws):
        w = np.concatenate(ws, 1)
        return np.stack([w[:P], np.concatenate([w[P:], w[P:]])], 1)

    def slots(w):
        q, k, v = w[..., :C], w[..., C:2 * C], w[..., 2 * C:]
        return np.concatenate([q[..., :P], k[..., :P], v[..., :P], k[..., P:], v[..., P:], q[..., P:]], -1)

    early = two([slots(g["L0_attn_qkv_w"].T), g["L0_attn_out_w"].T, g["L0_ffn_router_w"]])
    w1, w2, b1 = g["L0_ffn_w1"], g["L0_ffn_w2"], g["L0_ffn_b1"]
    w1c = np.concatenate([w1[:, :, :256].transpose(1, 0, 2).reshape(C, -1), w1[:, :, 256:].transpose(1, 0, 2).reshape(C, -1)], 1)
    moe1 = two([w1c]).reshape(P, -1)
    w2c = np.concatenate([w2[:, :256].reshape(-1, C), w2[:, 256:].reshape(-1, C)])
    moe2 = w2c.reshape(NCH, P, C).transpose(1, 0, 2).reshape(P, -1)
    b1c = np.concatenate([b1[:, :256].reshape(-1), b1[:, 256:].reshape(-1)]).reshape(NCH, P).T
    la = g["L1_ffn_A"].transpose(2, 1, 0).reshape(C, P)
    bm = slots(g["L1_ffn_Bm"].transpose(2, 0, 1).reshape(P, 3 * C))
    bbs = np.zeros((P, 3 * C), f32)
    for r in (0, 32, 64):
        bbs[r:r + E] = slots(g["L1_ffn_bb"])
    late = two([g["L1_attn_Wk_a"].T, g["L1_attn_Wv_a"].T, g["L1_attn_Wr_a"].T, g["L1_attn_Wo_a"].T, g["L1_attn_Wk_f"].T,
                g["L1_attn_Wr_f"].T, g["L1_ffn_Wg"].T, la, slots(g["L1_ffn_Wqkv"].T), g["L1_ffn_Wproj"].T])
    wv = g["L1_attn_Wv_f"].T.reshape(6, P, C).transpose(1, 0, 2).reshape(P, -1)
    full = np.concatenate([wv, bm, bbs], 1)

    def qcols(b):
        s = slots(b)
        return [s[:128], s[128:256], s[256:384], s[384:512], np.concatenate([s[512:], s[512:]])]

    def ab(v):
        return [v[:P], np.concatenate([v[P:], v[P:]])]
    cols = qcols(g["L0_attn_qkv_b"]) + list(b1c.T) + ab(g["L1_attn_ln1_w"]) + ab(g["L1_attn_ln1_b"]) \
        + ab(g["L1_attn_ln2_w"]) + ab(g["L1_attn_ln2_b"]) + ab(g["L1_attn_decay"]) + ab(g["L1_attn_first"]) \
        + [g["L1_ffn_ba"].T.reshape(P)] + qcols(g["L1_ffn_bqkv"])
    cols = np.stack(cols, 1)
    brow = np.concatenate([g["L0_attn_out_b"], g["L0_ffn_router_b"], g["L1_ffn_bproj"], g["L1_ffn_bg"]])[None]
    tok_b = np.broadcast_to(g["L0_tok_b"], (P, C))

    nc = bacc.Bacc("TRN2", target_bir_lowering=False, num_devices=1)
    arrays, args = {}, []
    for name, a in (("tok_x", tok_x), ("tok_w", tok_w), ("tok_wh", tok_wh), ("tok_g", tok_g), ("tok_bt", tok_bt),
                    ("tok_b", tok_b), ("early", early), ("moe1", moe1), ("moe2", moe2), ("moe_b2", g["L0_ffn_b2"]),
                    ("late", late.reshape(P, -1)), ("full", full), ("cols", cols), ("rows", brow),
                    ("consts", _constants())):
        a = np.ascontiguousarray(a)
        arrays[name] = a
        args.append(nc.dram_tensor(name, a.shape, F32, kind="ExternalInput").ap())
    args.append(nc.dram_tensor("out", (P, NT, C), F32, kind="ExternalOutput").ap())
    build(nc, *args)
    r = run_bass_kernel_spmd(nc, [arrays], core_ids=[0])
    return r.results[0]["out"].transpose(1, 0, 2).reshape(64, SEQ, C)
```

```python
from contextlib import ExitStack

import numpy as np

from concourse import mybir

F32 = mybir.dt.float32
F16 = mybir.dt.float16
ALU = mybir.AluOpType
ACT = mybir.ActivationFunctionType
AX = mybir.AxisListType.X

P = 128
C = 192
CB = C - P
SEQ = 16
NT = 8
TOK = NT * P
HALF = TOK // 2
SH = HALF // SEQ
HD = 16
HA, HB = P // HD, CB // HD
NH = HA + HB
E = 8
HID = 288
NCH = E * HID // P
KF = 768
PIX = 768
FEAT = 960
PDIM = 3840
WS = 16.0
EPS = 1e-5
BIG = 1e38

GROUPS = ((294, 5), (294, 5), (168, 4), (12, 3), (192, 1))

K_ID = 0
K_HM = K_ID + P
K_HMB = K_HM + HA
K_AM = K_HMB + HB
K_BNW = K_AM + SEQ
K_TRI = K_BNW + 30
K_N = K_TRI + E * E

C_QB0, C_B1, C_LN1WA, C_LN1WB, C_LN1BA, C_LN1BB, C_LN2WA, C_LN2WB, C_LN2BA, C_LN2BB, C_DECA, C_DECB, \
    C_FIRA, C_FIRB, C_BA, C_QB1 = 0, 5, 23, 24, 25, 26, 27, 28, 29, 30, 31, 32, 33, 34, 35, 36
C_N = 41
R_OUT, R_RT, R_PJ, R_GT, R_N = 0, C, C + E, 2 * C + E, 2 * C + 2 * E

LATE = {}
_at = 0
for _name, _width in (("kvr", 3 * C), ("wo", C), ("kf", KF), ("wr", C), ("gate", E), ("la", P),
                      ("qkv1", 3 * C), ("proj", C)):
    LATE[_name] = _at
    _at += _width
LATE_N = _at
EARLY = {"qkv0": 0, "out0": 3 * C, "router": 4 * C}
EARLY_N = 4 * C + E
FULL_N = 6 * C + 3 * C + 3 * C
SLOTS = (("QA", 0, P), ("KA", P, P), ("VA", 2 * P, P), ("KVB", 3 * P, P), ("QB", 4 * P, CB))


UNITS = 2 * E


def unit_chunks(u):
    e = u % E
    n = 2 * u + u // 4
    chunks = []
    if e % 4 == 0:
        chunks.append((n, 2 * E + e // 4, 4 + u // 4 % 2))
        n += 1
    else:
        n += 1
    return chunks + [(n + i, 2 * e + i, (2 * u + i) % 4) for i in range(2)]


class Fills:

    def __init__(self):
        self.bank, self.before, self.done, self.release = {}, {}, {}, {}
        self.latest, self.count, self.total = {}, {}, 0

    def add(self, name, bank=None, by=None, at=None, counted=True):
        if bank is None:
            bank = self.total % 8
        self.bank[name] = bank
        self.before[name] = self.latest.get(bank)
        self.latest[bank] = name
        by = by or f"bank_free{bank}"
        self.count[by] = at or self.count.get(by, 0) + 1
        self.release[name] = (by, self.count[by])
        if counted:
            self.total += 1
            self.done[name] = self.total


def plan_fills():
    f = Fills()

    def gated(hf):
        f.add(("ce", hf))
        f.add(("la", hf), by="hw_ready", at=2 * hf + 1)

    def norm(phase, pairs=range(4)):
        for pr in pairs:
            if phase.startswith("mix"):
                f.add(("x", phase, pr), by="xf_ready")
            else:
                f.add(("x", phase, pr), by="x_ready", at=4 * PHASES.index(phase) + pr + 1)

    for t in range(NT + 1):
        if t < NT:
            f.add(("tokT", t, 0))
            f.add(("tokT", t, 1), by="tokx_ready")
        if t == 0:
            f.add("beta")
        if t:
            f.add(("tok", t - 1))
        if t in (4, 6, 8):
            norm("attn0", (t // 2 - 2,))

    def attention(a):
        for step, hf in ATTENTION_ORDER:
            if a == 0 and (step, hf) == ("st", 0):
                norm("attn0", (3,))
            if a == 1 and (step, hf) == ("values1", 0):
                gated(1)
            if a == 1 and (step, hf) == ("st", 0):
                norm("attn1", (2, 3))
            if a == 1 and (step, hf) == ("values0", 0):
                f.add(("router1", 1))
            if a == 0 and (step, hf) == ("pj", 1):
                norm("moe", (0, 1))
            if step == "qkv":
                for s in SLOTS:
                    f.add(("qkv", a, hf, s[0]), by="qkv_ready")
            elif step in ("values0", "values1"):
                for g in range(4):
                    f.add(("va", a, hf, int(step[-1]), g), by="v_dve_ready" if g % 2 == 0 else "v_act_ready")
                for g in range(2):
                    f.add(("vb", a, hf, int(step[-1]), g), by="v_act_ready")
            else:
                for i in range(4 if step in ("st", "ot") else 2):
                    f.add((step, a, hf, i), by={"st": "st_ready", "pt": "pt_ready", "ot": "os_ready"}.get(step))

    attention(0)
    for u in range(UNITS + 1):
        if u < UNITS:
            for n, _, _ in unit_chunks(u):
                f.add(("h", n), bank=n % 4, by="gelu_ready")
            if u == 0:
                f.add(("x", "moe", 2), bank=4, by="x_ready", at=7)
                f.add(("x", "moe", 3), bank=5, by="x_ready", at=8)
                f.add("router0", bank=6)
        if u:
            for pr in range(2):
                f.add(("y", u - 1, pr), bank=4 + 2 * ((u - 1) % 2) + pr)
            if u == 2:
                for hf in range(2):
                    f.add(("ct", hf), bank=4 + hf, by="ct_ready")
            if u == UNITS - 1:
                for pr in range(2):
                    f.add(("x", "mix1", pr), bank=pr, by="xf_ready")
            if u % E == 0:
                for pr in range(2):
                    f.add(("b2", 2 * (u // E - 1) + pr), bank=4 + 2 * (u % 2) + pr)
    for n in "kvr":
        f.add((n, 0), by="kvr_ready")
    norm("mix1", (2, 3))
    for block in (1, 2):
        for n in "kvr":
            f.add((n, block), by="kvr_ready")
    for pr in range(4):
        f.add(("wo", pr))
    norm("mix2", (0, 1))
    for m in range(6):
        if m == 3:
            norm("mix2", (2, 3))
        f.add(("kf", 0, m), by="relu_ready")
    for pr in range(2):
        f.add(("r", 0, pr), by="tanh_ready")
    for m in range(6):
        f.add(("kf", 1, m), by="relu_ready")
    for pr in range(2):
        f.add(("kv", 0, pr))
    for pr in range(2):
        f.add(("r", 1, pr), by="tanh_ready")
    for pr in range(2):
        f.add(("kv", 1, pr))
    norm("attn1", (0, 1))
    f.add(("router1", 0))
    gated(0)
    attention(1)
    return f


ATTENTION_ORDER = (("qkv", 0), ("st", 0), ("values0", 0), ("s", 0), ("values1", 0), ("qkv", 1), ("pt", 0), ("ot", 0),
                   ("st", 1), ("pj", 0), ("values0", 1), ("s", 1), ("values1", 1), ("pt", 1), ("ot", 1), ("pj", 1))
RECURRENCE_ORDER = (("maxima", 0), ("maxima", 1), ("states", 0), ("maxima", 2), ("states", 1), ("sums", 0),
                    ("states", 2), ("sums", 1), ("outputs", 0), ("sums", 2), ("outputs", 1), ("outputs", 2))
PHASES = ("attn0", "moe", "mix1", "mix2", "attn1")


def build(nc, tok_x, tok_w, tok_wh, tok_g, tok_bt, tok_b, early, moe1, moe2, moe_b2, late, full, cols, rows, consts,
          out):
    f = plan_fills()
    with ExitStack() as ctx:
        def sb(name, shape, dt=F32):
            return ctx.enter_context(nc.sbuf_tensor(name, shape, dt))

        def sem(name):
            return ctx.enter_context(nc.semaphore(name))

        H = sb("H", [P, NT, C])
        K = sb("K", [P, K_N])
        col = sb("col", [P, C_N])
        col16 = sb("col16", [P, C_N])
        rowr = sb("rowr", [1, R_N])
        rowh = sb("rowh", [1, R_N], F16)
        rowl = sb("rowl", [1, R_N], F16)
        ones = sb("ones", [1, P], F16)
        id16 = sb("id16", [P, P], F16)
        mhalf = sb("mhalf", [P, 1])
        tokb = sb("tokb", [P, C])
        nbias = sb("nbias", [P, 2])
        stats = sb("stats", [P, 2, 30])
        wstats = sb("wstats", [P, 2, 30])
        mv = sb("mv", [P, NT, 2])
        ve = sb("ve", [P, NT])
        rstd = sb("rstd", [P, NT])
        xn = sb("xn", [P, NT // 2, 2 * P])
        X_hi = sb("X_hi", [P, NT, 2, P], F16)
        X_lo = sb("X_lo", [P, NT, P], F16)
        gat = sb("gat", [P, 6, NT, E])
        gsum = sb("gsum", [P, 3, NT])
        early_a = sb("early_a", [P, 2, EARLY_N], F16)
        early_b = sb("early_b", [P, 2, EARLY_N], F16)
        late_a = sb("late_a", [P, 2, LATE_N], F16)
        late_b = sb("late_b", [P, 2, LATE_N], F16)
        fullp = sb("fullp", [P, 2, FULL_N], F16)
        b2s = sb("b2s", [E, C])
        T_WORDS = 6144
        T = sb("T", [P, T_WORDS])
        BW = HALF + 1
        RW = 3 * BW
        R = sb("R", [P, 14 * RW])
        Q = sb("Q", [P, 6144])
        PS = ctx.enter_context(nc.psum_tensor("PS", [P, 8, 512], F32))

        def bank(name):
            return PS[:, f.bank[name], :]

        Z = T[:, 0:NT * C].rearrange("p (t n) -> p t n", t=NT)
        raw_w = T[:, 0:5760].rearrange("p (k s n) -> p k s n", k=6, s=5)
        raw_wh = T[:, 5760:6144].rearrange("p (k n) -> p k n", k=2)
        tok_in = [R[:, 8192 + 960 * i:8192 + 960 * (i + 1)] for i in range(3)]
        tx_n = [R[:, 1024 * i:1024 * i + 1024] for i in range(2)]
        tx_hi = [R[:, 2048 + 512 * i:2560 + 512 * i].bitcast(F16).rearrange("p (k n) -> p k n", k=8) for i in range(2)]
        tx_lo = [R[:, 3072 + 512 * i:3584 + 512 * i].bitcast(F16).rearrange("p (k n) -> p k n", k=8) for i in range(2)]
        wf = R[:, 4096:4096 + 1536].rearrange("p (k n) -> p k n", k=8)
        wt_hi = R[:, 5632:6400].bitcast(F16).rearrange("p (k n) -> p k n", k=8)
        wt_lo = R[:, 6400:7168].bitcast(F16).rearrange("p (k n) -> p k n", k=8)
        gbt = R[:, 7168:7168 + 64]
        scaled = R[:, 14080:14080 + 3 * 5 * C].rearrange("p (k s n) -> p k s n", k=3, s=5)
        raw_early = R[:, 12416:12416 + 2 * EARLY_N].rearrange("p (k n) -> p k n", k=2)
        KAbd = R[:, 0:4096].bitcast(F16).rearrange("p (l s n) -> p l s n", l=2, s=SH)
        KVBbd = R[:, 4096:6144].bitcast(F16).rearrange("p (l s n) -> p l s n", l=2, s=SH)
        VAbd = R[:, 6144:10240].bitcast(F16).rearrange("p (l s n) -> p l s n", l=2, s=SH)
        VA = R[:, 12288:16384].bitcast(F16).rearrange("p (l s n) -> p l s n", l=2, s=SH)
        VB = R[:, 10240:12288].bitcast(F16).rearrange("p (l s n) -> p l s n", l=2, s=SH)
        M1 = 2304
        raw_m1a = T[:, 0:M1]
        raw_m1b = T[:, M1:2 * M1]
        raw_m2 = T[:, 0:NCH * C]
        m1a = R[:, 16384:16384 + M1].bitcast(F16).rearrange("p (l n) -> p l n", l=2)
        m1b = R[:, 16384 + M1:16384 + 2 * M1].bitcast(F16).rearrange("p (l n) -> p l n", l=2)
        m2 = sb("m2", [P, 2, NCH * C], F16)

        def qv(at, n):
            return Q[:, at:at + n].bitcast(F16)
        pairs = {"QA": qv(0, 512), "KA": qv(512, 512), "VA": qv(1024, 512), "KVB": qv(1536, 512), "QB": qv(2048, 512)}
        pairs = {k: v.rearrange("p (l n) -> p l n", l=2) for k, v in pairs.items()}
        ST = Q[:, 2560:3584].rearrange("p (r t k n) -> p r t k n", r=2, t=2, k=2)
        OS = Q[:, 2560:3584].rearrange("p (t k n) -> p t k n", t=4, k=2)
        SM = Q[:, 3584:4352].rearrange("p (r h j) -> p r h j", r=2, j=SEQ)
        PT = Q[:, 4352:5376].bitcast(F16).rearrange("p (l t k n) -> p l t k n", l=2, t=4, k=2)
        O_hi = Q[:, 5376:5888].bitcast(F16).rearrange("p (t k n) -> p t k n", t=4, k=2)
        O_lo = Q[:, 5888:6144].bitcast(F16).rearrange("p (t n) -> p t n", t=4)
        smx = sb("smx", [P, 2, 3, 2 * NH])
        ranks = [v.rearrange("p (l t e f) -> p l t e f", l=2, t=NT, e=E) for v in (Q[:, 5120:6144], R[:, 20480:21504])]
        ge = [Q[:, 512 * i:512 * i + 512] for i in range(3)]
        hgh = [Q[:, 1536 + 512 * i:1792 + 512 * i].bitcast(F16) for i in range(6)]
        hgl = [Q[:, 1792 + 512 * i:2048 + 512 * i].bitcast(F16) for i in range(6)]
        ctT = Q[0:E, 4608:5632]
        sy_ah = Q[:, 0:512].bitcast(F16)
        sy_al = Q[:, 512:1024].bitcast(F16)
        sy_bh = Q[:, 1024:1280].bitcast(F16)
        sy_bl = Q[:, 1280:1536].bitcast(F16)
        sy_hi = (sy_ah[:, 0:HALF], sy_bh, sy_ah[:, HALF:TOK])
        sy_lo = (sy_al[:, 0:HALF], sy_bl, sy_al[:, HALF:TOK])
        kfr = [Q[:, 1536 + 512 * i:2048 + 512 * i] for i in range(2)]
        kfs = [R[:, 512 * i:512 + 512 * i] for i in range(2)]
        kfh = Q[:, 3072:4608].bitcast(F16).rearrange("p (m n) -> p m n", m=6)
        kfl = Q[:, 4608:6144].bitcast(F16).rearrange("p (m n) -> p m n", m=6)
        kfh = (kfh, R[:, 8192:9728].bitcast(F16).rearrange("p (m n) -> p m n", m=6))
        kfl = (kfl, R[:, 9728:11264].bitcast(F16).rearrange("p (m n) -> p m n", m=6))
        tr_ = R[:, 2048:2048 + 4 * 2 * C].rearrange("p (r n) -> p r n", r=4)
        uu = R[:, 6144:6144 + 4 * C].rearrange("p (r n) -> p r n", r=2)
        xt_f = {n: v.rearrange("p (r t k n) -> p r t k n", r=4, t=2, k=2)
                for n, v in (("mix1", R[:, 4 * RW:4 * RW + 2048]), ("mix2", R[:, 4096:6144]))}
        EV = Q[:, 2048:2048 + 3 * HALF]
        crep1 = R[:, 19456:20480].rearrange("p (t n) -> p t n", t=NT)
        ceF = R[:, 16384:17408]
        hwF = R[:, 17408:17920]
        hw_hi = R[:, 17920:18432].bitcast(F16)
        hw_lo = R[:, 18432:18944].bitcast(F16)
        cstack = R[:, 18944:19456].bitcast(F16)
        r_ = [R[:, RW * i:RW * (i + 1)] for i in range(14)]
        rK, rV, rT, rW0, Mf, Mb, E1f, E2f, E1b, E2b, Af, Ab, Bf, Bb = r_

        def start(buf, b, shift=0):
            return buf[:, BW * b + shift:BW * b + shift + HALF]

        loaded = {n: sem("in_" + n) for n in ("consts", "cols", "tokg", "early", "moe", "late", "full", "b2")}
        tokw_in = [sem(f"tokw_in{k}") for k in range(7)]
        scaled_ready = sem("scaled_ready")
        folded = sem("folded")
        x_in = [sem(f"x_in{i}") for i in range(3)]
        out_done = sem("out_done")
        psum_filled = sem("psum_filled")
        bank_free = [sem(f"bank_free{i}") for i in range(8)]
        const_ready = sem("const_ready")
        cols_ready = sem("cols_ready")
        dve_step = sem("dve_step")
        act_step = sem("act_step")
        pool_step = sem("pool_step")
        nbias_ready = sem("nbias_ready")
        var_ready = sem("var_ready")
        rstd_ready = sem("rstd_ready")
        xn_ready = sem("xn_ready")
        tokn_ready = sem("tokn_ready")
        hi_ready = sem("hi_ready")
        tokw_ready = sem("tokw_ready")
        tokx_ready = sem("tokx_ready")
        x_ready = sem("x_ready")
        wearly = sem("wearly")
        early_low = sem("early_low")
        whi = sem("whi")
        wlo = sem("wlo")
        qkv_ready = sem("qkv_ready")
        bd_ready = sem("bd_ready")
        st_ready = sem("st_ready")
        v_act_ready = sem("v_act_ready")
        v_dve_ready = sem("v_dve_ready")
        smax_ready = sem("smax_ready")
        gmax_ready = sem("gmax_ready")
        exp_ready = sem("exp_ready")
        p_ready = sem("p_ready")
        pt_ready = sem("pt_ready")
        os_ready = sem("os_ready")
        ot_ready = sem("ot_ready")
        gate_ready = sem("gate_ready")
        ct_ready = sem("ct_ready")
        gelu_ready = sem("gelu_ready")
        hp_ready = sem("hp_ready")
        kvr_ready = sem("kvr_ready")
        rd_ready = sem("rd_ready")
        re_ready = sem("re_ready")
        M_ready = sem("M_ready")
        mm_ready = sem("mm_ready")
        ev_ready = sem("ev_ready")
        ew_ready = sem("ew_ready")
        state_ready = sem("state_ready")
        num_ready = sem("num_ready")
        den_ready = sem("den_ready")
        sy_ready = sem("sy_ready")
        xf_ready = sem("xf_ready")
        relu_ready = sem("relu_ready")
        sq_ready = sem("sq_ready")
        kf_ready = sem("kf_ready")
        tanh_ready = sem("tanh_ready")
        ce_ready = sem("ce_ready")
        hw_ready = sem("hw_ready")
        h_ready = sem("h_ready")

        readers = {"tokx_ready": tokx_ready, "x_ready": x_ready, "xf_ready": xf_ready, "qkv_ready": qkv_ready,
                   "st_ready": st_ready, "v_dve_ready": v_dve_ready, "v_act_ready": v_act_ready, "pt_ready": pt_ready,
                   "os_ready": os_ready, "ct_ready": ct_ready, "gelu_ready": gelu_ready,
                   "kvr_ready": kvr_ready, "relu_ready": relu_ready, "tanh_ready": tanh_ready, "hw_ready": hw_ready}
        readers.update({f"bank_free{i}": bank_free[i] for i in range(8)})

        block = ctx.enter_context(nc.Block())

        moe_pieces = []
        for a in range(0, M1, 576):
            moe_pieces.append((raw_m1a[:, a:a + 576], m1a[:, 0, a:a + 576], m1a[:, 1, a:a + 576], WS))
        for a in range(0, M1, 576):
            moe_pieces.append((raw_m1b[:, a:a + 576], m1b[:, 0, a:a + 576], m1b[:, 1, a:a + 576], WS))
        for a in range(0, NCH * C, 576):
            moe_pieces.append((raw_m2[:, a:a + 576], m2[:, 0, a:a + 576], m2[:, 1, a:a + 576], WS))
        late_pieces = []
        raw_la = T[:, 0:LATE_N]
        raw_lb = T[:, LATE_N:2 * LATE_N]
        raw_f = T[:, 0:FULL_N]
        late_cuts = [(a, min(a + 576, LATE_N)) for a in range(0, LATE_N, 576)]
        for a, b in late_cuts:
            late_pieces.append((raw_la[:, a:b], late_a[:, 0, a:b], late_a[:, 1, a:b], WS))
            late_pieces.append((raw_lb[:, a:b], late_b[:, 0, a:b], late_b[:, 1, a:b], WS))
        FW = 6 * C
        for a, b, s in ((0, 576, WS), (576, FW, WS), (FW, FW + 576, 1.0), (FW + 576, FULL_N, WS)):
            late_pieces.append((raw_f[:, a:b], fullp[:, 0, a:b], fullp[:, 1, a:b], s))
        NM, NL, N1 = len(moe_pieces), len(late_pieces), 2 * M1 // 576

        @block.sync
        def _(sp):
            sp.dma_start(K[:], consts).then_inc(loaded["consts"], 16)
            sp.dma_start(gbt[:, 0:32], tok_g).then_inc(loaded["tokg"], 16)
            sp.dma_start(gbt[:, 32:64], tok_bt).then_inc(loaded["tokg"], 16)
            sp.dma_start(tok_in[0], tok_x[0]).then_inc(x_in[0], 16)
            for k in (3, 0, 4, 1, 5, 2):
                sp.dma_start(raw_w[:, k], tok_w[:, k]).then_inc(tokw_in[k], 16)
            sp.dma_start(raw_wh, tok_wh).then_inc(tokw_in[6], 16)
            sp.dma_start(tok_in[1], tok_x[1]).then_inc(x_in[1], 16)
            sp.dma_start(tokb[:], tok_b).then_inc(loaded["cols"], 16)
            sp.dma_start(col[:], cols).then_inc(loaded["cols"], 16)
            sp.dma_start(rowr[:], rows).then_inc(loaded["cols"], 16)
            sp.dma_start(tok_in[2], tok_x[2]).then_inc(x_in[2], 16)
            sp.dma_start(raw_early, early).then_inc(loaded["early"], 16)
            sp.dma_start(b2s[:], moe_b2).then_inc(loaded["b2"], 16)
            for t in range(3, NT):
                sp.wait_ge(tokn_ready, t - 2)
                sp.dma_start(tok_in[t % 3], tok_x[t]).then_inc(x_in[t % 3], 16)
            sp.wait_ge(tokw_ready, 2)
            sp.wait_ge(bank_free[f.bank["beta"]], f.release["beta"][1])
            sp.dma_start(T[:, 0:2 * M1], moe1).then_inc(loaded["moe"], 16)
            sp.wait_ge(wlo, N1)
            sp.dma_start(raw_m2, moe2).then_inc(loaded["moe"], 16)
            sp.wait_ge(wlo, NM)
            sp.dma_start(T[:, 0:2 * LATE_N], late).then_inc(loaded["late"], 16)
            sp.wait_ge(wlo, NM + 2 * len(late_cuts))
            sp.dma_start(raw_f, full).then_inc(loaded["full"], 16)
            for pr in range(4):
                sp.wait_ge(h_ready, pr + 1)
                sp.dma_start(out[:, 2 * pr:2 * pr + 2, :], H[:, 2 * pr:2 * pr + 2, :]).then_inc(out_done, 16)
            sp.wait_ge(out_done, 4 * 16)

        @block.gpsimd
        def _(pool):
            nc.gpsimd.memset(mhalf[:], -0.5)
            nc.gpsimd.memset(ones[:], 1.0).then_inc(const_ready, 1)
            steps = [0]

            def one_over_std(n, t):
                pool.wait_ge(var_ready, n + 1)
                nc.gpsimd.tensor_scalar(ve[:, t:t + 1], mv[:, t, 1:2], EPS, None, ALU.add).then_inc(pool_step, 1)
                steps[0] += 1
                pool.wait_ge(pool_step, steps[0])
                nc.gpsimd.tensor_tensor(rstd[:, t:t + 1], ve[:, t:t + 1], mhalf[:], ALU.pow).then_inc(rstd_ready, 1)

            def low_part(n, raw, hi, lo):
                pool.wait_ge(whi, n + 1)
                nc.gpsimd.tensor_tensor(lo, raw, hi, ALU.subtract).then_inc(wlo, 1)

            def tile_norm(n, t):
                one_over_std(n, t)
                pool.wait_ge(rstd_ready, n + 1)
                if t >= 2:
                    pool.wait_ge(tokn_ready, t - 1)
                nc.gpsimd.tensor_scalar(nbias[:, t % 2:t % 2 + 1], mv[:, t, 0:1], rstd[:, t:t + 1], -1.0, ALU.mult,
                                        ALU.mult).then_inc(nbias_ready, 1)

            pool.wait_ge(const_ready, 1)
            n = 0
            tile_norm(0, 0)
            for i in range(3):
                pool.wait_ge(scaled_ready, i + 1)
                nc.gpsimd.tensor_tensor(wf[:, 3 + i], scaled[:, i, 0], scaled[:, i, 1], ALU.add).then_inc(pool_step, 1)
                steps[0] += 1
                for j in (2, 3, 4):
                    pool.wait_ge(pool_step, steps[0])
                    ins = nc.gpsimd.tensor_tensor(wf[:, 3 + i], wf[:, 3 + i], scaled[:, i, j], ALU.add)
                    if j < 4:
                        ins.then_inc(pool_step, 1)
                        steps[0] += 1
                    else:
                        ins.then_inc(folded, 1)
            for t in range(1, 4):
                tile_norm(t, t)
            pool.wait_ge(wearly, 2)
            nc.gpsimd.tensor_tensor(early_a[:, 1], raw_early[:, 0], early_a[:, 0], ALU.subtract).then_inc(early_low, 1)
            n = 4
            for t in range(4, NT):
                tile_norm(n, t)
                one_over_std(n + 1, t - 4)
                n += 2
                if t == 4:
                    pool.wait_ge(wearly, 4)
                    pool.wait_ge(rstd_ready, n)
                    nc.gpsimd.tensor_tensor(early_b[0:CB, 1], raw_early[0:CB, 1], early_b[0:CB, 0],
                                            ALU.subtract).then_inc(early_low, 1)
                    pool.wait_ge(early_low, 2)
            for t in range(4, NT):
                one_over_std(n, t)
                n += 1
            for i, (raw, hi, lo, _) in enumerate(moe_pieces):
                if i == 11:
                    for t in range(4):
                        one_over_std(n, t)
                        n += 1
                low_part(i, raw, hi, lo)
            for t in range(4, NT):
                one_over_std(n, t)
                n += 1
            for i, (raw, hi, lo, _) in enumerate(late_pieces):
                low_part(NM + i, raw, hi, lo)
            pool.wait_ge(wlo, NM + NL)
            nc.gpsimd.tensor_copy(fullp[64:64 + E, 0, FW + 576:FULL_N],
                                  fullp[64:64 + E, 1, FW + 576:FULL_N]).then_inc(wlo, 1)
            pool.wait_ge(wlo, NM + NL + 1)
            for hf in range(2):
                for k in range(5):
                    if k:
                        one_over_std(n, 4 * hf + k - 1)
                        n += 1
                    if k < 4:
                        one_over_std(n, 4 * hf + k)
                        n += 1

            def link(ins):
                ins.then_inc(pool_step, 1)
                steps[0] += 1
                pool.wait_ge(pool_step, steps[0])

            def exponents(b):
                pool.wait_ge(M_ready, b + 1)
                mf, mb, m = start(Mf, b), start(Mb, b, 1), start(rW0, b)
                nc.gpsimd.tensor_tensor(mf, mf, m, ALU.subtract).then_inc(pool_step, 1)
                nc.gpsimd.tensor_tensor(mb, mb, m, ALU.subtract).then_inc(mm_ready, 1)
                steps[0] += 1

            def weighted(b):
                pool.wait_ge(re_ready, 4 * b + 4)
                nc.gpsimd.tensor_tensor(EV[:, HALF * b:HALF * b + HALF], start(E2b, b), start(rV, b),
                                        ALU.mult).then_inc(ev_ready, 1)

            def denominator(b):
                pool.wait_ge(ew_ready, b + 1)
                pool.wait_ge(state_ready, b + 1)
                ec, ef, eb = start(rK, b), start(Mf, b), start(Mb, b, 1)
                ab, bf, bb = start(Ab, b, 1), start(Bf, b), start(Bb, b, 1)
                nc.gpsimd.tensor_tensor(ab, ab, eb, ALU.mult).then_inc(num_ready, 1)
                nc.gpsimd.tensor_tensor(bf, bf, ef, ALU.mult).then_inc(pool_step, 1)
                steps[0] += 1
                link(nc.gpsimd.tensor_tensor(bb, bb, eb, ALU.mult))
                link(nc.gpsimd.tensor_tensor(bf, bf, bb, ALU.add))
                nc.gpsimd.tensor_tensor(bf, bf, ec, ALU.add).then_inc(den_ready, 1)

            for step, b in RECURRENCE_ORDER:
                if step == "maxima":
                    exponents(b)
                elif step == "states":
                    weighted(b)
                elif step == "sums":
                    denominator(b)
            for phase in range(2):
                for t in range(NT):
                    one_over_std(n, t)
                    n += 1

        @block.scalar
        def _(act):
            hn = [0]

            def filled(name):
                act.wait_ge(psum_filled, f.done[name])

            def x_high(phase, pairs_=range(4)):
                for pr in pairs_:
                    name = ("x", phase, pr)
                    filled(name)
                    nc.scalar.activation(X_hi[:, 2 * pr:2 * pr + 2],
                                         bank(name).rearrange("p (t k n) -> p t k n", t=2, k=2),
                                         ACT.Copy).then_inc(hi_ready, 1)
                    hn[0] += 1

            def tok_norm(t):
                act.wait_ge(nbias_ready, t + 1)
                x, n, s_, b = tok_in[t % 3], tx_n[t % 2], rstd[:, t:t + 1], nbias[:, t % 2:t % 2 + 1]
                nc.scalar.activation(n[:, 0:FEAT], x, ACT.Identity, scale=s_, bias=b)
                nc.scalar.activation(n[:, FEAT:1024], x[:, FEAT - 64:FEAT], ACT.Identity, scale=s_,
                                     bias=b).then_inc(tokn_ready, 1)

            act.wait_ge(loaded["tokg"], 32)
            for i in range(3):
                k = 3 + i
                act.wait_ge(tokw_in[k], 16)
                for s_ in range(5):
                    c = 5 * k + s_
                    ins = nc.scalar.activation(scaled[:, i, s_], raw_w[:, k, s_], ACT.Copy, scale=gbt[:, c:c + 1])
                ins.then_inc(scaled_ready, 1)
                if i == 0:
                    tok_norm(0)
            act.wait_ge(tokw_in[6], 16)
            nc.scalar.activation(wf[:, 6], raw_wh[:, 0], ACT.Copy, scale=gbt[:, 30:31]).then_inc(act_step, 1)
            nc.scalar.activation(wf[:, 7], raw_wh[:, 1], ACT.Copy, scale=gbt[:, 31:32]).then_inc(act_step, 1)
            tok_norm(1)
            act.wait_ge(act_step, 2)
            act.wait_ge(tokw_ready, 1)
            act.wait_ge(folded, 3)
            nc.scalar.activation(wt_hi[:], wf[:], ACT.Copy, scale=WS).then_inc(tokw_ready, 1)
            for t in range(NT):
                for i in range(2):
                    name = ("tokT", t, i)
                    filled(name)
                    if i == 0 and t >= 2:
                        filled(("tok", t - 2))
                    nc.scalar.activation(tx_hi[t % 2][:, 4 * i:4 * i + 4, :], bank(name), ACT.Copy).then_inc(hi_ready, 1)
                    hn[0] += 1
                if t + 2 < NT:
                    tok_norm(t + 2)
                if t == 0:
                    act.wait_ge(loaded["cols"], 48)
                    nc.scalar.activation(col16[:], col[:], ACT.Copy, scale=WS).then_inc(cols_ready, 1)
                    act.wait_ge(loaded["consts"], 16)
                    nc.scalar.activation(id16[:], K[:, K_ID:K_ID + P], ACT.Copy).then_inc(cols_ready, 1)
                    for a, b, s_ in ((R_OUT, C, WS * WS), (R_RT, E, WS), (R_PJ, C, WS * WS), (R_GT, E, WS)):
                        nc.scalar.activation(rowh[:, a:a + b], rowr[:, a:a + b], ACT.Copy,
                                             scale=s_).then_inc(cols_ready, 1)
                if t in (1, 2):
                    act.wait_ge(loaded["early"], 16)
                    w = (early_a, early_b)[t - 1]
                    nc.scalar.activation(w[:, 0, :], raw_early[:, t - 1], ACT.Copy, scale=WS).then_inc(wearly, 1)
                    nc.scalar.activation(raw_early[:, t - 1], raw_early[:, t - 1], ACT.Copy, scale=WS).then_inc(wearly, 1)
                if t in (4, 6):
                    x_high("attn0", (t // 2 - 2,))

            def high_part(raw, hi, lo, scale):
                nc.scalar.activation(hi, raw, ACT.Copy, scale=scale).then_inc(act_step, 1)
                ast[0] += 1
                nc.scalar.activation(raw, raw, ACT.Copy, scale=scale).then_inc(whi, 1)
            ast = [2]

            def x_high_affine(phase, pairs_):
                for pr in pairs_:
                    act.wait_ge(xf_ready, xf[0] + 1)
                    xf[0] += 1
                    nc.scalar.activation(X_hi[:, 2 * pr:2 * pr + 2], xt_f[phase][:, pr], ACT.Copy).then_inc(hi_ready, 1)
                    hn[0] += 1
            xf = [0]


            def attention(a, before, spare=lambda step: None):
                cb = C_QB0 if a == 0 else C_QB1

                def values(hf, hl):
                    for g in (1, 3):
                        name = ("va", a, hf, hl, g)
                        filled(name)
                        nc.scalar.activation(VA[:, hl, 8 * g:8 * g + 8, :],
                                             bank(name).bitcast(F16).rearrange("p (s n) -> p s n", s=8),
                                             ACT.Copy).then_inc(v_act_ready, 1)
                    for g in range(2):
                        name = ("vb", a, hf, hl, g)
                        filled(name)
                        nc.scalar.activation(VB[0:CB, hl, 16 * g:16 * g + 16, :],
                                             bank(name)[0:CB].bitcast(F16).rearrange("p (s n) -> p s n", s=16),
                                             ACT.Copy).then_inc(v_act_ready, 1)

                for step, hf in ATTENTION_ORDER:
                    if (step, hf) in before:
                        before[step, hf]()
                    if step == "qkv":
                        n0 = 2 * a + hf
                        if n0:
                            act.wait_ge(bd_ready, 3 * n0)
                        for i, (s, o, m) in enumerate(SLOTS):
                            name = ("qkv", a, hf, s)
                            filled(name)
                            nc.scalar.activation(pairs[s][0:m, 0, :], bank(name)[0:m], ACT.Identity,
                                                 bias=col16[0:m, cb + i:cb + i + 1]).then_inc(hi_ready, 1)
                            hn[0] += 1
                    elif step in ("values0", "values1"):
                        values(hf, int(step[-1]))
                    elif step == "s":
                        for pr in range(2):
                            act.wait_ge(smax_ready, 2 * (2 * a + hf) + pr + 1)
                            nc.scalar.activation(SM[:, pr], SM[:, pr], ACT.Exp).then_inc(exp_ready, 1)
                    elif step in ("pt", "ot"):
                        for pr in range(2):
                            if step == "pt":
                                name = (step, a, hf, pr)
                                filled(name)
                                d, v = PT[:, 0], bank(name).rearrange("p (t k n) -> p t k n", t=2, k=2)
                            else:
                                act.wait_ge(os_ready, 4 * (2 * a + hf) + 2 * pr + 2)
                                d, v = O_hi, OS[:, 2 * pr:2 * pr + 2]
                            nc.scalar.activation(d[:, 2 * pr:2 * pr + 2, 0], v[:, :, 0], ACT.Copy).then_inc(act_step, 1)
                            ast[0] += 1
                            nc.scalar.activation(d[0:CB, 2 * pr:2 * pr + 2, 1], v[0:CB, :, 1],
                                                 ACT.Copy).then_inc(hi_ready, 1)
                            hn[0] += 1
                    spare((step, hf))
            x_high("attn0", (2,))
            mp = [0]

            spare_pieces = {("qkv", 0): 3, ("st", 0): 4, ("pt", 0): 1, ("ot", 0): 1, ("st", 1): 2, ("pt", 1): 2,
                            ("ot", 1): 1}

            def moe_high(step):
                for _ in range(spare_pieces.get(step, 0)):
                    if mp[0] < NM:
                        if mp[0] in (0, N1):
                            act.wait_ge(loaded["moe"], 16 if mp[0] == 0 else 32)
                        high_part(*moe_pieces[mp[0]])
                        mp[0] += 1
            attention(0, {("st", 0): lambda: x_high("attn0", (3,)), ("pj", 1): lambda: x_high("moe", (0, 1))}, moe_high)
            lp = [0]

            def late_high():
                if lp[0] < NL:
                    if lp[0] == 0:
                        act.wait_ge(loaded["late"], 16)
                    if lp[0] == 2 * len(late_cuts):
                        act.wait_ge(loaded["full"], 16)
                    high_part(*late_pieces[lp[0]])
                    lp[0] += 1
            for u in range(UNITS):
                for n, c, slot in unit_chunks(u):
                    filled(("h", n))
                    if n >= 3:
                        act.wait_ge(hp_ready, n - 2)
                    b = col[:, C_B1 + c:C_B1 + c + 1]
                    nc.scalar.activation(ge[n % 3], bank(("h", n)), ACT.Gelu, bias=b,
                                         scale=1.0 / WS).then_inc(act_step, 1)
                    ast[0] += 1
                    if u >= 2:
                        filled(("y", u - 2, 1))
                    nc.scalar.activation(hgh[slot], bank(("h", n)), ACT.Gelu, bias=b,
                                         scale=1.0 / WS).then_inc(gelu_ready, 1)
                if u == 0:
                    x_high("moe", (2, 3))
                    act.wait_ge(gmax_ready, 1)
                    nc.scalar.activation(gat[:, 1], gat[:, 1], ACT.Exp).then_inc(exp_ready, 1)
                if u == 3:
                    for hf in range(2):
                        name = ("ct", hf)
                        filled(name)
                        nc.scalar.activation(ctT[:, HALF * hf:HALF * (hf + 1)], bank(name)[0:E],
                                             ACT.Copy).then_inc(ct_ready, 1)
                if u > 1:
                    late_high()
                    late_high()
                if u == UNITS - 1:
                    x_high_affine("mix1", (0, 1))
            while lp[0] < NL:
                late_high()
            def kvr(block):
                for i, n in enumerate("kvr"):
                    dst, fn, sc = ((rK, ACT.Copy, 1 / WS), (rV, ACT.Copy, 1 / WS), (rT, ACT.Tanh, 0.5 / WS))[i]
                    name = (n, block)
                    filled(name)
                    nc.scalar.activation(start(dst, block), bank(name), fn, scale=sc).then_inc(kvr_ready, 1)

            def decays(b):
                for i, (e1, e2) in enumerate(((start(E1f, b), start(E2f, b)), (start(E1b, b), start(E2b, b)))):
                    act.wait_ge(rd_ready, 2 * b + i + 1)
                    nc.scalar.activation(e2, e1, ACT.Relu).then_inc(act_step, 1)
                    ast[0] += 1
                    act.wait_ge(act_step, ast[0])
                    nc.scalar.activation(e1, e1, ACT.Relu, scale=-1.0).then_inc(act_step, 1)
                    nc.scalar.activation(e2, e2, ACT.Exp, scale=-1.0).then_inc(re_ready, 1)
                    ast[0] += 1
                    act.wait_ge(act_step, ast[0])
                    nc.scalar.activation(e1, e1, ACT.Exp, scale=-1.0).then_inc(re_ready, 1)

            def weights(b):
                act.wait_ge(mm_ready, b + 1)
                for e in (start(Mf, b), start(Mb, b, 1)):
                    nc.scalar.activation(e, e, ACT.Exp).then_inc(act_step, 1)
                    ast[0] += 1
                e = start(rK, b)
                nc.scalar.activation(e, e, ACT.Exp).then_inc(ew_ready, 1)

            def sy_high(b):
                act.wait_ge(sy_ready, 2 * b + 1)
                nc.scalar.activation(sy_hi[b], start(E1b, b), ACT.Copy).then_inc(hi_ready, 1)
                hn[0] += 1

            kvr(0)
            x_high_affine("mix1", (2, 3))
            kvr(1)
            for step, b in RECURRENCE_ORDER:
                if step == "maxima":
                    decays(b)
                    if b == 0:
                        kvr(2)
                elif step == "states":
                    weights(b)
                elif step == "outputs":
                    sy_high(b)
            x_high_affine("mix2", range(4))

            def ffn_high(hf):
                for m in range(6):
                    n = 6 * hf + m
                    filled(("kf", hf, m))
                    if n >= 2:
                        act.wait_ge(sq_ready, n - 1)
                    nc.scalar.activation(kfr[m % 2], bank(("kf", hf, m)), ACT.Relu, scale=1 / WS).then_inc(relu_ready, 1)
                    act.wait_ge(relu_ready, n + 1)
                    nc.scalar.activation(kfh[hf][:, m], kfr[m % 2], ACT.Square).then_inc(hi_ready, 1)
                    hn[0] += 1

            def receptance(hf):
                for pr in range(2):
                    name = ("r", hf, pr)
                    filled(name)
                    nc.scalar.activation(tr_[:, 2 * hf + pr], bank(name)[:, 0:2 * C], ACT.Tanh,
                                         scale=0.5 / WS).then_inc(tanh_ready, 1)
            ffn_high(0)
            receptance(0)
            ffn_high(1)
            receptance(1)
            def gate_exp(hf):
                act.wait_ge(gmax_ready, 2 + hf)
                ts = slice(4 * hf, 4 * hf + 4)
                nc.scalar.activation(gat[:, 1, ts], gat[:, 1, ts], ACT.Exp).then_inc(exp_ready, 1)

            def gated(hf):
                sl = slice(HALF * hf, HALF * (hf + 1))
                name = ("ce", hf)
                filled(name)
                nc.scalar.activation(ceF[:, sl], bank(name), ACT.Copy).then_inc(ce_ready, 1)
                nc.scalar.activation(cstack[0:E, sl], bank(name)[0:E], ACT.Copy).then_inc(act_step, 1)
                nc.scalar.activation(cstack[64:64 + E, sl], bank(name)[0:E], ACT.Copy).then_inc(hi_ready, 1)
                ast[0] += 1
                act.wait_ge(hw_ready, 2 * hf + 1)
                nc.scalar.activation(hw_hi[:, sl], hwF, ACT.Copy).then_inc(hi_ready, 1)
                hn[0] += 2
            x_high("attn1", (0, 1))
            gate_exp(0)
            gated(0)
            attention(1, {("st", 0): lambda: x_high("attn1", (2, 3)), ("values0", 0): lambda: gate_exp(1),
                          ("values1", 0): lambda: gated(1)})

        @block.vector
        def _(dve):
            V = nc.vector
            chain = [0]
            hn = [0]
            nn = [0]

            def link(ins):
                ins.then_inc(dve_step, 1)
                chain[0] += 1
                dve.wait_ge(dve_step, chain[0])

            def filled(name):
                dve.wait_ge(psum_filled, f.done[name])

            def released(name):
                dve.wait_ge(bank_free[f.bank[name]], f.release[name][1])

            deca = [col[:, c:c + 1] for c in (C_DECA, C_DECB, C_DECA)]
            fira = [col[:, c:c + 1] for c in (C_FIRA, C_FIRB, C_FIRA)]

            def next_high():
                hn[0] += 1
                dve.wait_ge(hi_ready, hn[0])

            dve.wait_ge(loaded["consts"], 16)
            wgt = K[:, K_BNW:K_BNW + 30]

            def tok_stats(t):
                dve.wait_ge(x_in[t % 3], 16 * (t // 3 + 1))
                a = 0
                for i, (n, _) in enumerate(GROUPS):
                    ins = V.bn_stats(stats[:, t % 2, 6 * i:6 * i + 6], tok_in[t % 3][:, a:a + n])
                    a += n
                link(ins)
                link(V.tensor_tensor(wstats[:, t % 2], stats[:, t % 2], wgt, ALU.mult))
                V.bn_aggr(mv[:, t], wstats[:, t % 2]).then_inc(var_ready, 1)
                nn[0] += 1

            def tok_low(t):
                for i in range(2):
                    name = ("tokT", t, i)
                    next_high()
                    b = bank(name).rearrange("p (k n) -> p k n", k=4)
                    if i == 0:
                        V.tensor_tensor(tx_lo[t % 2][:, 0:4, :], b, tx_hi[t % 2][:, 0:4, :],
                                        ALU.subtract).then_inc(bank_free[f.bank[name]], 1)
                    else:
                        V.tensor_tensor(tx_lo[t % 2][:, 4:7, :], b[:, 0:3], tx_hi[t % 2][:, 4:7, :], ALU.subtract)
                        V.tensor_tensor(tx_hi[t % 2][64:P, 7, :], b[64:P, 3], tx_hi[t % 2][64:P, 7, :],
                                        ALU.subtract).then_inc(tokx_ready, 1)

            def tok_out(t):
                name = ("tok", t)
                filled(name)
                V.scalar_tensor_tensor(H[:, t], bank(name)[:, 0:C], 1.0 / WS, tokb[:], ALU.mult,
                                       ALU.add).then_inc(bank_free[f.bank[name]], 1)
                dve.wait_ge(bank_free[f.bank[name]], f.release[name][1])

            tok_stats(0)
            dve.wait_ge(loaded["tokg"], 32)
            for k in range(3):
                dve.wait_ge(tokw_in[k], 16)
                for s in range(5):
                    g = gbt[:, 5 * k + s:5 * k + s + 1]
                    if s == 0:
                        ins = V.tensor_scalar(wf[:, k], raw_w[:, k, 0], g, None, ALU.mult)
                    else:
                        ins = V.scalar_tensor_tensor(wf[:, k], raw_w[:, k, s], g, wf[:, k], ALU.mult, ALU.add)
                    if s < 4:
                        link(ins)
            ins.then_inc(tokw_ready, 1)
            tok_stats(1)
            tok_stats(2)
            dve.wait_ge(tokw_ready, 2)
            V.scalar_tensor_tensor(wt_lo[:], wf[:], WS, wt_hi[:], ALU.mult, ALU.subtract).then_inc(tokw_ready, 1)

            def ln_stats(t, src):
                link(V.bn_stats(stats[:, t % 2, 0:6], src[:, t]))
                V.bn_aggr(mv[:, t], stats[:, t % 2, 0:6]).then_inc(var_ready, 1)
                nn[0] += 1
                return nn[0]

            def ln_norm(t, src, n, k):
                dve.wait_ge(rstd_ready, n)
                if k >= 4:
                    dve.wait_ge(psum_filled, x_fill(k - 4))
                V.tensor_scalar(xn[:, t % 4, 0:C], src[:, t], mv[:, t, 0:1], rstd[:, t:t + 1], ALU.subtract,
                                ALU.mult).then_inc(dve_step, 1)
                chain[0] += 1
                V.tensor_scalar(xn[:, t % 4, C:2 * P], src[:, t, P:C], mv[:, t, 0:1], rstd[:, t:t + 1], ALU.subtract,
                                ALU.mult).then_inc(xn_ready, 1)

            def x_fill(k):
                return f.done[("x", PHASES[k // NT], k % NT // 2)]

            xc = [0]

            def norm_tiles(src, ready=None, tiles=range(NT)):
                last = None
                for t in range(tiles[0], tiles[-1] + 2):
                    if t in tiles:
                        if ready:
                            ready(t)
                        now = ln_stats(t, src)
                    if last:
                        ln_norm(t - 1, src, last, xc[0])
                        xc[0] += 1
                    last = now

            def norm_twice(hf, k):
                if k >= 2:
                    ln_norm(4 * hf + k - 2, Z, second[k - 2], xc[0])
                    xc[0] += 1
                if 1 <= k < 5:
                    t = 4 * hf + k - 1
                    dve.wait_ge(rstd_ready, first[k - 1])
                    link(V.tensor_scalar(Z[:, t], H[:, t], mv[:, t, 0:1], rstd[:, t:t + 1], ALU.subtract, ALU.mult))
                    second[k - 1] = ln_stats(t, Z)
                if k < 4:
                    first[k] = ln_stats(4 * hf + k, H)
            first, second = {}, {}

            def x_low(phase, pairs_=range(4)):
                for pr in pairs_:
                    name = ("x", phase, pr)
                    next_high()
                    b = bank(name).rearrange("p (t k n) -> p t k n", t=2, k=2)
                    V.tensor_tensor(X_lo[:, 2 * pr:2 * pr + 2], b[:, :, 0], X_hi[:, 2 * pr:2 * pr + 2, 0], ALU.subtract)
                    V.tensor_tensor(X_hi[64:P, 2 * pr:2 * pr + 2, 1], b[64:P, :, 1], X_hi[64:P, 2 * pr:2 * pr + 2, 1],
                                    ALU.subtract).then_inc(x_ready, 1)

            def x_affine(phase, pairs_):
                wa, wb, ba, bb = {"mix1": (C_LN1WA, C_LN1WB, C_LN1BA, C_LN1BB),
                                  "mix2": (C_LN2WA, C_LN2WB, C_LN2BA, C_LN2BB)}[phase]
                for pr in pairs_:
                    name = ("x", phase, pr)
                    filled(name)
                    b = bank(name).rearrange("p (t k n) -> p t k n", t=2, k=2)
                    V.tensor_scalar(xt_f[phase][:, pr, :, 0], b[:, :, 0], col[:, wa:wa + 1], col[:, ba:ba + 1],
                                    ALU.mult, ALU.add).then_inc(dve_step, 1)
                    chain[0] += 1
                    V.tensor_scalar(xt_f[phase][:, pr, :, 1], b[:, :, 1], col[:, wb:wb + 1], col[:, bb:bb + 1],
                                    ALU.mult, ALU.add).then_inc(xf_ready, 1)

            def x_affine_low(phase, pairs_):
                for pr in pairs_:
                    next_high()
                    x = xt_f[phase]
                    V.tensor_tensor(X_lo[:, 2 * pr:2 * pr + 2], x[:, pr, :, 0], X_hi[:, 2 * pr:2 * pr + 2, 0],
                                    ALU.subtract)
                    V.tensor_tensor(X_hi[64:P, 2 * pr:2 * pr + 2, 1], x[64:P, pr, :, 1],
                                    X_hi[64:P, 2 * pr:2 * pr + 2, 1], ALU.subtract).then_inc(x_ready, 1)

            def attention(a, after_pair):
                cb = C_QB0 if a == 0 else C_QB1

                def low(hf, i):
                    s, o, m = SLOTS[i]
                    name = ("qkv", a, hf, s)
                    next_high()
                    V.scalar_tensor_tensor(pairs[s][0:m, 1, :], bank(name)[0:m], col16[0:m, cb + i:cb + i + 1],
                                           pairs[s][0:m, 0, :], ALU.add, ALU.subtract).then_inc(qkv_ready, 1)

                def spread(hf, i):
                    dst, src, nh, mask = ((KAbd, "KA", HA, K_HM), (VAbd, "VA", HA, K_HM), (KVBbd, "KVB", HB, K_HMB))[i - 1]
                    dve.wait_ge(qkv_ready, 5 * (2 * a + hf) + i + 1)
                    v = dst.rearrange("p l s (h j) -> p l s h j", h=nh)
                    w = pairs[src].rearrange("p l (s j) -> p l s j", j=SEQ)
                    for h in range(nh):
                        ins = V.tensor_scalar(v[:, :, :, h], w, K[:, mask + h:mask + h + 1], None, ALU.mult)
                    ins.then_inc(bd_ready, 1)

                def softmax_in(hf, pr):
                    name = ("s", a, hf, pr)
                    filled(name)
                    s = bank(name)[:, 0:2 * C].rearrange("p (h j) -> p h j", j=SEQ)
                    sc = HD ** -0.5 / (WS * WS)
                    if a == 0:
                        am = K[:, K_AM:K_AM + SEQ][:, None, :].broadcast_to([P, 2 * NH, SEQ])
                        V.scalar_tensor_tensor(SM[:, pr], s, sc, am, ALU.mult, ALU.add).then_inc(
                            bank_free[f.bank[name]], 1)
                    else:
                        V.tensor_scalar(SM[:, pr], s, sc, None, ALU.mult).then_inc(bank_free[f.bank[name]], 1)
                    released(name)
                    link(V.tensor_reduce(smx[:, pr, 0], SM[:, pr], AX, ALU.max))
                    V.tensor_tensor(SM[:, pr], SM[:, pr], smx[:, pr, 0][:, :, None].broadcast_to([P, 2 * NH, SEQ]),
                                    ALU.subtract).then_inc(smax_ready, 1)

                def softmax_out(pr):
                    dve.wait_ge(exp_ready, en[0] + 1)
                    en[0] += 1
                    link(V.tensor_reduce(smx[:, pr, 1], SM[:, pr], AX, ALU.add))
                    link(V.reciprocal(smx[:, pr, 2], smx[:, pr, 1]))
                    V.tensor_tensor(SM[:, pr], SM[:, pr], smx[:, pr, 2][:, :, None].broadcast_to([P, 2 * NH, SEQ]),
                                    ALU.mult).then_inc(p_ready, 1)

                def values(hf, hl):
                    for g in (0, 2):
                        name = ("va", a, hf, hl, g)
                        filled(name)
                        V.tensor_copy(VA[:, hl, 8 * g:8 * g + 8, :],
                                      bank(name).bitcast(F16).rearrange("p (s n) -> p s n", s=8)).then_inc(v_dve_ready, 1)

                def two_columns(dst, src):
                    return V.tensor_reduce(dst, src.rearrange("p (l n) -> p n l", l=2), AX, ALU.add)

                def scores_sum(hf):
                    if 2 * a + hf:
                        dve.wait_ge(ot_ready, 2 * (2 * a + hf))
                    for i in range(4):
                        name = ("st", a, hf, i)
                        filled(name)
                        b = bank(name)
                        two_columns(ST[:, i // 2, i % 2, 0], b[:, 0:2 * P])
                        two_columns(ST[0:CB, i // 2, i % 2, 1], b[0:CB, 2 * P:4 * P]).then_inc(st_ready, 1)

                def probabilities_low(hf):
                    for pr in range(2):
                        name = ("pt", a, hf, pr)
                        next_high()
                        v = bank(name).rearrange("p (t k n) -> p t k n", t=2, k=2)
                        sl = slice(2 * pr, 2 * pr + 2)
                        V.tensor_tensor(PT[:, 1, sl, 0], v[:, :, 0], PT[:, 0, sl, 0], ALU.subtract)
                        V.tensor_tensor(PT[0:CB, 1, sl, 1], v[0:CB, :, 1], PT[0:CB, 0, sl, 1],
                                        ALU.subtract).then_inc(pt_ready, 1)

                def outputs_low(hf):
                    for i in range(4):
                        name = ("ot", a, hf, i)
                        filled(name)
                        b = bank(name)
                        two_columns(OS[:, i, 0], b[:, 0:2 * P])
                        two_columns(OS[0:CB, i, 1], b[0:CB, 2 * P:4 * P]).then_inc(os_ready, 1)
                    for pr in range(2):
                        next_high()
                        sl = slice(2 * pr, 2 * pr + 2)
                        V.tensor_tensor(O_lo[:, sl], OS[:, sl, 0], O_hi[:, sl, 0], ALU.subtract)
                        V.tensor_tensor(O_hi[64:P, sl, 1], OS[0:CB, sl, 1], O_hi[0:CB, sl, 1],
                                        ALU.subtract).then_inc(ot_ready, 1)

                def project(hf):
                    for pr in range(2):
                        name = ("pj", a, hf, pr)
                        filled(name)
                        t = 4 * hf + 2 * pr
                        V.scalar_tensor_tensor(H[:, t:t + 2],
                                               bank(name)[:, 0:2 * C].rearrange("p (t n) -> p t n", t=2),
                                               1.0 / (WS * WS), H[:, t:t + 2], ALU.mult,
                                               ALU.add).then_inc(bank_free[f.bank[name]], 1)
                        released(name)
                        after_pair(2 * hf + pr)

                def probabilities(hf, between=lambda: None):
                    values(hf, 0)
                    softmax_in(hf, 0)
                    softmax_in(hf, 1)
                    between()
                    values(hf, 1)
                    softmax_out(0)
                    softmax_out(1)

                def operands(hf, between=lambda: None):
                    low(hf, 0)
                    low(hf, 1)
                    spread(hf, 1)
                    low(hf, 2)
                    low(hf, 3)
                    spread(hf, 3)
                    low(hf, 4)
                    between()
                    spread(hf, 2)

                if a == 0:
                    operands(0, lambda: x_low("attn0", (3,)))
                    scores_sum(0)
                    probabilities(0)
                else:
                    norm_tiles(H, tiles=range(4, 8))
                    operands(0, lambda: x_low("attn1", (2, 3)))
                    gates_by_rank(1)
                    scores_sum(0)
                    probabilities(0, lambda: gated(1))
                for i in range(5):
                    low(1, i)
                probabilities_low(0)
                spread(1, 1)
                spread(1, 3)
                outputs_low(0)
                spread(1, 2)
                scores_sum(1)
                project(0)
                probabilities(1)
                probabilities_low(1)
                if a == 0:
                    norm_tiles(H, tiles=range(0, 4))
                outputs_low(1)
                if a == 0:
                    x_low("moe", (0, 1))
                project(1)
            en = [0]

            def gate_logits(name, tiles):
                nt = tiles.stop - tiles.start
                filled(name)
                lg = bank(name)[:, 0:nt * E].rearrange("p (t e) -> p t e", t=nt)
                g = gat[:, :, tiles]
                V.tensor_scalar(g[:, 0], lg, 1.0 / WS, None, ALU.mult).then_inc(bank_free[f.bank[name]], 1)
                released(name)
                small = [P, nt, E]
                link(V.tensor_reduce(gsum[:, 0, tiles], g[:, 0], AX, ALU.max))
                V.tensor_tensor(g[:, 1], g[:, 0], gsum[:, 0, tiles][:, :, None].broadcast_to(small),
                                ALU.subtract).then_inc(gmax_ready, 1)

            def gates(tiles, twice):
                nt = tiles.stop - tiles.start
                small = [P, nt, E]
                g = gat[:, :, tiles]
                dve.wait_ge(exp_ready, en[0] + 1)
                en[0] += 1
                link(V.tensor_reduce(gsum[:, 1, tiles], g[:, 1], AX, ALU.add))
                link(V.reciprocal(gsum[:, 2, tiles], gsum[:, 1, tiles]))
                link(V.tensor_tensor(g[:, 2], g[:, 1], gsum[:, 2, tiles][:, :, None].broadcast_to(small), ALU.mult))
                full4 = [P, nt, E, E]
                of = g[:, 2][:, :, None, :].broadcast_to(full4)
                oe = g[:, 2][:, :, :, None].broadcast_to(full4)
                tri = K[:, K_TRI:K_TRI + E * E].rearrange("p (e f) -> p e f", e=E)[:, None].broadcast_to(full4)
                equal, greater = ranks[twice][:, 0, tiles], ranks[twice][:, 1, tiles]
                V.tensor_tensor(greater, of, oe, ALU.is_gt)
                link(V.tensor_tensor(equal, of, oe, ALU.is_equal))
                link(V.tensor_tensor(equal, equal, tri, ALU.mult))
                link(V.tensor_tensor(equal, equal, greater, ALU.add))
                link(V.tensor_reduce(g[:, 3], equal, AX, ALU.add))
                link(V.scalar_tensor_tensor(g[:, 4], g[:, 3], 1.5, g[:, 2], ALU.is_lt, ALU.mult))
                if twice:
                    link(V.tensor_scalar(g[:, 5], g[:, 4], 2.0, None, ALU.mult))

            seen = {}
            for t in range(NT):
                if t in (5, 7):
                    x_low("attn0", (t // 2 - 2,))
                tok_low(t)
                if t + 3 < NT:
                    tok_stats(t + 3)
                if t == 0:
                    filled("beta")
                    dve.wait_ge(loaded["cols"], 48)
                    V.tensor_tensor(tokb[:], tokb[:], bank("beta")[:, 0:C], ALU.add).then_inc(bank_free[f.bank["beta"]], 1)
                    released("beta")
                if t == 2:
                    dve.wait_ge(cols_ready, 6)
                    for a, b, s in ((R_OUT, C, WS * WS), (R_RT, E, WS), (R_PJ, C, WS * WS), (R_GT, E, WS)):
                        V.scalar_tensor_tensor(rowl[:, a:a + b], rowr[:, a:a + b], s, rowh[:, a:a + b], ALU.mult,
                                               ALU.subtract).then_inc(cols_ready, 1)
                if t >= 1:
                    tok_out(t - 1)
                    seen[t - 1] = ln_stats(t - 1, H)
                if t >= 2:
                    ln_norm(t - 2, H, seen[t - 2], t - 2)
            tok_out(NT - 1)
            seen[NT - 1] = ln_stats(NT - 1, H)
            ln_norm(NT - 2, H, seen[NT - 2], NT - 2)
            x_low("attn0", (2,))
            ln_norm(NT - 1, H, seen[NT - 1], NT - 1)
            xc[0] = NT
            attention(0, lambda pr: None)
            norm_tiles(H, tiles=range(4, 8))
            x_low("moe", (2, 3))
            dve.wait_ge(loaded["b2"], 16)
            link(V.tensor_scalar(b2s[:], b2s[:], WS, None, ALU.mult))
            gate_logits("router0", slice(0, NT))
            for u in range(UNITS + 1):
                if u == UNITS:
                    x_affine_low("mix1", (0, 1))
                if u < UNITS:
                    for n, _, slot in unit_chunks(u):
                        dve.wait_ge(gelu_ready, n + 1)
                        V.tensor_tensor(hgl[slot], ge[n % 3], hgh[slot], ALU.subtract).then_inc(hp_ready, 1)
                if u == 1:
                    gates(slice(0, NT), False)
                    V.tensor_scalar(gat[:, 5], gat[:, 4], 1.0 / WS, None, ALU.mult).then_inc(gate_ready, 1)
                    dve.wait_ge(gate_ready, 1)
                if u:
                    hf, e = divmod(u - 1, E)
                    for pr in range(2):
                        name = ("y", u - 1, pr)
                        filled(name)
                        if e:
                            released(("y", u - 2, pr))
                        for j in range(2):
                            t = 4 * hf + 2 * pr + j
                            ins = V.scalar_tensor_tensor(H[:, t], bank(name)[:, C * j:C * j + C], gat[:, 5, t, e:e + 1],
                                                         H[:, t], ALU.mult, ALU.add)
                        ins.then_inc(bank_free[f.bank[name]], 1)
                    if e == E - 1:
                        for pr in range(2):
                            name = ("b2", 2 * hf + pr)
                            filled(name)
                            released(("y", u - 1, pr))
                            t = 4 * hf + 2 * pr
                            V.scalar_tensor_tensor(H[:, t:t + 2],
                                                   bank(name)[:, 0:2 * C].rearrange("p (t n) -> p t n", t=2), 1.0 / WS,
                                                   H[:, t:t + 2], ALU.mult, ALU.add).then_inc(bank_free[f.bank[name]], 1)
                            released(name)
                if u == E:
                    link(V.tensor_scalar(col[:, C_DECA:C_FIRB + 1], col[:, C_DECA:C_FIRB + 1], 1.0 / SEQ, None, ALU.mult))
                    link(V.memset(rW0[:], 0.0))
                    for b in range(3):
                        w = start(rW0, b)
                        link(V.tensor_scalar(w, w, deca[b], None, ALU.add))
                        link(V.memset(w[:, ::SEQ], -BIG))
                if E < u < E + 7:
                    norm_twice(0, u - E - 1)
                if u == UNITS - 1:
                    x_affine("mix1", (0, 1))
            norm_twice(1, 0)
            norm_twice(1, 1)
            norm_twice(1, 2)
            norm_twice(1, 3)
            norm_twice(1, 4)
            norm_twice(1, 5)
            x_affine("mix1", (2, 3))
            x_affine_low("mix1", (2, 3))

            def scan(dst, d0, d1, back, op0, op1):
                if back:
                    link(V.tensor_tensor_scan(dst[:, 0:HALF][:, ::-1], d0, d1[:, ::-1], 0.0, op0, op1))
                else:
                    link(V.tensor_tensor_scan(dst[:, 1:BW], d0, d1, 0.0, op0, op1))

            def block(buf, b):
                return buf[:, BW * b:BW * b + BW]

            def maxima(b):
                dve.wait_ge(kvr_ready, 3 * b + 1)
                k = start(rK, b)
                for i, (M, D) in enumerate(((Mf, E1f), (Mb, E1b))):
                    scan(block(M, b), start(rW0, b), k, i, ALU.add, ALU.max)
                    link(V.memset(block(M, b)[:, ::SEQ], -BIG))
                    V.scalar_tensor_tensor(start(D, b), start(M, b, i), deca[b], k, ALU.add,
                                           ALU.subtract).then_inc(rd_ready, 1)
                m = start(rW0, b)
                link(V.tensor_tensor(m, start(Mf, b), start(Mb, b, 1), ALU.max))
                link(V.scalar_tensor_tensor(m, k, fira[b], m, ALU.add, ALU.max))
                dve.wait_ge(rd_ready, 2 * b + 2)
                V.scalar_tensor_tensor(k, k, fira[b], m, ALU.add, ALU.subtract).then_inc(M_ready, 1)

            def states(b):
                dve.wait_ge(kvr_ready, 3 * b + 2)
                dve.wait_ge(re_ready, 4 * b + 2)
                e1, e2 = start(E1f, b), start(E2f, b)
                scan(block(Bf, b), e1, e2, 0, ALU.mult, ALU.add)
                link(V.tensor_tensor(e2, e2, start(rV, b), ALU.mult))
                scan(block(Af, b), e1, e2, 0, ALU.mult, ALU.add)
                dve.wait_ge(re_ready, 4 * b + 4)
                e1, e2 = start(E1b, b)[:, ::-1], start(E2b, b)
                scan(block(Bb, b), e1, e2, 1, ALU.mult, ALU.add)
                dve.wait_ge(ev_ready, b + 1)
                scan(block(Ab, b), e1, EV[:, HALF * b:HALF * b + HALF], 1, ALU.mult, ALU.add)
                for A in (Af, Ab, Bf, Bb):
                    ins = V.memset(block(A, b)[:, ::SEQ], 0.0)
                ins.then_inc(state_ready, 1)

            def sums(b):
                dve.wait_ge(ew_ready, b + 1)
                dve.wait_ge(state_ready, b + 1)
                n = start(Af, b)
                v = start(rV, b)
                V.tensor_tensor(n, n, start(Mf, b), ALU.mult)
                link(V.tensor_tensor(v, v, start(rK, b), ALU.mult))
                link(V.tensor_tensor(n, n, v, ALU.add))
                dve.wait_ge(num_ready, b + 1)
                link(V.tensor_tensor(n, n, start(Ab, b, 1), ALU.add))
                dve.wait_ge(kvr_ready, 3 * b + 3)
                link(V.scalar_tensor_tensor(n, start(rT, b), 1.0, n, ALU.add, ALU.mult))

            def outputs(b):
                dve.wait_ge(den_ready, b + 1)
                link(V.reciprocal(start(E2b, b), start(Bf, b)))
                V.tensor_tensor(start(E1b, b), start(Af, b), start(E2b, b), ALU.mult).then_inc(sy_ready, 1)
                next_high()
                V.tensor_tensor(sy_lo[b], start(E1b, b), sy_hi[b], ALU.subtract).then_inc(sy_ready, 1)

            for step, b in RECURRENCE_ORDER:
                {"maxima": maxima, "states": states, "sums": sums, "outputs": outputs}[step](b)

            def wo_out(t):
                if t % 2 == 0:
                    name = ("wo", t // 2)
                    filled(name)
                    V.scalar_tensor_tensor(Z[:, t:t + 2], bank(name)[:, 0:2 * C].rearrange("p (t n) -> p t n", t=2),
                                           0.5 / WS, Z[:, t:t + 2], ALU.mult, ALU.add).then_inc(
                                               bank_free[f.bank[name]], 1)
                    released(name)
            norm_tiles(Z, wo_out, range(0, 4))
            x_affine("mix2", (0, 1))
            x_affine_low("mix2", (0, 1))
            norm_tiles(Z, wo_out, range(4, 8))
            x_affine("mix2", (2, 3))
            x_affine_low("mix2", (2, 3))

            def ffn_low(hf):
                for m in range(6):
                    n = 6 * hf + m
                    dve.wait_ge(relu_ready, n + 1)
                    if n >= 2:
                        dve.wait_ge(kf_ready, n - 1)
                    V.tensor_tensor(kfs[m % 2], kfr[m % 2], kfr[m % 2], ALU.mult).then_inc(sq_ready, 1)
                    dve.wait_ge(sq_ready, n + 1)
                    next_high()
                    V.tensor_tensor(kfl[hf][:, m], kfs[m % 2], kfh[hf][:, m], ALU.subtract).then_inc(kf_ready, 1)

            def ffn_out(hf):
                for pr in range(2):
                    name = ("kv", hf, pr)
                    t = 4 * hf + 2 * pr
                    filled(name)
                    dve.wait_ge(tanh_ready, 2 * hf + pr + 1)
                    V.scalar_tensor_tensor(uu[:, pr], tr_[:, 2 * hf + pr], 1.0, bank(name)[:, 0:2 * C], ALU.add,
                                           ALU.mult).then_inc(bank_free[f.bank[name]], 1)
                    released(name)
                    u = uu[:, pr].rearrange("p (t n) -> p t n", t=2)
                    link(V.scalar_tensor_tensor(Z[:, t:t + 2], u, 0.5 / WS, Z[:, t:t + 2], ALU.mult, ALU.add))
                    link(V.tensor_tensor(H[:, t:t + 2], H[:, t:t + 2], Z[:, t:t + 2], ALU.add))
            ffn_low(0)
            ffn_low(1)
            ffn_out(0)
            norm_tiles(H, tiles=range(0, 4))
            ffn_out(1)
            link(V.memset(cstack[0:96, :], 0.0))

            def gates_by_rank(hf):
                tiles = slice(4 * hf, 4 * hf + 4)
                gate_logits(("router1", hf), tiles)
                gates(tiles, True)
                V.tensor_copy(crep1[:, tiles].rearrange("p t (r e) -> p t r e", e=E),
                              gat[:, 5, tiles][:, :, None, :].broadcast_to([P, 4, 16, E])).then_inc(gate_ready, 1)

            def gated(hf):
                sl = slice(HALF * hf, HALF * (hf + 1))
                name = ("ce", hf)
                next_high()
                V.tensor_tensor(cstack[32:32 + E, sl], bank(name)[0:E], cstack[0:E, sl],
                                ALU.subtract).then_inc(bank_free[f.bank[name]], 1)
                name = ("la", hf)
                filled(name)
                dve.wait_ge(ce_ready, hf + 1)
                if hf:
                    dve.wait_ge(hw_ready, 2)
                V.scalar_tensor_tensor(hwF, bank(name), col16[:, C_BA:C_BA + 1], ceF[:, sl], ALU.add,
                                       ALU.mult).then_inc(hw_ready, 1)
                next_high()
                V.tensor_tensor(hw_lo[:, sl], hwF, hw_hi[:, sl], ALU.subtract).then_inc(hw_ready, 1)

            x_low("attn1", (0, 1))
            gates_by_rank(0)
            gated(0)
            attention(1, lambda pr: dve.sem_inc(h_ready, 1))

        @block.tensor
        def _(pe):
            T_ = nc.tensor

            def free(name):
                if f.before[name]:
                    by, count = f.release[f.before[name]]
                    pe.wait_ge(readers[by], count)

            def mm(o, w, x, start, stop):
                return T_.matmul(o, w, x, start=start, stop=stop, skip_group_check=True)

            ident = K[:, K_ID:K_ID + P]

            pe.wait_ge(loaded["consts"], 16)
            pe.wait_ge(loaded["tokg"], 32)

            def beta(chunks):
                b = bank("beta")[:, 0:C]
                for k in chunks:
                    pe.wait_ge(tokw_in[min(k, 6)], 16)
                    for s in range(5 if k < 6 else 1):
                        w = raw_w[:, k, s] if k < 6 else raw_wh[:, k - 6]
                        c = 32 + (5 * k + s if k < 6 else 24 + k)
                        last = mm(b, gbt[:, c:c + 1].broadcast_to([P, P]), w, (k, s) == (3, 0), k == 7)
                return last

            def tok_turn(t):
                pe.wait_ge(tokn_ready, t + 1)
                for i in range(2):
                    name = ("tokT", t, i)
                    free(name)
                    for k in range(4):
                        j = 4 * i + k
                        last = T_.transpose(bank(name)[:, P * k:P * k + P], tx_n[t % 2][:, P * j:P * j + P], ident)
                    last.then_inc(psum_filled, 1)

            def tok_product(t):
                name = ("tok", t)
                pe.wait_ge(tokx_ready, t + 1)
                if t == 0:
                    pe.wait_ge(tokw_ready, 3)
                free(name)
                o = bank(name)[:, 0:C]
                hi, lo = tx_hi[t % 2], tx_lo[t % 2]
                for k in range(7):
                    mm(o, hi[:, k], wt_hi[:, k], k == 0, False)
                    mm(o, lo[:, k], wt_hi[:, k], False, False)
                    mm(o, hi[:, k], wt_lo[:, k], False, False)
                mm(o, hi[:, 7], wt_hi[:, 7], False, False)
                mm(o, hi[0:64, 7], wt_lo[0:64, 7], False, True).then_inc(psum_filled, 1)

            xc = [0]

            def turn(phase, pairs_=range(4)):
                for pr in pairs_:
                    name = ("x", phase, pr)
                    free(name)
                    for j in range(2):
                        xc[0] += 1
                        pe.wait_ge(xn_ready, xc[0])
                        t = 2 * pr + j
                        for k in range(2):
                            last = T_.transpose(bank(name)[:, 256 * j + P * k:256 * j + P * k + P],
                                                xn[:, t % 4, P * k:P * k + P], ident)
                    last.then_inc(psum_filled, 1)

            def by_rows(o, wa, wb, col0, m, hf, more=()):
                xa, xb = X_hi[:, 4 * hf:4 * hf + 4, 0], X_hi[:, 4 * hf:4 * hf + 4, 1]
                xl = X_lo[:, 4 * hf:4 * hf + 4]
                s = slice(col0, col0 + m)
                mm(o, wa[:, 0, s], xa, True, False)
                mm(o, wa[:, 0, s], xl, False, False)
                mm(o, wa[:, 1, s], xa, False, False)
                mm(o, wb[:, 0, s], xb, False, False)
                for w, x in more:
                    mm(o, w, x, False, False)
                return mm(o, wb[0:64, 1, s], xb[0:64], False, True)

            def by_tokens(o, ah, al, b, wa, wb, s, bias=None, start=True):
                mm(o, ah, wa[:, 0, s], start, False)
                mm(o, al, wa[:, 0, s], False, False)
                mm(o, ah, wa[:, 1, s], False, False)
                mm(o, b, wb[:, 0, s], False, False)
                if bias is not None:
                    mm(o, ones[:], rowh[:, bias:bias + (s.stop - s.start)], False, False)
                    mm(o, ones[:], rowl[:, bias:bias + (s.stop - s.start)], False, False)
                return mm(o, b[0:64], wb[0:64, 1, s], False, True)

            def attention(a, x_pairs, before):
                wa, wb = (early_a, early_b) if a == 0 else (late_a, late_b)

                def qkv(hf):
                    c0 = 0 if a == 0 else LATE["qkv1"]
                    if x_pairs:
                        pe.wait_ge(x_ready, x_pairs + 2 * hf)
                    for i, (s, o, m) in enumerate(SLOTS):
                        name = ("qkv", a, hf, s)
                        free(name)
                        more = ()
                        if a == 1:
                            pe.wait_ge(hw_ready, 2 * hf + 2)
                            sl = slice(HALF * hf, HALF * (hf + 1))
                            bh, bl = fullp[:, 0, FW + o:FW + o + m], fullp[:, 1, FW + o:FW + o + m]
                            bb = fullp[0:72, 0, FW + 576 + o:FW + 576 + o + m]
                            more = ((bh, hw_hi[:, sl]), (bh, hw_lo[:, sl]), (bl, hw_hi[:, sl]), (bb, cstack[0:72, sl]))
                        by_rows(bank(name)[0:m], wa, wb, c0 + o, m, hf, more).then_inc(psum_filled, 1)

                def scores(hf):
                    n0 = 2 * a + hf
                    pe.wait_ge(bd_ready, 3 * n0 + 2)
                    pe.wait_ge(qkv_ready, 5 * n0 + 5)
                    qa, qb = pairs["QA"], pairs["QB"]
                    for t in range(4):
                        name = ("st", a, hf, t)
                        free(name)
                        oa, ob = (bank(name)[:, 2 * P * k:2 * P * (k + 1)].rearrange("p (l n) -> p l n", l=2) for k in range(2))
                        for s in range(8):
                            g = 8 * t + s
                            q, o = slice(16 * g, 16 * g + 16), slice(16 * s, 16 * s + 16)
                            mm(oa[:, :, o], KAbd[:, 0, g], qa[:, :, q], True, False)
                            mm(oa[:, 0, o], KAbd[:, 1, g], qa[:, 0, q], False, True)
                            mm(ob[0:CB, :, o], KVBbd[0:CB, 0, g], qb[0:CB, :, q], True, False)
                            last = mm(ob[0:CB, 0, o], KVBbd[0:CB, 1, g], qb[0:CB, 0, q], False, True)
                        last.then_inc(psum_filled, 1)

                def values(hf, hl):
                    pe.wait_ge(bd_ready, 3 * (2 * a + hf) + 3)
                    for g in range(4):
                        name = ("va", a, hf, hl, g)
                        free(name)
                        o = bank(name).bitcast(F16)
                        for s in range(8):
                            last = T_.transpose(o[:, P * s:P * s + P], VAbd[:, hl, 8 * g + s], id16[:])
                        last.then_inc(psum_filled, 1)
                    for g in range(2):
                        name = ("vb", a, hf, hl, g)
                        free(name)
                        o = bank(name)[0:CB].bitcast(F16)
                        for s in range(16):
                            last = T_.transpose(o[:, CB * s:CB * s + CB], KVBbd[64:P, hl, 16 * g + s], id16[64:P, 64:P])
                        last.then_inc(psum_filled, 1)

                def turn_scores(hf):
                    for pr in range(2):
                        name = ("s", a, hf, pr)
                        free(name)
                        pe.wait_ge(st_ready, 4 * (2 * a + hf) + 2 * pr + 2)
                        for j in range(2):
                            T_.transpose(bank(name)[:, C * j:C * j + P], ST[:, pr, j, 0], ident)
                            last = T_.transpose(bank(name)[:, C * j + P:C * j + C], ST[0:CB, pr, j, 1],
                                                ident[0:CB, 0:CB])
                        last.then_inc(psum_filled, 1)

                def turn_probabilities(hf):
                    for pr in range(2):
                        name = ("pt", a, hf, pr)
                        free(name)
                        pe.wait_ge(p_ready, 2 * (2 * a + hf) + pr + 1)
                        sm = SM[:, pr].rearrange("p h j -> p (h j)")
                        for j in range(2):
                            T_.transpose(bank(name)[:, 256 * j:256 * j + P], sm[:, C * j:C * j + P], ident)
                            last = T_.transpose(bank(name)[0:CB, 256 * j + P:256 * j + 2 * P],
                                                sm[:, C * j + P:C * j + C], ident)
                        last.then_inc(psum_filled, 1)

                def outputs(hf):
                    n0 = 2 * a + hf
                    pe.wait_ge(v_act_ready, 8 * (n0 + 1))
                    pe.wait_ge(v_dve_ready, 4 * (n0 + 1))
                    for t in range(4):
                        name = ("ot", a, hf, t)
                        free(name)
                        pe.wait_ge(pt_ready, 2 * n0 + t // 2 + 1)
                        oa, ob = (bank(name)[:, 2 * P * k:2 * P * (k + 1)].rearrange("p (l n) -> p l n", l=2) for k in range(2))
                        for s in range(8):
                            g = 8 * t + s
                            q = o = slice(16 * s, 16 * s + 16)
                            mm(oa[:, :, o], VA[:, 0, g], PT[:, :, t, 0, q], True, False)
                            mm(oa[:, 0, o], VA[:, 1, g], PT[:, 0, t, 0, q], False, True)
                            mm(ob[0:CB, :, o], VB[0:CB, 0, g], PT[0:CB, :, t, 1, q], True, False)
                            last = mm(ob[0:CB, 0, o], VB[0:CB, 1, g], PT[0:CB, 0, t, 1, q], False, True)
                        last.then_inc(psum_filled, 1)

                def project(hf):
                    c1 = EARLY["out0"] if a == 0 else LATE["proj"]
                    for pr in range(2):
                        name = ("pj", a, hf, pr)
                        free(name)
                        pe.wait_ge(ot_ready, 2 * (2 * a + hf) + pr + 1)
                        for j in range(2):
                            t = 2 * pr + j
                            last = by_tokens(bank(name)[:, C * j:C * j + C], O_hi[:, t, 0], O_lo[:, t], O_hi[:, t, 1],
                                             wa, wb, slice(c1, c1 + C), R_OUT if a == 0 else R_PJ)
                        last.then_inc(psum_filled, 1)

                for step, hf in ATTENTION_ORDER:
                    if (step, hf) in before:
                        before[step, hf]()
                    if step == "qkv":
                        qkv(hf)
                    elif step == "st":
                        scores(hf)
                    elif step in ("values0", "values1"):
                        values(hf, int(step[-1]))
                    elif step == "s":
                        turn_scores(hf)
                    elif step == "pt":
                        turn_probabilities(hf)
                    elif step == "ot":
                        outputs(hf)
                    else:
                        project(hf)

            def router(name, tiles, wa, wb, at, bias):
                free(name)
                for i, t in enumerate(tiles):
                    last = by_tokens(bank(name)[:, E * i:E * i + E], X_hi[:, t, 0], X_lo[:, t], X_hi[:, t, 1],
                                     wa, wb, slice(at, at + E), bias)
                last.then_inc(psum_filled, 1)

            beta((3, 0, 4))
            for t in range(NT + 1):
                if t < NT:
                    tok_turn(t)
                if t == 0:
                    beta((1, 5, 2, 6, 7)).then_inc(psum_filled, 1)
                if t:
                    tok_product(t - 1)
                if t in (4, 6, 8):
                    turn("attn0", (t // 2 - 2,))
            pe.wait_ge(early_low, 2)
            pe.wait_ge(cols_ready, 10)
            attention(0, 2, {("st", 0): lambda: turn("attn0", (3,)), ("pj", 1): lambda: turn("moe", (0, 1))})
            pe.wait_ge(x_ready, 6)
            pe.wait_ge(wlo, N1)
            for u in range(UNITS + 1):
                if u < UNITS:
                    for n, c, _ in unit_chunks(u):
                        free(("h", n))
                        by_rows(bank(("h", n)), m1a, m1b, P * c, P, u // E).then_inc(psum_filled, 1)
                if u == 0:
                    turn("moe", (2, 3))
                    pe.wait_ge(x_ready, 8)
                    router("router0", range(NT), early_a, early_b, EARLY["router"], R_RT)
                if u:
                    v = u - 1
                    q = v // 4
                    r = slice(32 * (v % 4), 32 * (v % 4) + 32)
                    terms = [(r, 4 + q % 2, 2 * E + q % 2)] + [(slice(0, P), s_, c) for n, c, s_ in unit_chunks(v)[-2:]]
                    pe.wait_ge(hp_ready, unit_chunks(v)[-1][0] + 1)
                    if v == 0:
                        pe.wait_ge(wlo, NM)
                    for pr in range(2):
                        free(("y", v, pr))
                        for j in range(2):
                            o = bank(("y", v, pr))[:, C * j:C * j + C]
                            x = slice(P * (2 * pr + j), P * (2 * pr + j) + P)
                            for i, (rows_, slot, c) in enumerate(terms):
                                w = slice(C * c, C * c + C)
                                mm(o, hgh[slot][rows_, x], m2[rows_, 0, w], i == 0, False)
                                mm(o, hgl[slot][rows_, x], m2[rows_, 0, w], False, False)
                                last = mm(o, hgh[slot][rows_, x], m2[rows_, 1, w], False, i == 2)
                        last.then_inc(psum_filled, 1)
                    if u == 2:
                        pe.wait_ge(gate_ready, 1)
                        for hf in range(2):
                            name = ("ct", hf)
                            free(name)
                            for i in range(4):
                                last = T_.transpose(bank(name)[0:E, P * i:P * i + P], gat[:, 4, 4 * hf + i], ident)
                            last.then_inc(psum_filled, 1)
                    if u == UNITS - 1:
                        turn("mix1", (0, 1))
                    if u % E == 0:
                        pe.wait_ge(ct_ready, 2)
                        for pr in range(2):
                            name = ("b2", 2 * (u // E - 1) + pr)
                            free(name)
                            for j in range(2):
                                t = 2 * name[1] + j
                                last = mm(bank(name)[:, C * j:C * j + C], ctT[:, P * t:P * t + P], b2s[:], True, True)
                            last.then_inc(psum_filled, 1)
            pe.wait_ge(wlo, NM + NL + 1)

            def kvr(block):
                for i in range(3):
                    name = ("kvr"[i], block)
                    c0 = LATE["kvr"] + C * i
                    free(name)
                    if block == 1:
                        for hf in range(2):
                            last = by_rows(bank(name)[64 * hf:64 * hf + 64], late_a, late_b, c0 + P, CB, hf)
                    else:
                        last = by_rows(bank(name), late_a, late_b, c0, P, block // 2)
                    last.then_inc(psum_filled, 1)

            pe.wait_ge(x_ready, 10)
            kvr(0)
            turn("mix1", (2, 3))
            pe.wait_ge(x_ready, 12)
            kvr(1)
            kvr(2)
            c0 = slice(LATE["wo"], LATE["wo"] + C)
            for pr in range(4):
                name = ("wo", pr)
                free(name)
                pe.wait_ge(sy_ready, 4 + 2 * (pr // 2))
                for j in range(2):
                    t = 2 * pr + j
                    o = bank(name)[:, C * j:C * j + C]
                    x = slice(P * t, P * t + P)
                    y = slice(P * (t % 4), P * (t % 4) + P)
                    r = slice(64 * (t // 4), 64 * (t // 4) + 64)
                    mm(o, sy_ah[:, x], late_a[:, 0, c0], True, False)
                    mm(o, sy_al[:, x], late_a[:, 0, c0], False, False)
                    mm(o, sy_ah[:, x], late_a[:, 1, c0], False, False)
                    mm(o, sy_bh[r, y], late_b[r, 0, c0], False, False)
                    mm(o, sy_bl[r, y], late_b[r, 0, c0], False, False)
                    last = mm(o, sy_bh[r, y], late_b[r, 1, c0], False, True)
                last.then_inc(psum_filled, 1)

            def ffn_keys(hf):
                for m in range(6):
                    if hf == 0 and m == 3:
                        turn("mix2", (2, 3))
                    name = ("kf", hf, m)
                    free(name)
                    by_rows(bank(name), late_a, late_b, LATE["kf"] + P * m, P, hf).then_inc(psum_filled, 1)

            def receptance(hf):
                for pr in range(2):
                    name = ("r", hf, pr)
                    free(name)
                    for j in range(2):
                        t = 4 * hf + 2 * pr + j
                        last = by_tokens(bank(name)[:, C * j:C * j + C], X_hi[:, t, 0], X_lo[:, t], X_hi[:, t, 1],
                                         late_a, late_b, slice(LATE["wr"], LATE["wr"] + C))
                    last.then_inc(psum_filled, 1)

            def ffn_values(hf):
                for pr in range(2):
                    name = ("kv", hf, pr)
                    free(name)
                    for j in range(2):
                        o = bank(name)[:, C * j:C * j + C]
                        x = slice(P * (2 * pr + j), P * (2 * pr + j) + P)
                        for m in range(6):
                            if pr == 0 and j == 0:
                                pe.wait_ge(kf_ready, 6 * hf + m + 1)
                            w = slice(C * m, C * m + C)
                            mm(o, kfh[hf][:, m, x], fullp[:, 0, w], m == 0, False)
                            mm(o, kfl[hf][:, m, x], fullp[:, 0, w], False, False)
                            last = mm(o, kfh[hf][:, m, x], fullp[:, 1, w], False, m == 5)
                    last.then_inc(psum_filled, 1)

            turn("mix2", (0, 1))
            pe.wait_ge(x_ready, 14)
            ffn_keys(0)
            receptance(0)
            pe.wait_ge(x_ready, 16)
            ffn_keys(1)
            ffn_values(0)
            receptance(1)
            ffn_values(1)

            def gated(hf):
                name = ("ce", hf)
                free(name)
                pe.wait_ge(gate_ready, 2 + hf)
                for i in range(4):
                    last = T_.transpose(bank(name)[:, P * i:P * i + P], crep1[:, 4 * hf + i], ident)
                last.then_inc(psum_filled, 1)
                name = ("la", hf)
                free(name)
                by_rows(bank(name), late_a, late_b, LATE["la"], P, hf).then_inc(psum_filled, 1)

            def gate_router(hf):
                pe.wait_ge(x_ready, 18 + 2 * hf)
                router(("router1", hf), range(4 * hf, 4 * hf + 4), late_a, late_b, LATE["gate"], R_GT)

            turn("attn1", (0, 1))
            gate_router(0)
            gated(0)
            attention(1, None, {("st", 0): lambda: turn("attn1", (2, 3)), ("values0", 0): lambda: gate_router(1),
                                ("values1", 0): lambda: gated(1)})


def _patch_order():
    inner, edge, corner, halo = [], [], [], []
    for i in range(-1, 17):
        for j in range(-1, 17):
            a, b = i in (-1, 16), j in (-1, 16)
            if a and b:
                continue
            where = halo if a or b else (corner, edge, inner)[2 - (i in (0, 15)) - (j in (0, 15))]
            where += [(i, j, c) for c in range(3)]
    return inner + edge + corner + halo


def _weight_rows(order):
    rows = np.full((FEAT, 5), PDIM)
    for n, (i, j, c) in enumerate(order):
        for s, (di, dj) in enumerate(((0, 0), (0, 1), (0, -1), (1, 0), (-1, 0))):
            p, q = i + di, j + dj
            if 0 <= p < 16 and 0 <= q < 16:
                rows[n, s] = (p * 16 + q) * 15 + 3 * s + c
    return rows


def _constants():
    k = np.zeros((P, K_N), np.float32)
    p = np.arange(P)
    k[:, K_ID:K_ID + P] = np.eye(P)
    k[:, K_HM:K_HM + HA] = p[:, None] // HD == np.arange(HA)
    k[:, K_HMB:K_HMB + HB] = p[:, None] % CB // HD == np.arange(HB)
    i, j = p[:, None] % SEQ, np.arange(SEQ)
    k[:, K_AM:K_AM + SEQ] = np.where(((j % 8 == 0) & (j <= i)) | (j == i) | (j == i - 1), 0.0, -1e30)
    k[:, K_BNW:K_BNW + 30] = [x for _, w in GROUPS for x in (w, 1, w) * 2]
    k[:, K_TRI:K_TRI + E * E] = (np.arange(E)[None, :] < np.arange(E)[:, None]).reshape(-1)
    return k


def kernel(**inputs):
    import concourse.bacc as bacc
    from concourse.bass_utils import run_bass_kernel_spmd

    g = {k: np.asarray(v) for k, v in inputs.items()}
    f32 = np.float32
    order = _patch_order()
    rows = _weight_rows(order)
    x = np.pad(g["x"], ((0, 0), (0, 0), (1, 1), (1, 1)))
    oi, oj, oc = (np.array(v) for v in zip(*order))
    tok = np.stack([x[:, oc, 16 * a + 1 + oi, 16 * b + 1 + oj] for a in range(4) for b in range(4)], axis=1)
    tok_x = tok.reshape(NT, P, FEAT)
    wz = np.concatenate([g["L0_tok_W"], np.zeros((1, C), f32)])
    tok_w = wz[rows[:PIX]].reshape(6, P, 5, C).transpose(1, 0, 2, 3)
    live = rows[PIX:].min(axis=1)
    live = np.concatenate([live, np.full(64, PDIM)])
    tok_wh = wz[live].reshape(2, P, C).transpose(1, 0, 2).copy()
    tok_wh[64:, 1] = tok_wh[:64, 1]

    def spread(v):
        z = np.concatenate([v, np.zeros(1, f32)])
        a = z[rows[:PIX]].reshape(6, P, 5).transpose(1, 0, 2).reshape(P, 30)
        b = z[live].reshape(2, P).T.copy()
        return a, b
    ga, gb = spread(g["L0_tok_gamma"])
    gb[64:, 1] = gb[:64, 1]
    ba, bb = spread(g["L0_tok_beta"])
    tok_g = np.concatenate([ga, gb], 1)
    tok_bt = np.concatenate([ba, bb], 1)

    def two(ws):
        w = np.concatenate(ws, 1)
        return np.stack([w[:P], np.concatenate([w[P:], w[P:]])], 1)

    def slots(w):
        q, k, v = w[..., :C], w[..., C:2 * C], w[..., 2 * C:]
        return np.concatenate([q[..., :P], k[..., :P], v[..., :P], k[..., P:], v[..., P:], q[..., P:]], -1)

    early = two([slots(g["L0_attn_qkv_w"].T), g["L0_attn_out_w"].T, g["L0_ffn_router_w"]])
    w1, w2, b1 = g["L0_ffn_w1"], g["L0_ffn_w2"], g["L0_ffn_b1"]
    w1c = np.concatenate([w1[:, :, :256].transpose(1, 0, 2).reshape(C, -1), w1[:, :, 256:].transpose(1, 0, 2).reshape(C, -1)], 1)
    moe1 = two([w1c]).reshape(P, -1)
    w2c = np.concatenate([w2[:, :256].reshape(-1, C), w2[:, 256:].reshape(-1, C)])
    moe2 = w2c.reshape(NCH, P, C).transpose(1, 0, 2).reshape(P, -1)
    b1c = np.concatenate([b1[:, :256].reshape(-1), b1[:, 256:].reshape(-1)]).reshape(NCH, P).T
    la = g["L1_ffn_A"].transpose(2, 1, 0).reshape(C, P)
    bm = slots(g["L1_ffn_Bm"].transpose(2, 0, 1).reshape(P, 3 * C))
    bbs = np.zeros((P, 3 * C), f32)
    for r in (0, 32, 64):
        bbs[r:r + E] = slots(g["L1_ffn_bb"])
    late = two([g["L1_attn_Wk_a"].T, g["L1_attn_Wv_a"].T, g["L1_attn_Wr_a"].T, g["L1_attn_Wo_a"].T, g["L1_attn_Wk_f"].T,
                g["L1_attn_Wr_f"].T, g["L1_ffn_Wg"].T, la, slots(g["L1_ffn_Wqkv"].T), g["L1_ffn_Wproj"].T])
    wv = g["L1_attn_Wv_f"].T.reshape(6, P, C).transpose(1, 0, 2).reshape(P, -1)
    full = np.concatenate([wv, bm, bbs], 1)

    def qcols(b):
        s = slots(b)
        return [s[:128], s[128:256], s[256:384], s[384:512], np.concatenate([s[512:], s[512:]])]

    def ab(v):
        return [v[:P], np.concatenate([v[P:], v[P:]])]
    cols = qcols(g["L0_attn_qkv_b"]) + list(b1c.T) + ab(g["L1_attn_ln1_w"]) + ab(g["L1_attn_ln1_b"]) \
        + ab(g["L1_attn_ln2_w"]) + ab(g["L1_attn_ln2_b"]) + ab(g["L1_attn_decay"]) + ab(g["L1_attn_first"]) \
        + [g["L1_ffn_ba"].T.reshape(P)] + qcols(g["L1_ffn_bqkv"])
    cols = np.stack(cols, 1)
    brow = np.concatenate([g["L0_attn_out_b"], g["L0_ffn_router_b"], g["L1_ffn_bproj"], g["L1_ffn_bg"]])[None]
    tok_b = np.broadcast_to(g["L0_tok_b"], (P, C))

    nc = bacc.Bacc("TRN2", target_bir_lowering=False, num_devices=1)
    arrays, args = {}, []
    for name, a in (("tok_x", tok_x), ("tok_w", tok_w), ("tok_wh", tok_wh), ("tok_g", tok_g), ("tok_bt", tok_bt),
                    ("tok_b", tok_b), ("early", early), ("moe1", moe1), ("moe2", moe2), ("moe_b2", g["L0_ffn_b2"]),
                    ("late", late.reshape(P, -1)), ("full", full), ("cols", cols), ("rows", brow),
                    ("consts", _constants())):
        a = np.ascontiguousarray(a)
        arrays[name] = a
        args.append(nc.dram_tensor(name, a.shape, F32, kind="ExternalInput").ap())
    args.append(nc.dram_tensor("out", (P, NT, C), F32, kind="ExternalOutput").ap())
    build(nc, *args)
    r = run_bass_kernel_spmd(nc, [arrays], core_ids=[0])
    return r.results[0]["out"].transpose(1, 0, 2).reshape(64, SEQ, C)
```
